# Optimizing a Trainium2 kernel written in Bass

```python
import numpy as np
import jax
import jax.numpy as jnp

def _softmax(x, axis=-1):
    return jax.nn.softmax(x, axis=axis)

def _gelu(x):
    return jax.nn.gelu(x, approximate=True)

def _silu(x):
    return jax.nn.silu(x)

def _sigmoid(x):
    return jax.nn.sigmoid(x)

def _layernorm(x, axis=-1, eps=1e-05):
    m = jnp.mean(x, axis=axis, keepdims=True)
    v = jnp.var(x, axis=axis, keepdims=True)
    return (x - m) / jnp.sqrt(v + eps)

def _scatter_add(tgt, idx, src, axis=0):
    return tgt.at[idx].add(src)

def _segment_sum(src, seg, n):
    return jax.ops.segment_sum(src, seg, n)
kernel_name = 'mk_decoder_preln_d1_seqx_r2_c34046'

def setup_inputs(seed: int=0):
    np.random.seed(seed)
    _w = jnp.asarray

    def _rec_inputs():
        import jax
        import jax.numpy as jnp
        _rk = jax.random.key(seed)
        x = -0.0002928 + 1 * jax.random.normal(jax.random.fold_in(_rk, 1), (4, 1024, 512), jnp.float32)
        _lenS = 1024 - jax.random.randint(jax.random.fold_in(_rk, 7), (4,), 0, max(1, 1024 // 4) + 1, jnp.int32)
        _lenS2 = 1024 - jax.random.randint(jax.random.fold_in(_rk, 8), (4,), 0, max(1, 1024 // 4) + 1, jnp.int32)
        _ctx_1024P = jax.random.normal(jax.random.fold_in(_rk, 11), (4, 16, 512), jnp.float32)
        _ctx_1024c = jax.random.dirichlet(jax.random.fold_in(_rk, 511), 0.3 * jnp.ones((16,), jnp.float32), (4, 1024))
        _ctx_1024t = jnp.einsum('bsk,bkd->bsd', _ctx_1024c, _ctx_1024P)
        _ctx_1024t = _ctx_1024t * jax.lax.rsqrt(jnp.mean(jnp.square(_ctx_1024t)) + 1e-12) * 0.953939
        ctx_1024 = -1.39393e-06 + 0.999914 * (_ctx_1024t + 0.3 * jax.random.normal(jax.random.fold_in(_rk, 611), (4, 1024, 512), jnp.float32))
        return (x, ctx_1024)
    x, ctx_1024 = _rec_inputs()

    def _L0_attn_setup():
        import jax, jax.numpy as jnp
        import numpy as np
        B, N, D_IN, D_OUT, HEADS = (4, 2048, 512, 512, 16)
        D_HEAD = D_OUT // HEADS
        key = jax.random.key(seed)
        ks = jax.random.split(key, 5)
        x = jax.random.normal(ks[0], (B, N, D_IN), dtype=jnp.float32)
        s_in = 1.0 / np.sqrt(D_IN)
        s_out = 1.0 / np.sqrt(D_OUT)
        Wq = jax.random.normal(ks[1], (D_IN, D_OUT), dtype=jnp.float32) * s_in
        Wk = jax.random.normal(ks[2], (D_IN, D_OUT), dtype=jnp.float32) * s_in
        Wv = jax.random.normal(ks[3], (D_IN, D_OUT), dtype=jnp.float32) * s_in
        Wo = jax.random.normal(ks[4], (D_OUT, D_OUT), dtype=jnp.float32) * s_out
        bo = jnp.zeros((D_OUT,), dtype=jnp.float32)
        return {'x': x, 'Wq': Wq, 'Wk': Wk, 'Wv': Wv, 'Wo': Wo, 'bo': bo}
    _L0_attn_all = _L0_attn_setup()
    _L0_attn_in = {k: v for k, v in _L0_attn_all.items() if k in ('Wq', 'Wk', 'Wv', 'Wo', 'bo')}
    del _L0_attn_all

    def _L0_xattn_setup():
        import jax, jax.numpy as jnp
        import numpy as np
        B, S, E, H = (2, 1024, 512, 16)
        HD = E // H
        key = jax.random.key(seed)
        ks = jax.random.split(key, 7)
        mk = lambda k, shp: jax.random.normal(k, shp, dtype=jnp.float32) * 0.02
        return {'q': jax.random.normal(ks[0], (B, S, E), dtype=jnp.float32), 'k': jax.random.normal(ks[1], (B, S, E), dtype=jnp.float32), 'v': jax.random.normal(ks[2], (B, S, E), dtype=jnp.float32), 'wq': mk(ks[3], (E, E)), 'wk': mk(ks[4], (E, E)), 'wv': mk(ks[5], (E, E)), 'wo': mk(ks[6], (E, E)), 'autoregressive_mask': 1}
    _L0_xattn_all = _L0_xattn_setup()
    _L0_xattn_in = {k: v for k, v in _L0_xattn_all.items() if k in ('wq', 'wk', 'wv', 'wo')}
    del _L0_xattn_all

    def _L0_ffn_setup():
        import jax, jax.numpy as jnp
        import numpy as np
        INT4_QMAX = 7.0

        def simulate_quantize_int4(w):
            scale = jnp.max(jnp.abs(w)) / INT4_QMAX
            q = jnp.clip(jnp.round(w / scale), -8.0, 7.0)
            return q * scale
        key = jax.random.key(seed)
        k_x, k_w, k_bias, k_a, k_b = jax.random.split(key, 5)
        d_in, features, rank = (512, 512, 16)
        x = jax.random.normal(k_x, (4, 4096, d_in), dtype=jnp.float32)
        kernel = jax.random.normal(k_w, (d_in, features), dtype=jnp.float32)
        bias = jax.random.normal(k_bias, (features,), dtype=jnp.float32)
        a = jax.random.normal(k_a, (d_in, rank), dtype=jnp.float32) * (1.0 / np.sqrt(d_in))
        b = jax.random.normal(k_b, (rank, features), dtype=jnp.float32) * 0.01
        return {'x': x, 'kernel': kernel, 'bias': bias, 'a': a, 'b': b}
    _L0_ffn_all = _L0_ffn_setup()
    _L0_ffn_in = {k: v for k, v in _L0_ffn_all.items() if k in ('kernel', 'bias', 'a', 'b')}
    del _L0_ffn_all
    return {'x': x, 'ctx_1024': ctx_1024, 'L0_attn_Wq': _L0_attn_in['Wq'], 'L0_attn_Wk': _L0_attn_in['Wk'], 'L0_attn_Wv': _L0_attn_in['Wv'], 'L0_attn_Wo': _L0_attn_in['Wo'], 'L0_attn_bo': _L0_attn_in['bo'], 'L0_xattn_wq': _L0_xattn_in['wq'], 'L0_xattn_wk': _L0_xattn_in['wk'], 'L0_xattn_wv': _L0_xattn_in['wv'], 'L0_xattn_wo': _L0_xattn_in['wo'], 'L0_ffn_kernel': _L0_ffn_in['kernel'], 'L0_ffn_bias': _L0_ffn_in['bias'], 'L0_ffn_a': _L0_ffn_in['a'], 'L0_ffn_b': _L0_ffn_in['b']}

def reference(x, ctx_1024, L0_attn_Wq, L0_attn_Wk, L0_attn_Wv, L0_attn_Wo, L0_attn_bo, L0_xattn_wq, L0_xattn_wk, L0_xattn_wv, L0_xattn_wo, L0_ffn_kernel, L0_ffn_bias, L0_ffn_a, L0_ffn_b):
    import jax
    import jax.numpy as jnp

    def _L0_attn_ref(x, Wq, Wk, Wv, Wo, bo):
        import jax, jax.numpy as jnp
        import numpy as np
        B, N, D_IN, D_OUT, HEADS = (4, 2048, 512, 512, 16)
        D_HEAD = D_OUT // HEADS
        q = jax.nn.softmax(jnp.einsum('bni,io->bno', x, Wq), axis=-1)
        k = jax.nn.softmax(jnp.einsum('bni,io->bno', x, Wk), axis=-2)
        v = jnp.einsum('bni,io->bno', x, Wv)
        scale = 1.0 / np.sqrt(D_HEAD).astype(np.float32)
        ctx = jnp.einsum('bnd,bne->bde', k, v) * scale
        y = jnp.einsum('bnd,bde->bne', q, ctx) / jnp.float32(D_OUT)
        return jnp.einsum('bnd,de->bne', y, Wo) + bo

    def _L0_xattn_ref(q, k, v, wq, wk, wv, wo, autoregressive_mask):
        import jax, jax.numpy as jnp
        import numpy as np
        B, S, E, H = (2, 1024, 512, 16)
        HD = E // H
        scale = 1.0 / np.sqrt(HD).astype(np.float32)
        qp = (q @ wq.T).reshape(-1, H, S, HD)
        kp = (k @ wk.T).reshape(-1, H, S, HD)
        vp = (v @ wv.T).reshape(-1, H, S, HD)
        scores = jnp.einsum('bhqd,bhkd->bhqk', qp, kp) * scale
        if autoregressive_mask:
            causal = jnp.tril(jnp.ones((S, S), dtype=bool))
            scores = jnp.where(causal, scores, jnp.float32(-1000000000.0))
        attn = jax.nn.softmax(scores, axis=-1)
        out = jnp.einsum('bhqk,bhkd->bhqd', attn, vp).reshape(-1, S, E)
        return out @ wo.T

    def _L0_ffn_ref(x, kernel, bias, a, b):
        import jax, jax.numpy as jnp
        import numpy as np
        INT4_QMAX = 7.0

        def simulate_quantize_int4(w):
            scale = jnp.max(jnp.abs(w)) / INT4_QMAX
            q = jnp.clip(jnp.round(w / scale), -8.0, 7.0)
            return q * scale
        w = simulate_quantize_int4(kernel)
        y = jnp.einsum('bsd,df->bsf', x, w) + bias
        lora = jnp.einsum('bsr,rf->bsf', jnp.einsum('bsd,dr->bsr', x, a), b)
        return y + lora
    x = x + _L0_attn_ref(_layernorm(x, axis=-1), L0_attn_Wq, L0_attn_Wk, L0_attn_Wv, L0_attn_Wo, L0_attn_bo)
    x = x + _L0_xattn_ref(_layernorm(x, axis=-1), ctx_1024, ctx_1024, L0_xattn_wq, L0_xattn_wk, L0_xattn_wv, L0_xattn_wo, 1)
    x = x + _L0_ffn_ref(_layernorm(x, axis=-1), L0_ffn_kernel, L0_ffn_bias, L0_ffn_a, L0_ffn_b)
    return x

_drawn_inputs = setup_inputs


def setup_inputs(seed=0):
    import zlib

    import numpy as np

    out = dict(_drawn_inputs(seed))
    spreads = {'L0_attn_bo': (0.0, 0.1)}
    factors = {'L0_attn_Wq': 27.234,
     'L0_attn_Wk': 27.045,
     'L0_attn_Wv': 27.091,
     'L0_attn_Wo': 27.064,
     'L0_xattn_wq': 8.0,
     'L0_xattn_wk': 8.0,
     'L0_ffn_a': 8.0,
     'L0_ffn_b': 8.0}
    for name, (base, spread) in spreads.items():
        noise = np.random.default_rng([zlib.crc32(name.encode()), seed]).standard_normal(out[name].shape)
        drawn = base * np.exp(spread * noise) if base else spread * noise
        out[name] = jnp.asarray(drawn.astype(out[name].dtype))
    for name, factor in factors.items():
        out[name] = (out[name] * factor).astype(out[name].dtype)
    return out
```

```python
from contextlib import ExitStack

import numpy as np

import concourse.bass as bass
from concourse import mybir

F32 = mybir.dt.float32
F32R = mybir.dt.float32r
BF16 = mybir.dt.bfloat16
ALU = mybir.AluOpType
ACT = mybir.ActivationFunctionType
RED = bass.bass_isa.ReduceOp
AX = mybir.AxisListType.X

P = 128
D = 512
C = D // P
HEADS = 16
HD = D // HEADS
EPS = 1e-5
MASKED = -1.0e30


def mm3(pe, out, lhsT, rhs, first, last):
    (lh, ll), (rh, rl) = lhsT, rhs
    pe.matmul(out, lh, rh, start=first, stop=False)
    pe.matmul(out, lh, rl, start=False, stop=False)
    return pe.matmul(out, ll, rh, start=False, stop=last)


def transposes(pe, bank, src, ident):
    for i, s in enumerate(src):
        last = pe.transpose(bank[:, i * P:(i + 1) * P], s, ident)
    return last


def wait_apart(v, sem, value, spare):
    v.wait_ge(sem, value)
    v.memset(spare[:, :], 0.0)


class Scope:

    def __init__(self, nc, ctx, tag):
        self.nc, self.ctx, self.tag, self.held = nc, ctx, tag, []

    def block(self):
        self.ctx.callback(self.release)
        return self.ctx.enter_context(self.nc.Block())

    def release(self):
        self.nc.clear_and_free_semaphores(self.held)
        self.nc.all_engine_barrier()

    def sb(self, name, shape, dt=F32):
        return self.ctx.enter_context(self.nc.sbuf_tensor(f"{self.tag}_{name}", shape, dt))

    def pair(self, name, shape):
        return self.sb(name + "_hi", shape, F32R), self.sb(name + "_lo", shape, F32R)

    def sem(self, name):
        self.held.append(self.nc.alloc_semaphore(f"{self.tag}_{name}"))
        return self.held[-1]

    def sems(self, name, n):
        return [self.sem(f"{name}{i}") for i in range(n)]


def linear_attention(nc, ps, x, Wq, Wk, Wv, Wo, bo, ident_in, x1):
    B, N, _ = x.shape
    T = N // P
    SCALE = float(1.0 / np.sqrt(np.float32(HD))) / D
    with ExitStack() as ctx:
        s = Scope(nc, ctx, "a")
        W = {n: s.pair(f"w{n}", [P, C, D]) for n in ("q", "k", "vo")}
        xt = s.sb("xt", [P, T, D])
        h = s.sb("h", [P, 2, D])
        hn = s.pair("hn", [P, T, D])
        hT = s.pair("hT", [P, C * N])
        hT_v = [a[:, :].rearrange("p (c n) -> p c n", c=C) for a in hT]
        k_v = [a[:, :].rearrange("p (t d) -> p t d", t=T) for a in hT]
        c_v = [a[:, 0:C * D].rearrange("p (c e) -> p c e", c=C) for a in hT]
        qT = s.pair("qT", [P, C, N])
        ek = s.sb("ek", [P, C, N])
        M = s.pair("M", [P, C, D])
        eq = s.sb("eq", [P, 2, D])
        ident, bob = s.sb("ident", [P, P]), s.sb("bob", [P, D])
        bn, mv, rstd = s.sb("bn", [P, 2, 6]), s.sb("mv", [P, 2, 2]), s.sb("rstd", [P, 2])
        power, spare = s.sb("power", [P, 1]), s.sb("spare", [P, 1])
        nmq, smq, rsq = (s.sb(n, [P, T]) for n in ("nmq", "smq", "rsq"))
        nmk, smk, rsk = (s.sb(n, [P, C]) for n in ("nmk", "smk", "rsk"))

        ld_w, ld_c, ld_x, st_x = s.sems("ld_w", 4), s.sem("ld_c"), s.sems("ld_x", T), s.sems("st_x", T)
        prep_hi, prep_lo, prep_pe, setup = s.sem("prep_hi"), s.sem("prep_lo"), s.sem("prep_pe"), s.sem("setup")
        bn_ready, var_eps, var_ready, rstd_ready, h_ready = (s.sem(n) for n in ("bn", "ve", "var", "rstd", "h"))
        hn_hi, hn_lo, xb_done = s.sem("hn_hi"), s.sem("hn_lo"), s.sem("xb")
        hT_pe, hT_hi, hT_lo = s.sem("hT_pe"), s.sem("hT_hi"), s.sem("hT_lo")
        q_pe, q_max, q_exp = s.sem("q_pe"), s.sem("q_max"), s.sem("q_exp")
        qT_pe, qT_hi, qT_lo = s.sem("qT_pe"), s.sem("qT_hi"), s.sem("qT_lo")
        k_pe, k_max, k_exp = s.sem("k_pe"), s.sem("k_max"), s.sem("k_exp")
        kn_pe, kn_hi, kn_lo = s.sem("kn_pe"), s.sem("kn_hi"), s.sem("kn_lo")
        M_pe, M_hi, M_lo = s.sem("M_pe"), s.sem("M_hi"), s.sem("M_lo")
        rq_ready, rk_ready, c_scale = s.sem("rq"), s.sem("rk"), s.sem("c_scale")
        c_pe, c_tmp, c_hi, c_done = s.sem("c_pe"), s.sem("c_tmp"), s.sem("c_hi"), s.sem("c_done")
        o_pe, o_done = s.sem("o_pe"), s.sem("o_done")

        raw = {"q": ek[:, :, 0:D], "k": ek[:, :, D:2 * D], "v": xt[:, 0:C, :], "o": xt[:, C:2 * C, :]}
        wo = [a[:, :, 0:D] for a in qT]
        wvT = [a[:, :, 0:D] for a in hT_v]
        xf = x.rearrange("b n d -> (b n) d")
        block = s.block()

        @block.sync
        def _(sp):
            for i, (n, w) in enumerate((("v", Wv), ("o", Wo), ("q", Wq), ("k", Wk))):
                sp.dma_start(raw[n], w.rearrange("(c p) n -> p c n", p=P)).then_inc(ld_w[i], 16)
            sp.dma_start(ident[:, :], ident_in).then_inc(ld_c, 16)
            sp.dma_start(bob[:, :], bo.partition_broadcast(P)).then_inc(ld_c, 16)
            sp.wait_ge(prep_pe, C)
            sp.wait_ge(prep_lo, 1)
            for t in range(T):
                sp.dma_start(xt[:, t, :], xf[t * P:(t + 1) * P, :]).then_inc(ld_x[t], 16)

            def store(b, t):
                sp.wait_ge(o_done, b * T + (t + 1))
                sp.dma_start(x1[bass.ds(b * N + t * P, P), :], xt[:, t, :]).then_inc(st_x[t], 16)

            with sp.Fori(0, B - 1) as b:
                for t in range(T):
                    store(b, t)
                    if t >= 2:
                        sp.wait_ge(st_x[t - 2], b * 16 + 16)
                        sp.dma_start(xt[:, t - 2, :], xf[bass.ds(b * N + (N + (t - 2) * P), P), :]
                                     ).then_inc(ld_x[t - 2], 16)
                for t in (T - 2, T - 1):
                    sp.wait_ge(st_x[t], b * 16 + 16)
                    sp.dma_start(xt[:, t, :], xf[bass.ds(b * N + (N + t * P), P), :]).then_inc(ld_x[t], 16)
            for t in range(T):
                store(B - 1, t)
            for t in range(T):
                sp.wait_ge(st_x[t], 16 * B)

        def low_rows(pool, b, t):
            pool.wait_ge(hn_hi, b * T + (t + 1))
            pool.tensor_tensor(hn[1][:, t, :], h[:, t % 2, :], hn[0][:, t, :], ALU.subtract).then_inc(hn_lo, 1)

        @block.gpsimd
        def _(pool):
            pool.memset(power[:, :], -0.5).then_inc(setup, 1)
            pool.wait_ge(setup, 1)
            with pool.Fori(0, B) as b:
                for t in range(T):
                    pool.wait_ge(var_ready, b * T + (t + 1))
                    pool.tensor_tensor(rstd[:, t % 2:t % 2 + 1], mv[:, t % 2, 1:2], power[:, :], ALU.pow
                                       ).then_inc(rstd_ready, 1)
                    if t >= 1:
                        low_rows(pool, b, t - 1)
                low_rows(pool, b, T - 1)
                for t in range(T):
                    pool.tensor_tensor(xt[:, t, :], xt[:, t, :], bob[:, :], ALU.add).then_inc(xb_done, 1)

        @block.vector
        def _(v):
            def split(i, dst, src, n):
                v.wait_ge(prep_hi, n)
                v.tensor_tensor(dst[1], src, dst[0], ALU.subtract).then_inc(prep_lo, 1)

            v.wait_ge(ld_w[1], 16)
            split(1, wo, raw["o"], 1)
            for oc in range(C):
                split(2, [a[:, oc, :] for a in wvT], ps[:, oc, :], 2 + oc)
            split(3, [a[:, :, :] for a in W["q"]], raw["q"], 6)
            split(4, [a[:, :, :] for a in W["k"]], raw["k"], 7)
            for f in range(C):
                split(5, [a[:, f, :] for a in W["vo"]], ps[:, 4 + f, :], 8 + f)

            def layernorm(b, t):
                v.wait_ge(ld_x[t], b * 16 + 16)
                v.bn_stats(bn[:, t % 2, :], xt[:, t, :]).then_inc(bn_ready, 1)
                wait_apart(v, bn_ready, b * T + (t + 1), spare)
                v.bn_aggr(mv[:, t % 2, :], bn[:, t % 2, :]).then_inc(var_eps, 1)
                v.wait_ge(var_eps, b * T + (t + 1))
                v.tensor_scalar(mv[:, t % 2, 1:2], mv[:, t % 2, 1:2], EPS, None, ALU.add).then_inc(var_ready, 1)
                if t >= 2:
                    v.wait_ge(hT_pe, b * T + (t - 1))
                    v.wait_ge(hn_lo, b * T + (t - 1))
                v.wait_ge(rstd_ready, b * T + (t + 1))
                v.tensor_scalar(h[:, t % 2, :], xt[:, t, :], mv[:, t % 2, 0:1], rstd[:, t % 2:t % 2 + 1],
                                ALU.subtract, ALU.mult).then_inc(h_ready, 1)

            with v.Fori(0, B) as b:
                layernorm(b, 0)
                for i in range(T + 2):
                    if i + 1 < T:
                        layernorm(b, i + 1)
                    if i < T:
                        v.wait_ge(hT_hi, b * T + (i + 1))
                        bank = ps[:, i % 2, :].rearrange("p (c n) -> p c n", c=C)
                        v.tensor_tensor(hT_v[1][:, :, i * P:(i + 1) * P], bank, hT_v[0][:, :, i * P:(i + 1) * P],
                                        ALU.subtract).then_inc(hT_lo, 1)
                    if 1 <= i <= T:
                        t = i - 1
                        v.wait_ge(q_pe, b * T + (t + 1))
                        v.tensor_reduce(nmq[:, t:t + 1], ps[:, 2 + t % 2, :], AX, ALU.max, negate=True
                                        ).then_inc(q_max, 1)
                    if i >= 2:
                        t = i - 2
                        v.wait_ge(qT_hi, b * T + (t + 1))
                        bank = ps[:, 4 + t % 2, :].rearrange("p (c n) -> p c n", c=C)
                        v.tensor_tensor(qT[1][:, :, t * P:(t + 1) * P], bank, qT[0][:, :, t * P:(t + 1) * P],
                                        ALU.subtract).then_inc(qT_lo, 1)
                v.wait_ge(q_exp, b * T + T)
                v.reciprocal(rsq[:, :], smq[:, :]).then_inc(rq_ready, 1)
                for dc in range(C):
                    v.wait_ge(k_pe, b * C + (dc + 1))
                    pair = ps[:, 6:8, :] if dc % 2 == 0 else ps[:, 4:6, :]
                    v.tensor_reduce(nmk[:, dc:dc + 1], pair.rearrange("p a n -> p (a n)"), AX, ALU.max,
                                    negate=True).then_inc(k_max, 1)
                v.wait_ge(k_exp, b * C + C)
                v.reciprocal(rsk[:, :], smk[:, :]).then_inc(rk_ready, 1)
                v.wait_ge(rk_ready, b + 1)
                v.tensor_scalar(rsk[:, :], rsk[:, :], SCALE, None, ALU.mult).then_inc(c_scale, 1)
                for t in range(T):
                    v.wait_ge(kn_hi, b * T + (t + 1))
                    v.tensor_tensor(k_v[1][:, t, :], ps[:, t % 2, :], k_v[0][:, t, :], ALU.subtract
                                    ).then_inc(kn_lo, 1)
                for f in range(C):
                    v.wait_ge(M_hi, b * C + (f + 1))
                    v.tensor_tensor(M[1][:, f, :], ps[:, 2 + f, :], M[0][:, f, :], ALU.subtract).then_inc(M_lo, 1)
                for dc in range(C):
                    v.wait_ge(c_tmp, b * C + (dc + 1))
                    v.tensor_copy(c_v[0][:, dc, :], eq[:, dc % 2, :]).then_inc(c_hi, 1)
                    v.wait_ge(c_hi, b * C + (dc + 1))
                    v.tensor_tensor(c_v[1][:, dc, :], eq[:, dc % 2, :], c_v[0][:, dc, :], ALU.subtract
                                    ).then_inc(c_done, 1)
                v.wait_ge(xb_done, b * T + T)
                v.wait_ge(rq_ready, b + 1)
                for t in range(T):
                    v.wait_ge(o_pe, b * T + (t + 1))
                    v.scalar_tensor_tensor(out=xt[:, t, :], in0=ps[:, t % 2, :], scalar=rsq[:, t:t + 1],
                                           in1=xt[:, t, :], op0=ALU.mult, op1=ALU.add).then_inc(o_done, 1)

        @block.scalar
        def _(act):
            def high(dst, src):
                act.activation(dst, src, ACT.Copy).then_inc(prep_hi, 1)

            act.wait_ge(ld_w[1], 16)
            high(wo[0], raw["o"])
            for oc in range(C):
                act.wait_ge(prep_pe, oc + 1)
                high(wvT[0][:, oc, :], ps[:, oc, :])
            act.wait_ge(ld_w[2], 16)
            high(W["q"][0][:, :, :], raw["q"])
            act.wait_ge(ld_w[3], 16)
            high(W["k"][0][:, :, :], raw["k"])
            for f in range(C):
                act.wait_ge(prep_pe, C + f + 1)
                high(W["vo"][0][:, f, :], ps[:, 4 + f, :])

            with act.Fori(0, B) as b:
                for i in range(T + 2):
                    if i < T:
                        act.wait_ge(hT_pe, b * T + (i + 1))
                        bank = ps[:, i % 2, :].rearrange("p (c n) -> p c n", c=C)
                        act.activation(hT_v[0][:, :, i * P:(i + 1) * P], bank, ACT.Copy).then_inc(hT_hi, 1)
                        act.activation(hn[0][:, i, :], h[:, i % 2, :], ACT.Copy).then_inc(hn_hi, 1)
                    if 1 <= i <= T:
                        t = i - 1
                        act.wait_ge(q_max, b * T + (t + 1))
                        if t >= 2:
                            act.wait_ge(qT_pe, b * T + (t - 1))
                        act.activation(eq[:, t % 2, :], ps[:, 2 + t % 2, :], ACT.Exp, bias=nmq[:, t:t + 1],
                                       accum_out=smq[:, t:t + 1]).then_inc(q_exp, 1)
                    if i >= 2:
                        t = i - 2
                        act.wait_ge(qT_pe, b * T + (t + 1))
                        bank = ps[:, 4 + t % 2, :].rearrange("p (c n) -> p c n", c=C)
                        act.activation(qT[0][:, :, t * P:(t + 1) * P], bank, ACT.Copy).then_inc(qT_hi, 1)
                for dc in range(C):
                    act.wait_ge(k_max, b * C + (dc + 1))
                    pair = ps[:, 6:8, :] if dc % 2 == 0 else ps[:, 4:6, :]
                    act.activation(ek[:, dc, :], pair.rearrange("p a n -> p (a n)"), ACT.Exp,
                                   bias=nmk[:, dc:dc + 1], accum_out=smk[:, dc:dc + 1]).then_inc(k_exp, 1)
                for t in range(T):
                    act.wait_ge(kn_pe, b * T + (t + 1))
                    act.activation(k_v[0][:, t, :], ps[:, t % 2, :], ACT.Copy).then_inc(kn_hi, 1)
                for f in range(C):
                    act.wait_ge(M_pe, b * C + (f + 1))
                    act.activation(M[0][:, f, :], ps[:, 2 + f, :], ACT.Copy).then_inc(M_hi, 1)
                act.wait_ge(c_scale, b + 1)
                for dc in range(C):
                    act.wait_ge(c_pe, b * C + (dc + 1))
                    if dc >= 2:
                        act.wait_ge(c_done, b * C + (dc - 1))
                    act.activation(eq[:, dc % 2, :], ps[:, 6 + dc % 2, :], ACT.Copy,
                                   scale=rsk[:, dc:dc + 1]).then_inc(c_tmp, 1)

        @block.tensor
        def _(pe):
            pe.wait_ge(ld_c, 32)
            pe.wait_ge(ld_w[0], 16)
            for oc in range(C):
                transposes(pe, ps[:, oc, :], [raw["v"][:, f, oc * P:(oc + 1) * P] for f in range(C)], ident[:, :]
                           ).then_inc(prep_pe, 1)
            pe.wait_ge(prep_lo, 1 + C)
            for f in range(C):
                for oc in range(C):
                    last = mm3(pe, ps[:, 4 + f, :], [a[:, oc, f * P:(f + 1) * P] for a in wvT],
                               [a[:, oc, :] for a in wo], oc == 0, oc == C - 1)
                last.then_inc(prep_pe, 1)
            pe.wait_ge(prep_lo, 3 + 2 * C)

            with pe.Fori(0, B) as b:
                for i in range(T + 2):
                    if i < T:
                        pe.wait_ge(h_ready, b * T + (i + 1))
                        if i >= 2:
                            pe.wait_ge(hT_lo, b * T + (i - 1))
                        transposes(pe, ps[:, i % 2, :], [h[:, i % 2, c * P:(c + 1) * P] for c in range(C)],
                                   ident[:, :]).then_inc(hT_pe, 1)
                    if 1 <= i <= T:
                        t = i - 1
                        pe.wait_ge(hT_lo, b * T + (t + 1))
                        if t >= 2:
                            pe.wait_ge(q_exp, b * T + (t - 1))
                        for c in range(C):
                            last = mm3(pe, ps[:, 2 + t % 2, :], [a[:, c, t * P:(t + 1) * P] for a in hT_v],
                                       [a[:, c, :] for a in W["q"]], c == 0, c == C - 1)
                        last.then_inc(q_pe, 1)
                    if i >= 2:
                        t = i - 2
                        pe.wait_ge(q_exp, b * T + (t + 1))
                        if t >= 2:
                            pe.wait_ge(qT_lo, b * T + (t - 1))
                        transposes(pe, ps[:, 4 + t % 2, :], [eq[:, t % 2, c * P:(c + 1) * P] for c in range(C)],
                                   ident[:, :]).then_inc(qT_pe, 1)
                for dc in range(C):
                    if dc == 1:
                        pe.wait_ge(qT_lo, b * T + T)
                    if dc >= 2:
                        pe.wait_ge(k_exp, b * C + (dc - 1))
                    first_bank = 6 if dc % 2 == 0 else 4
                    for c in range(C):
                        lhsT = [a[:, c, dc * P:(dc + 1) * P] for a in W["k"]]
                        for half in range(2):
                            last = mm3(pe, ps[:, first_bank + half, :], lhsT,
                                       [a[:, c, half * 512:(half + 1) * 512] for a in hT_v], c == 0, c == C - 1)
                    last.then_inc(k_pe, 1)
                pe.wait_ge(k_exp, b * C + C)
                pe.wait_ge(hn_lo, b * T + T)
                for i in range(T + 1):
                    if i < T:
                        if i >= 2:
                            pe.wait_ge(kn_lo, b * T + (i - 1))
                        transposes(pe, ps[:, i % 2, :], [ek[:, dc, i * P:(i + 1) * P] for dc in range(C)],
                                   ident[:, :]).then_inc(kn_pe, 1)
                    if i >= 1:
                        t = i - 1
                        pe.wait_ge(kn_lo, b * T + (t + 1))
                        for f in range(C):
                            last = mm3(pe, ps[:, 2 + f, :], [a[:, t, f * P:(f + 1) * P] for a in hn],
                                       [a[:, t, :] for a in k_v], t == 0, t == T - 1)
                            if t == T - 1:
                                last.then_inc(M_pe, 1)
                pe.wait_ge(M_lo, b * C + C)
                for dc in range(C):
                    if dc >= 2:
                        pe.wait_ge(c_tmp, b * C + (dc - 1))
                    for f in range(C):
                        last = mm3(pe, ps[:, 6 + dc % 2, :], [a[:, f, dc * P:(dc + 1) * P] for a in M],
                                   [a[:, f, :] for a in W["vo"]], f == 0, f == C - 1)
                    last.then_inc(c_pe, 1)
                pe.wait_ge(c_done, b * C + C)
                for t in range(T):
                    if t >= 2:
                        pe.wait_ge(o_done, b * T + (t - 1))
                    for dc in range(C):
                        last = mm3(pe, ps[:, t % 2, :], [a[:, dc, t * P:(t + 1) * P] for a in qT],
                                   [a[:, dc, :] for a in c_v], dc == 0, dc == C - 1)
                    last.then_inc(o_pe, 1)
                pe.wait_ge(o_done, b * T + T)


def projections(nc, ps, x1, cx, wq, wk, wv, ident_in, qk, vd):
    ROWS = x1.shape[0]
    GR = 512
    G, T = ROWS // GR, GR // P
    UNITS = 3 * C
    BANKS = 6
    assert T == C and UNITS % BANKS == 0
    with ExitStack() as ctx:
        s = Scope(nc, ctx, "b")
        W = [s.pair(f"w{n}", [P, C, D]) for n in "qkv"]
        raw = [s.sb(f"raw{n}", [P, C, D]) for n in "qkv"]
        xt, ct = s.sb("xt", [P, T, D]), s.sb("ct", [P, T, D])
        h = s.sb("h", [P, 2, D])
        hT, cT = s.pair("hT", [P, C, GR]), s.pair("cT", [P, C, GR])
        res = [s.pair("q", [P, C, GR]), s.pair("k", [P, C, GR])]
        vals = s.sb("v", [P, T, D])
        ident = s.sb("ident", [P, P])
        bn, mv, rstd = s.sb("bn", [P, 2, 6]), s.sb("mv", [P, 2, 2]), s.sb("rstd", [P, 2])
        power, spare = s.sb("power", [P, 1]), s.sb("spare", [P, 1])

        ld_w, ld_c, ld_x, ld_t = s.sems("ld_w", 3), s.sem("ld_c"), s.sems("ld_x", T), s.sems("ld_t", T)
        st_r, st_v = [s.sems("st_q", C), s.sems("st_k", C)], s.sems("st_v", T)
        prep_pe, prep_hi, prep_lo, setup = s.sem("prep_pe"), s.sem("prep_hi"), s.sem("prep_lo"), s.sem("setup")
        bn_ready, var_eps, var_ready, rstd_ready, h_ready = (s.sem(n) for n in ("bn", "ve", "var", "rstd", "h"))
        hT_pe, hT_hi, hT_lo = s.sem("hT_pe"), s.sem("hT_hi"), s.sem("hT_lo")
        cT_pe, cT_hi, cT_lo = s.sem("cT_pe"), s.sem("cT_hi"), s.sem("cT_lo")
        q_pe, k_pe, v_pe, r_hi = s.sem("q_pe"), s.sem("k_pe"), s.sem("v_pe"), s.sem("r_hi")
        r_out = s.sem("r_out")
        block = s.block()

        def row0(g, t):
            return g * GR + t * P

        @block.sync
        def _(sp):
            sp.dma_start(ident[:, :], ident_in).then_inc(ld_c, 16)
            for i, w in enumerate((wq, wk, wv)):
                sp.dma_start(raw[i][:, :, :], w.rearrange("(c p) n -> p c n", p=P)).then_inc(ld_w[i], 16)
            for t in range(T):
                sp.dma_start(xt[:, t, :], x1[t * P:(t + 1) * P, :]).then_inc(ld_x[t], 16)
            for t in range(T):
                sp.dma_start(ct[:, t, :], cx[t * P:(t + 1) * P, :]).then_inc(ld_t[t], 16)

            def group(g, last):
                if not last:
                    for t in range(T):
                        sp.wait_ge(h_ready, g * T + (t + 1))
                        sp.dma_start(xt[:, t, :], x1[bass.ds(row0(g, t) + GR, P), :]).then_inc(ld_x[t], 16)
                for i in range(2):
                    for c in range(C):
                        sp.wait_ge(r_out, g * UNITS + (BANKS + i * C + c + 1))
                        for hl in (1, 0):
                            sp.dma_start(qk[i, hl, c * P:(c + 1) * P, bass.ds(g * GR, GR)], res[i][hl][:, c, :].bitcast(F32)
                                         ).then_inc(st_r[i][c], 16)
                        if not last and i == 0:
                            sp.wait_ge(cT_pe, g * T + (c + 1))
                            sp.dma_start(ct[:, c, :], cx[bass.ds(row0(g, c) + GR, P), :]).then_inc(ld_t[c], 16)
                for t in range(T):
                    sp.wait_ge(r_out, g * UNITS + (BANKS + 2 * C + t + 1))
                    sp.dma_start(vd[bass.ds(row0(g, t), P), :], vals[:, t, :]).then_inc(st_v[t], 16)

            with sp.Fori(0, G - 1) as g:
                group(g, False)
            group(G - 1, True)
            for c in range(C):
                sp.wait_ge(st_r[0][c], 32 * G)
                sp.wait_ge(st_r[1][c], 32 * G)
                sp.wait_ge(st_v[c], 16 * G)

        @block.gpsimd
        def _(pool):
            pool.wait_ge(r_out, BANKS)
            with pool.Fori(0, G) as g:
                for t in range(T):
                    pool.wait_ge(var_ready, g * T + (t + 1))
                    pool.tensor_tensor(rstd[:, t % 2:t % 2 + 1], mv[:, t % 2, 1:2], power[:, :], ALU.pow
                                       ).then_inc(rstd_ready, 1)

        @block.vector
        def _(v):
            n = 0
            for i in range(3):
                for c in range(C):
                    n += 1
                    v.wait_ge(prep_hi, n)
                    v.tensor_tensor(W[i][1][:, c, :], ps[:, 2 + n % 2, :], W[i][0][:, c, :], ALU.subtract
                                    ).then_inc(prep_lo, 1)
            v.memset(power[:, :], -0.5).then_inc(r_out, BANKS)

            def layernorm(g, t):
                v.wait_ge(ld_x[t], g * 16 + 16)
                v.bn_stats(bn[:, t % 2, :], xt[:, t, :]).then_inc(bn_ready, 1)
                wait_apart(v, bn_ready, g * T + (t + 1), spare)
                v.bn_aggr(mv[:, t % 2, :], bn[:, t % 2, :]).then_inc(var_eps, 1)
                v.wait_ge(var_eps, g * T + (t + 1))
                v.tensor_scalar(mv[:, t % 2, 1:2], mv[:, t % 2, 1:2], EPS, None, ALU.add).then_inc(var_ready, 1)
                v.wait_ge(rstd_ready, g * T + (t + 1))
                v.tensor_scalar(h[:, t % 2, :], xt[:, t, :], mv[:, t % 2, 0:1], rstd[:, t % 2:t % 2 + 1],
                                ALU.subtract, ALU.mult).then_inc(h_ready, 1)

            def low(bank, dst, t, ready, at, done):
                v.wait_ge(ready, at)
                rows = slice(t * P, (t + 1) * P)
                v.tensor_tensor(dst[1][:, :, rows], ps[:, bank, :].rearrange("p (c n) -> p c n", c=C),
                                dst[0][:, :, rows], ALU.subtract).then_inc(done, 1)

            def result(g, i, c):
                v.wait_ge(r_hi, g * (2 * C) + (i * C + c + 1))
                v.tensor_tensor(res[i][1][:, c, :], ps[:, 2 + (i * C + c) % BANKS, :], res[i][0][:, c, :],
                                ALU.subtract).then_inc(r_out, 1)

            def group(g, last):
                for c in range(C):
                    low(c % 2, cT, c, cT_hi, g * T + (c + 1), cT_lo)
                    result(g, 0, c)
                for c in range(C):
                    if not last:
                        layernorm(g + 1, c)
                        low(c % 2, hT, c, hT_hi, (g + 1) * T + (c + 1), hT_lo)
                    result(g, 1, c)
                for t in range(T):
                    v.wait_ge(v_pe, g * T + (t + 1))
                    v.wait_ge(st_v[t], g * 16)
                    v.tensor_copy(vals[:, t, :], ps[:, 2 + (2 * C + t) % BANKS, :]).then_inc(r_out, 1)

            for t in range(T):
                layernorm(0, t)
                low(t % 2, hT, t, hT_hi, t + 1, hT_lo)
            group(0, False)
            with v.Fori(1, G - 1) as g:
                group(g, False)
            group(G - 1, True)

        @block.scalar
        def _(act):
            n = 0
            for i in range(3):
                for c in range(C):
                    n += 1
                    act.wait_ge(prep_pe, n)
                    act.activation(W[i][0][:, c, :], ps[:, 2 + n % 2, :], ACT.Copy).then_inc(prep_hi, 1)

            def high(bank, dst, t, ready, at, done):
                act.wait_ge(ready, at)
                act.activation(dst[0][:, :, t * P:(t + 1) * P], ps[:, bank, :].rearrange("p (c n) -> p c n", c=C),
                               ACT.Copy).then_inc(done, 1)

            def result(g, i, c):
                act.wait_ge((q_pe, k_pe)[i], g * C + (c + 1))
                act.wait_ge(st_r[i][c], g * 32)
                act.activation(res[i][0][:, c, :], ps[:, 2 + (i * C + c) % BANKS, :], ACT.Copy).then_inc(r_hi, 1)

            def group(g, last):
                for c in range(C):
                    high(c % 2, cT, c, cT_pe, g * T + (c + 1), cT_hi)
                    result(g, 0, c)
                for c in range(C):
                    if not last:
                        high(c % 2, hT, c, hT_pe, (g + 1) * T + (c + 1), hT_hi)
                    result(g, 1, c)

            for t in range(T):
                high(t % 2, hT, t, hT_pe, t + 1, hT_hi)
            group(0, False)
            with act.Fori(1, G - 1) as g:
                group(g, False)
            group(G - 1, True)

        @block.tensor
        def _(pe):
            pe.wait_ge(ld_c, 16)
            n = 0
            for i in range(3):
                pe.wait_ge(ld_w[i], 16)
                for c in range(C):
                    n += 1
                    if n > 2:
                        pe.wait_ge(prep_lo, n - 2)
                    transposes(pe, ps[:, 2 + n % 2, :], [raw[i][:, o, c * P:(c + 1) * P] for o in range(C)],
                               ident[:, :]).then_inc(prep_pe, 1)
            pe.wait_ge(prep_lo, 3 * C)

            def turn_h(g, t, free):
                pe.wait_ge(h_ready, g * T + (t + 1))
                if free:
                    pe.wait_ge(free[0], free[1])
                transposes(pe, ps[:, t % 2, :], [h[:, t % 2, c * P:(c + 1) * P] for c in range(C)], ident[:, :]
                           ).then_inc(hT_pe, 1)

            def group(g, last):
                for c in range(C):
                    pe.wait_ge(ld_t[c], g * 16 + 16)
                    if c < 2:
                        pe.wait_ge(hT_lo, g * T + (T - 1 + c))
                    else:
                        pe.wait_ge(cT_lo, g * T + (c - 1))
                    transposes(pe, ps[:, c % 2, :], [ct[:, c, f * P:(f + 1) * P] for f in range(C)], ident[:, :]
                               ).then_inc(cT_pe, 1)
                    if c == 0:
                        pe.wait_ge(hT_lo, g * T + T)
                    product(g, c, W[0], hT, c, False).then_inc(q_pe, 1)
                for c in range(C):
                    if not last:
                        turn_h(g + 1, c, (cT_lo, g * T + (T - 1 + c)) if c < 2 else (hT_lo, g * T + (T + c - 1)))
                    if c == 0:
                        pe.wait_ge(cT_lo, g * T + T)
                    product(g, C + c, W[1], cT, c, False).then_inc(k_pe, 1)
                for t in range(T):
                    product(g, 2 * C + t, cT, W[2], t, True).then_inc(v_pe, 1)

            def product(g, u, lhs, rhs, m, rows):
                pe.wait_ge(r_out, g * UNITS + (u + 1))
                for c in range(C):
                    last = mm3(pe, ps[:, 2 + u % BANKS, :], [a[:, c, m * P:(m + 1) * P] for a in lhs],
                               [a[:, c, :] for a in rhs], c == 0, c == C - 1)
                return last

            for t in range(T):
                turn_h(0, t, (hT_lo, t - 1) if t >= 2 else None)
            with pe.Fori(0, G - 1) as g:
                group(g, False)
            group(G - 1, True)


def attention(nc, ps, x1, qk, vd, wo, ident_in, masks_in, nmd, x2):
    ROWS = x1.shape[0]
    PAIRS = ROWS // P
    R = P // 2
    U = R // 8
    NU = 2 * U
    K = 3 * HD
    BUF = 3
    LOOPS = (PAIRS - 2) // BUF
    FIRST = 6
    LAG = 2
    PT = 4
    SCALE = float(np.float32(1.0) / np.sqrt(np.float32(HD)))
    assert LOOPS * BUF == PAIRS - 2 and NU % PT == 0
    with ExitStack() as ctx:
        s = Scope(nc, ctx, "c")

        def banks(n, w):
            flat = ps[:, n:n + (2 if w > R // 2 else 1), :].rearrange("p a n -> p (a n)")
            return flat.rearrange("p (c r) -> p c r", c=HEADS)[:, :, 0:w]

        def scores(k):
            return banks(3 * (k % 2), 8 * (k % U + 1))

        def shifted(k):
            w = R - 8 * (k % U)
            return banks(3 * (k % 2) + (1 if w > R // 2 else 2), w)

        av = ps[:, 6, 0:256].rearrange("p (c r) -> p c r", c=C)
        den = ps[:, 6, 256:512].rearrange("p (c r) -> p c r", c=C)
        misc = ps[:, 7, :]
        qs = [s.sb(f"qs{i}", [P, HEADS, P], F32R) for i in range(BUF)]
        ks = [s.sb(f"ks{i}", [P, HEADS, P], F32R) for i in range(BUF)]
        qg, kg = s.sb("qg", [P, NU, P], F32R), s.sb("kg", [P, NU, P], F32R)
        vt = [s.sb(f"vt{i}", [P, NU, HD]) for i in range(BUF)]
        xt = [s.sb(f"xt{i}", [P, D]) for i in range(BUF)]
        W, raw = s.pair("w", [P, C, D]), s.sb("raw", [P, C, D])
        ident, identr = s.sb("ident", [P, P]), s.sb("identr", [P, P], F32R)
        maskf = [s.sb(f"maskf{i}", [P, HEADS, 8]) for i in range(2)]
        mask = [s.sb(f"mask{i}", [P, HEADS, 8], BF16) for i in range(2)]
        identb = s.sb("identb", [P, P], BF16)
        ones = s.sb("ones", [P, HD])
        pt = [s.sb(f"pt{i}", [P, HEADS * R]) for i in range(PT)]
        mx = s.sb("mx", [P, NU])
        nm = [s.sb(f"nm{i}", [P, P], F32R) for i in range(2)]
        nmt = [s.sb(f"nmt{i}", [2 * U, P], F32R) for i in range(2)]
        sums, rec, o = s.sb("sums", [P, 2 * C * R]), s.sb("rec", [P, C * R]), s.sb("o", [P, C, R])
        oT = s.pair("oT", [P, C, P])

        ld_c, ld_w, setup = s.sem("ld_c"), s.sem("ld_w"), s.sem("setup")
        ld_qk, ld_v, ld_x, st_x = s.sems("ld_qk", BUF), s.sems("ld_v", BUF), s.sems("ld_x", BUF), s.sems("st_x", BUF)
        prep_pe, prep_hi, prep_lo = s.sem("prep_pe"), s.sem("prep_hi"), s.sem("prep_lo")
        g_pe, g_max = s.sem("g_pe"), s.sem("g_max")
        nm_hi, nm_lo, nm_pe, nm_t, nm_st = (s.sem(n) for n in ("nm_hi", "nm_lo", "nm_pe", "nm_t", "nm_st"))
        nm_ld = s.sems("nm_ld", 2)
        qg_done, kg_done = s.sem("qg_done"), s.sem("kg_done")
        t_pe, t_exp, a_pe = s.sem("t_pe"), s.sem("t_exp"), s.sem("a_pe")
        o_out, r_done, o_done, o_hi, o_lo = s.sem("o_out"), s.sem("r_done"), s.sem("o_done"), s.sem("o_hi"), s.sem("o_lo")
        y_pe, y_done = s.sem("y_pe"), s.sem("y_done")
        block = s.block()
        vf = vd.rearrange("r (c e) -> (r c) e", e=HD)

        def probs(k):
            w = R - 8 * (k % U)
            rows = R if w > R // 2 else R // 2
            return pt[k % PT][:, 0:HEADS * rows].rearrange("p (c r) -> p c r", c=HEADS)[:, :, 0:w]

        def parts(w):
            return [slice(0, 8), slice(8, 16)] if w > R // 2 else [slice(0, 16)]

        @block.sync
        def _(sp):
            sp.dma_start(ident[:, :], ident_in).then_inc(ld_c, 16)
            for i in range(2):
                sp.dma_start(maskf[i][:, :, :], masks_in[i]).then_inc(ld_c, 16)
            sp.dma_start(raw[:, :, :], wo.rearrange("(c p) n -> p c n", p=P)).then_inc(ld_w, 16)

            def load_qk(p, a):
                for g in range(3):
                    for i, t in enumerate((qs[a], ks[a])):
                        hl = (0, 0, 1)[g] if i == 0 else (0, 1, 0)[g]
                        sp.dma_start(t[HD * g:HD * (g + 1), :, :].bitcast(F32),
                                     qk[i, hl].rearrange("(c d) r -> d c r", d=HD)[:, :, bass.ds(p * P, P)]
                                     ).then_inc(ld_qk[a], 16)

            def load_vx(p, a):
                sp.dma_start(vt[a][:, :, :], vf[bass.ds(p * (P * HEADS), P * HEADS), :].rearrange(
                    "(t p) e -> p t e", p=P)).then_inc(ld_v[a], 16)
                sp.dma_start(xt[a][:, :], x1[bass.ds(p * P, P), :]).then_inc(ld_x[a], 16)

            def maxima(p, a, hd):
                waits = [(nm_t, 2 * p + (hd + 1))]
                if not isinstance(p, int) or p > 0:
                    waits.append((nm_ld[hd], 16 * p))
                for sem, value in waits if hd else waits[::-1]:
                    sp.wait_ge(sem, value)
                for hl in range(2):
                    sp.dma_start(nmd[hd, hl].rearrange("c u r -> u c r"), nmt[hd][U * hl:U * (hl + 1), :].bitcast(F32)
                                 .rearrange("u (c r) -> u c r", c=HEADS)).then_inc(nm_st, 16)
                sp.wait_ge(nm_st, 64 * p + 32 * (hd + 1))
                sp.dma_start(qs[a][K:K + 2, :, R * hd:R * (hd + 1)].bitcast(F32),
                             nmd[hd].rearrange("l c u r -> l c (u r)")).then_inc(nm_ld[hd], 16)

            def store(i, a):
                p = i * BUF + a
                sp.wait_ge(y_done, p + 1)
                sp.dma_start(x2[bass.ds(p * P, P), :], xt[a][:, :]).then_inc(st_x[a], 16)

            def turn(i, a):
                p = i * BUF + a
                b = (a + 2) % BUF
                sp.wait_ge(t_pe, p * NU)
                load_qk(p + 2, b)
                maxima(p, a, 1)
                if not isinstance(p, int) or p > 0:
                    store(i - (a == 0), b)
                    sp.wait_ge(st_x[b], i * 16 + (16 if b < a else 0))
                load_vx(p + 2, b)
                maxima(p + 1, (a + 1) % BUF, 0)

            for p in range(2):
                load_qk(p, p)
                load_vx(p, p)
            maxima(0, 0, 0)
            for a in range(BUF):
                turn(0, a)
            with sp.Fori(1, LOOPS) as i:
                for a in range(BUF):
                    turn(i, a)
            maxima(PAIRS - 2, 0, 1)
            store(LOOPS - 1, BUF - 1)
            maxima(PAIRS - 1, 1, 0)
            maxima(PAIRS - 1, 1, 1)
            store(LOOPS, 0)
            store(LOOPS, 1)
            for a in range(BUF):
                sp.wait_ge(st_x[a], 16 * len(range(a, PAIRS, BUF)))

        @block.vector
        def _(v):
            v.memset(kg[K:K + 2, :, :].bitcast(F32), 1.0).then_inc(setup, 1)
            v.memset(ones[:, :], 1.0).then_inc(setup, 1)
            v.wait_ge(ld_c, 48)
            v.tensor_copy(identr[:, :], ident[:, :]).then_inc(setup, 1)
            v.tensor_copy(identb[:, :], ident[:, :]).then_inc(setup, 1)
            for i in range(2):
                v.tensor_copy(mask[i][:, :, :], maskf[i][:, :, :]).then_inc(setup, 1)
            for hd in range(2):
                v.tensor_scalar(nm[hd][:, :], ident[:, :], 0.0, None, ALU.mult).then_inc(setup, 1)
            for c in range(C):
                v.wait_ge(prep_hi, c + 1)
                v.tensor_tensor(W[1][:, c, :], ps[:, 2 + c, :], W[0][:, c, :], ALU.subtract).then_inc(prep_lo, 1)

            def first_pass(p, k):
                v.wait_ge(g_pe, p * NU + (k + 1))
                v.tensor_reduce(mx[:, k:k + 1], scores(k), mybir.AxisListType.XY, ALU.max,
                                negate=True).then_inc(g_max, 1)

            def negate(p, hd):
                v.wait_ge(g_max, p * NU + U * (hd + 1))
                if not isinstance(p, int) or p > 0:
                    v.wait_ge(nm_pe, 2 * p + (hd - 1))
                m = mx[:, U * hd:U * (hd + 1)]
                v.tensor_copy(nm[hd][:, 0:U], m).then_inc(nm_hi, 1)
                v.wait_ge(nm_hi, 2 * p + (hd + 1))
                v.tensor_tensor(nm[hd][:, U:2 * U], m, nm[hd][:, 0:U], ALU.subtract).then_inc(nm_lo, 1)

            def normalize(p, hd):
                v.wait_ge(a_pe, p * NU + U * (hd + 1))
                v.tensor_copy(sums[:, :], ps[:, 6, :]).then_inc(o_out, 1)
                v.wait_ge(o_out, 2 * p + (hd + 1))
                v.reciprocal(rec[:, :], sums[:, C * R:]).then_inc(r_done, 1)
                v.wait_ge(r_done, 2 * p + (hd + 1))
                v.tensor_tensor(o[:, :, :].rearrange("p c r -> p (c r)"), sums[:, 0:C * R], rec[:, :], ALU.mult
                                ).then_inc(o_done, 1)

            def low(p, hd):
                v.wait_ge(o_hi, 2 * p + (hd + 1))
                rows = slice(R * hd, R * (hd + 1))
                v.tensor_tensor(oT[1][:, :, rows], o[:, :, :], oT[0][:, :, rows], ALU.subtract).then_inc(o_lo, 1)

            def output(i, a):
                p = i * BUF + a
                v.wait_ge(y_pe, p + 1)
                v.wait_ge(ld_x[a], i * 16 + 16)
                v.tensor_tensor(xt[a][:, :], misc, xt[a][:, :], ALU.add).then_inc(y_done, 1)

            def turn(i, a, more):
                p = i * BUF + a
                for slot in range(FIRST, FIRST + NU):
                    if slot // NU + 1 <= more:
                        first_pass(p + (slot // NU + 1), slot % NU)
                    if more >= 1 and slot in (U, NU):
                        negate(p + 1, slot // U - 1)
                    if slot in (U + 1, NU + 1):
                        normalize(p, slot // U - 1)
                    if slot in (U + 3, NU + 3):
                        low(p, slot // U - 1)
                output(i, a)

            for k in range(NU):
                first_pass(0, k)
                if k == U:
                    negate(0, 0)
            negate(0, 1)
            for k in range(FIRST):
                first_pass(1, k)
            with v.Fori(0, LOOPS) as i:
                for a in range(BUF):
                    turn(i, a, 2)
            turn(LOOPS, 0, 1)
            turn(LOOPS, 1, 0)

        @block.scalar
        def _(act):
            for c in range(C):
                act.wait_ge(prep_pe, c + 1)
                act.activation(W[0][:, c, :], ps[:, 2 + c, :], ACT.Copy).then_inc(prep_hi, 1)

            def unit(p, k):
                n = p * NU + k
                act.wait_ge(t_pe, n + 1)
                if not isinstance(n, int) or n >= PT:
                    act.wait_ge(a_pe, n - (PT - 1))
                act.activation(probs(k), shifted(k), ACT.Exp, scale=SCALE).then_inc(t_exp, 1)

            def maxima(p, hd):
                act.wait_ge(nm_pe, 2 * p + (hd + 1))
                if not isinstance(p, int) or p > 0:
                    act.wait_ge(nm_st, 64 * p + 32 * (hd - 1))
                act.activation(nmt[hd][:, :], misc[0:2 * U, 0:P], ACT.Copy).then_inc(nm_t, 1)

            def gather(i, a, hd, done, before, dst, src, order, parts):
                q = i * BUF + a
                act.wait_ge(ld_qk[a % BUF], (i + a // BUF) * 96 + 96)
                if not isinstance(q, int) or q > 0:
                    act.wait_ge(before, q * NU - NU + U * (hd + 1))
                out = dst[0:K, U * hd:U * (hd + 1), :]
                rows = src[a % BUF][0:K, :, R * hd:R * (hd + 1)].rearrange("p c (u r) -> p u c r", u=U)
                for u in range(0, U, U // parts):
                    o4 = out[:, u:u + U // parts, :].rearrange(order, c=HEADS)
                    i4 = rows[:, u:u + U // parts]
                    last = act.activation(o4, i4.bitcast(F32), ACT.Copy)
                last.then_inc(done, 1)

            def gather_q(i, a, hd):
                gather(i, a, hd, qg_done, g_pe, qg, qs, "p u (c r) -> p u c r", 1)

            def gather_k(i, a, hd):
                gather(i, a, hd, kg_done, t_pe, kg, ks, "p u (r c) -> p u c r", 1)

            def high(p, hd):
                act.wait_ge(o_done, 2 * p + (hd + 1))
                act.activation(oT[0][:, :, R * hd:R * (hd + 1)], o[:, :, :], ACT.Copy).then_inc(o_hi, 1)

            def turn(i, a, more):
                p = i * BUF + a
                for slot in range(FIRST, FIRST + NU):
                    if slot // NU <= more:
                        unit(p + slot // NU, slot % NU)
                    if slot in (U + 2, NU + 2):
                        if more >= 1:
                            maxima(p + 1, slot // U - 1)
                        high(p, slot // U - 1)
                    if slot in (U + 4, NU + 3) and more >= 2:
                        gather_q(i, a + 2, slot // U - 1)
                    if slot in (U + 5, NU + 4) and more >= 1:
                        gather_k(i, a + 1, slot // U - 1)

            for hd in range(2):
                gather_q(0, 0, hd)
            for hd in range(2):
                gather_k(0, 0, hd)
            gather_q(0, 1, 0)
            maxima(0, 0)
            gather_q(0, 1, 1)
            maxima(0, 1)
            for k in range(FIRST):
                unit(0, k)
            with act.Fori(0, LOOPS) as i:
                for a in range(BUF):
                    turn(i, a, 2)
            turn(LOOPS, 0, 1)
            turn(LOOPS, 1, 0)

        @block.tensor
        def _(pe):
            pe.wait_ge(ld_c, 48)
            pe.wait_ge(ld_w, 16)
            for c in range(C):
                transposes(pe, ps[:, 2 + c, :], [raw[:, e, c * P:(c + 1) * P] for e in range(C)], ident[:, :]
                           ).then_inc(prep_pe, 1)
            pe.wait_ge(prep_lo, C)
            pe.wait_ge(setup, 8)

            def first_pass(i, a, k):
                q = i * BUF + a
                n = q * NU + k
                a = a % BUF
                if k % U == 0:
                    pe.wait_ge(qg_done, 2 * q + (k // U + 1))
                slot_free(n, n - NU)
                hd, w, out = k // U, 8 * (k % U + 1), scores(k)
                for cs in parts(w):
                    pe.matmul(out[:, cs, :], qg[0:K, k, :], ks[a][0:K, cs, R * hd:R * hd + w],
                              start=True, stop=False)
                for cs in parts(w):
                    last = pe.matmul(out[:, cs, w - 8:w], identb[:, :], mask[0][:, cs, :], start=False, stop=True)
                last.then_inc(g_pe, 1)

            def slot_free(g, t):
                if not isinstance(g, int) or g >= 2:
                    pe.wait_ge(g_max, g - 1)
                if not isinstance(t, int) or t >= 2:
                    pe.wait_ge(t_exp, t - 1)

            def second_pass(i, a, k, alone=False):
                p = i * BUF + a
                n = p * NU + k
                a = a % BUF
                hd, at = k // U, 8 * (k % U)
                if k % U == 0:
                    pe.wait_ge(nm_ld[hd], p * 16 + 16)
                    pe.wait_ge(kg_done, 2 * p + (hd + 1))
                if alone:
                    slot_free(min(n + NU, PAIRS * NU + 1), n)
                w, out = R - at, shifted(k)
                for cs in parts(w):
                    pe.matmul(out[:, cs, 0:8], identb[:, :], mask[1][:, cs, :], start=True, stop=False,
                              skip_group_check=True)
                for cs in parts(w):
                    last = pe.matmul(out[:, cs, :], kg[0:K + 2, k, :], qs[a][0:K + 2, cs, R * hd + at:R * (hd + 1)],
                                     start=False, stop=True, skip_group_check=True)
                last.then_inc(t_pe, 1)

            def values(i, a, k):
                p = i * BUF + a
                a, j = a % BUF, i + a // BUF
                hd, at = k // U, 8 * (k % U)
                pe.wait_ge(t_exp, p * NU + (k + 1))
                if k == 0:
                    pe.wait_ge(ld_v[a], j * 16 + 16)
                if k % U == 0:
                    pe.wait_ge(o_out, 2 * p + hd)
                rhs = probs(k).rearrange("p (c q) r -> p c q r", q=4)
                for lhsT, out in ((vt[a][:, k, :], av), (ones[:, :], den)):
                    for q in range(4):
                        last = pe.matmul(out[HD * q:HD * (q + 1), :, at:R], lhsT, rhs[:, :, q, :],
                                         start=(at == 0 and out is av), stop=(k % U == U - 1), skip_group_check=True)
                last.then_inc(a_pe, 1)

            def maxima(p, hd):
                pe.wait_ge(nm_lo, 2 * p + (hd + 1))
                if hd == 1:
                    pe.wait_ge(nm_t, 2 * p + 1)
                pe.matmul(misc[:, 0:P], nm[hd][:, :], identr[:, :], start=True, stop=True).then_inc(nm_pe, 1)

            def output(p, more):
                pe.wait_ge(o_lo, 2 * p + 2)
                if more:
                    pe.wait_ge(nm_t, 2 * p + 4)
                else:
                    pe.wait_ge(y_done, p)
                for c in range(C):
                    last = mm3(pe, misc, [t[:, c, :] for t in oT], [t[:, c, :] for t in W], c == 0, c == C - 1)
                last.then_inc(y_pe, 1)

            def turn(i, a, more):
                p = i * BUF + a
                for slot in range(FIRST, FIRST + NU):
                    if slot // NU + 1 <= more:
                        first_pass(i, a + slot // NU + 1, slot % NU)
                    if slot // NU <= more:
                        second_pass(i, a + slot // NU, slot % NU, slot // NU + 1 > more)
                    if (slot - LAG) // NU <= more:
                        values(i, a + (slot - LAG) // NU, (slot - LAG) % NU)
                    if more >= 1 and slot in (U + 2, NU + 2):
                        maxima(p + 1, slot // U - 1)
                    if slot == NU + 4:
                        output(p, more >= 1)

            for k in range(NU):
                first_pass(0, 0, k)
                if k == U + 2:
                    maxima(0, 0)
            maxima(0, 1)
            for k in range(FIRST):
                first_pass(0, 1, k)
                second_pass(0, 0, k)
                if k >= LAG:
                    values(0, 0, k - LAG)
            with pe.Fori(0, LOOPS) as i:
                for a in range(BUF):
                    turn(i, a, 2)
            turn(LOOPS, 0, 1)
            turn(LOOPS, 1, 0)


def feed_forward(nc, ps, x2, w, bias, aT, b, ident_in, out):
    ROWS = x2.shape[0]
    TILES = ROWS // P
    RANK = aT.shape[0]
    BUF = 4
    LOOPS = (TILES - 2) // BUF
    ROUND = 1.5 * 2.0 ** 23
    with ExitStack() as ctx:
        s = Scope(nc, ctx, "d")
        raw, W = s.sb("raw", [P, C, D]), s.pair("w", [P, C, D])
        whole = s.sb("whole", [P, C, D])
        aTs, bs = s.sb("aT", [RANK, D]), s.sb("b", [RANK, D])
        ident, bb, power = s.sb("ident", [P, P]), s.sb("bias", [P, D]), s.sb("power", [P, 1])
        spare = s.sb("spare", [P, 1])
        top, topall, step, inv = (s.sb(n, [P, 1]) for n in ("top", "topall", "step", "inv"))
        xt = [s.sb(f"xt{i}", [P, D]) for i in range(BUF)]
        yt = [s.sb(f"yt{i}", [P, D]) for i in range(BUF)]
        h = s.sb("h", [P, 2, D])
        hT = [s.pair(f"hT{i}", [P, C, P]) for i in range(2)]
        bn, mv, rstd = s.sb("bn", [P, 2, 6]), s.sb("mv", [P, 2, 2]), s.sb("rstd", [P, 2])

        ld_w, ld_c, ld_x, st_y = s.sem("ld_w"), s.sem("ld_c"), s.sems("ld_x", BUF), s.sems("st_y", BUF)
        setup, q_step, top_ready, lora, w_hi, w_lo = (s.sem(n) for n in (
            "setup", "q_step", "top_ready", "lora", "w_hi", "w_lo"))
        bn_ready, var_eps, var_ready, rstd_ready, h_ready = (s.sem(n) for n in ("bn", "ve", "var", "rstd", "h"))
        hT_pe, hT_hi, hT_lo, xb_done, y_pe, y_done = (s.sem(n) for n in (
            "hT_pe", "hT_hi", "hT_lo", "xb", "y_pe", "y_done"))
        block = s.block()

        @block.sync
        def _(sp):
            sp.dma_start(raw[:, :, :], w.rearrange("(c p) n -> p c n", p=P)).then_inc(ld_w, 16)
            sp.dma_start(aTs[:, :], aT).then_inc(ld_c, 16)
            sp.dma_start(bs[:, :], b).then_inc(ld_c, 16)
            sp.dma_start(ident[:, :], ident_in).then_inc(ld_c, 16)
            sp.dma_start(bb[:, :], bias.partition_broadcast(P)).then_inc(ld_c, 16)
            for a in range(BUF):
                sp.dma_start(xt[a][:, :], x2[a * P:(a + 1) * P, :]).then_inc(ld_x[a], 16)

            def turn(i, a, more):
                t = i * BUF + a
                sp.wait_ge(y_done, t + 1)
                sp.dma_start(out[bass.ds(t * P, P), :], yt[a][:, :]).then_inc(st_y[a], 16)
                if more:
                    sp.dma_start(xt[a][:, :], x2[bass.ds((t + BUF) * P, P), :]).then_inc(ld_x[a], 16)

            with sp.Fori(0, LOOPS) as i:
                for a in range(BUF):
                    turn(i, a, True)
            for t in range(LOOPS * BUF, TILES):
                turn(t // BUF, t % BUF, t + BUF < TILES)
            for a in range(BUF):
                sp.wait_ge(st_y[a], 16 * (TILES // BUF))

        @block.gpsimd
        def _(pool):
            pool.memset(power[:, :], -0.5).then_inc(setup, 1)
            pool.wait_ge(top_ready, 1)
            pool.wait_ge(setup, 1)
            pool.partition_all_reduce(topall[:, :], top[:, :], P, RED.max).then_inc(setup, 1)
            pool.wait_ge(setup, 2)
            pool.wait_ge(ld_c, 64)

            with pool.Fori(0, TILES // BUF) as i:
                for a in range(BUF):
                    t = i * BUF + a
                    pool.wait_ge(var_ready, t + 1)
                    pool.tensor_tensor(rstd[:, a % 2:a % 2 + 1], mv[:, a % 2, 1:2], power[:, :], ALU.pow
                                       ).then_inc(rstd_ready, 1)
                    pool.wait_ge(h_ready, t + 1)
                    pool.tensor_tensor(xt[a][:, :], xt[a][:, :], bb[:, :], ALU.add).then_inc(xb_done, 1)

        @block.vector
        def _(v):
            n = [0]

            def link(ins):
                n[0] += 1
                ins.then_inc(q_step, 1)
                v.wait_ge(q_step, n[0])

            v.wait_ge(ld_w, 16)
            flat = raw[:, :, :].rearrange("p c n -> p (c n)")
            v.tensor_reduce(top[:, :], flat, AX, ALU.max, apply_absolute_value=True).then_inc(top_ready, 1)
            v.wait_ge(setup, 2)
            link(v.tensor_scalar(step[:, :], topall[:, :], float(np.float32(1.0) / np.float32(7.0)), None, ALU.mult))
            link(v.reciprocal(inv[:, :], step[:, :]))
            link(v.tensor_scalar(flat, flat, inv[:, :], ROUND, ALU.mult, ALU.add))
            link(v.tensor_scalar(flat, flat, ROUND, 7.0, ALU.subtract, ALU.min))
            link(v.tensor_scalar(flat, flat, -8.0, None, ALU.max))
            for c in range(C):
                v.wait_ge(lora, c + 1)
                link(v.scalar_tensor_tensor(out=whole[:, c, :], in0=raw[:, c, :], scalar=step[:, 0:1],
                                            in1=ps[:, 2 + c, :], op0=ALU.mult, op1=ALU.add))
                v.tensor_copy(W[0][:, c, :], whole[:, c, :]).then_inc(w_hi, 1)
                v.wait_ge(w_hi, c + 1)
                v.tensor_tensor(W[1][:, c, :], whole[:, c, :], W[0][:, c, :], ALU.subtract).then_inc(w_lo, 1)

            def layernorm(i, a):
                t = i * BUF + a
                b, j = a % BUF, i + a // BUF
                x = xt[b]
                v.wait_ge(ld_x[b], j * 16 + 16)
                v.bn_stats(bn[:, a % 2, :], x[:, :]).then_inc(bn_ready, 1)
                wait_apart(v, bn_ready, t + 1, spare)
                v.bn_aggr(mv[:, a % 2, :], bn[:, a % 2, :]).then_inc(var_eps, 1)
                v.wait_ge(var_eps, t + 1)
                v.tensor_scalar(mv[:, a % 2, 1:2], mv[:, a % 2, 1:2], EPS, None, ALU.add).then_inc(var_ready, 1)
                v.wait_ge(rstd_ready, t + 1)
                v.tensor_scalar(h[:, a % 2, :], x[:, :], mv[:, a % 2, 0:1], rstd[:, a % 2:a % 2 + 1],
                                ALU.subtract, ALU.mult).then_inc(h_ready, 1)

            def low(i, a):
                v.wait_ge(hT_hi, i * BUF + (a + 1))
                v.tensor_tensor(hT[a % 2][1][:, :, :], ps[:, a % 2, :].rearrange("p (c n) -> p c n", c=C),
                                hT[a % 2][0][:, :, :], ALU.subtract).then_inc(hT_lo, 1)

            def output(i, a):
                t = i * BUF + a
                v.wait_ge(y_pe, t + 1)
                v.wait_ge(xb_done, t + 1)
                v.wait_ge(st_y[a], i * 16)
                v.tensor_tensor(yt[a][:, :], ps[:, 2 + a, :], xt[a][:, :], ALU.add).then_inc(y_done, 1)

            def turn(i, a, more):
                if more >= 2:
                    layernorm(i, a + 2)
                if more >= 1:
                    low(i, a + 1)
                output(i, a)

            layernorm(0, 0)
            layernorm(0, 1)
            low(0, 0)
            for a in range(BUF):
                turn(0, a, 2)
            with v.Fori(1, LOOPS) as i:
                for a in range(BUF):
                    turn(i, a, 2)
            for t in range(LOOPS * BUF, TILES):
                turn(t // BUF, t % BUF, TILES - 1 - t)

        @block.scalar
        def _(act):
            with act.Fori(0, TILES // BUF) as i:
                for a in range(BUF):
                    act.wait_ge(hT_pe, i * BUF + (a + 1))
                    act.activation(hT[a % 2][0][:, :, :], ps[:, a % 2, :].rearrange("p (c n) -> p c n", c=C),
                                   ACT.Copy).then_inc(hT_hi, 1)

        @block.tensor
        def _(pe):
            pe.wait_ge(ld_c, 64)
            for c in range(C):
                pe.matmul(ps[:, 2 + c, :], aTs[:, c * P:(c + 1) * P], bs[:, :], start=True, stop=True
                          ).then_inc(lora, 1)

            def turn_h(i, a):
                t = i * BUF + a
                pe.wait_ge(h_ready, t + 1)
                if not isinstance(t, int) or t >= 2:
                    pe.wait_ge(hT_lo, t - 1)
                transposes(pe, ps[:, a % 2, :], [h[:, a % 2, c * P:(c + 1) * P] for c in range(C)], ident[:, :]
                           ).then_inc(hT_pe, 1)

            def product(i, a):
                t = i * BUF + a
                pe.wait_ge(hT_lo, t + 1)
                if not isinstance(t, int) or t >= BUF:
                    pe.wait_ge(y_done, t - (BUF - 1))
                for c in range(C):
                    last = mm3(pe, ps[:, 2 + a, :], [u[:, c, :] for u in hT[a % 2]], [u[:, c, :] for u in W],
                               c == 0, c == C - 1)
                last.then_inc(y_pe, 1)

            turn_h(0, 0)
            pe.wait_ge(w_lo, C)
            for a in range(BUF):
                turn_h(0, a + 1)
                product(0, a)
            with pe.Fori(1, LOOPS) as i:
                for a in range(BUF):
                    turn_h(i, a + 1)
                    product(i, a)
            for t in range(LOOPS * BUF, TILES):
                if t + 1 < TILES:
                    turn_h(t // BUF, t % BUF + 1)
                product(t // BUF, t % BUF)


def decoder(nc, x, cx, Wq, Wk, Wv, Wo, bo, wq, wk, wv, wo, w, bias, aT, b, ident, masks_in, out):
    rows = x.shape[0] * x.shape[1]
    x1 = nc.dram_tensor("x1", (rows, D), F32, kind="Internal").ap()
    x2 = nc.dram_tensor("x2", (rows, D), F32, kind="Internal").ap()
    qk = nc.dram_tensor("qk", (2, 2, D, rows), F32, kind="Internal").ap()
    vd = nc.dram_tensor("vd", (rows, D), F32, kind="Internal").ap()
    nmd = nc.dram_tensor("nmd", (2, 2, HEADS, P // 16, 8), F32, kind="Internal").ap()
    with nc.psum_tensor("psum", [P, 8, 512], F32) as ps:
        linear_attention(nc, ps, x, Wq, Wk, Wv, Wo, bo, ident, x1)
        projections(nc, ps, x1, cx.rearrange("b n d -> (b n) d"), wq, wk, wv, ident, qk, vd)
        attention(nc, ps, x1, qk, vd, wo, ident, masks_in, nmd, x2)
        feed_forward(nc, ps, x2, w, bias, aT, b, ident, out.rearrange("b n d -> (b n) d"))


def masks():
    c, r = np.divmod(np.arange(P), 8)
    own = np.arange(HEADS)[:, None] + HEADS * np.arange(8)[None, :]
    keys_after = np.where(own[None] <= (HEADS * r + c)[:, None, None], 0.0, MASKED)
    queries_before = np.where(np.arange(P)[:, None, None] <= own[None], 0.0, MASKED)
    return np.stack([keys_after, queries_before]).astype(np.float32)


_INS = ['x', 'ctx_1024', 'L0_attn_Wq', 'L0_attn_Wk', 'L0_attn_Wv', 'L0_attn_Wo', 'L0_attn_bo', 'L0_xattn_wq',
        'L0_xattn_wk', 'L0_xattn_wv', 'L0_xattn_wo', 'L0_ffn_kernel', 'L0_ffn_bias', 'L0_ffn_a', 'L0_ffn_b']


def kernel(**inputs):
    import concourse.bacc as _bacc
    from concourse.bass_utils import run_bass_kernel_spmd as _run

    nc = _bacc.Bacc("TRN2", target_bir_lowering=False, num_devices=1)
    arrays, args = {}, []

    def add(name, a):
        arrays[f"in_{name}_dram"] = a
        args.append(nc.dram_tensor(f"in_{name}_dram", a.shape, mybir.dt.from_np(a.dtype), kind="ExternalInput").ap())

    for name in _INS:
        a = np.asarray(inputs[name])
        add(name, np.ascontiguousarray(a.T if name == 'L0_ffn_a' else a))
    add("ident", np.eye(P, dtype=np.float32))
    add("masks", masks())
    args.append(nc.dram_tensor("out_0_dram", (4, 1024, D), F32, kind="ExternalOutput").ap())
    decoder(nc, *args)
    r = _run(nc, [arrays], core_ids=[0])
    return r.results[0]["out_0_dram"]
```

```python
from contextlib import ExitStack

import numpy as np

import concourse.bass as bass
from concourse import mybir

F32 = mybir.dt.float32
F32R = mybir.dt.float32r
BF16 = mybir.dt.bfloat16
ALU = mybir.AluOpType
ACT = mybir.ActivationFunctionType
RED = bass.bass_isa.ReduceOp
AX = mybir.AxisListType.X

P = 128
D = 512
C = D // P
HEADS = 16
HD = D // HEADS
EPS = 1e-5
MASKED = -1.0e30


def mm3(pe, out, lhsT, rhs, first, last):
    (lh, ll), (rh, rl) = lhsT, rhs
    pe.matmul(out, lh, rh, start=first, stop=False)
    pe.matmul(out, lh, rl, start=False, stop=False)
    return pe.matmul(out, ll, rh, start=False, stop=last)


def transposes(pe, bank, src, ident):
    for i, s in enumerate(src):
        last = pe.transpose(bank[:, i * P:(i + 1) * P], s, ident)
    return last


def wait_apart(v, sem, value, spare):
    v.wait_ge(sem, value)
    v.memset(spare[:, :], 0.0)


class Scope:

    def __init__(self, nc, ctx, tag):
        self.nc, self.ctx, self.tag, self.held = nc, ctx, tag, []

    def block(self):
        self.ctx.callback(self.release)
        return self.ctx.enter_context(self.nc.Block())

    def release(self):
        self.nc.clear_and_free_semaphores(self.held)
        self.nc.all_engine_barrier()

    def sb(self, name, shape, dt=F32):
        return self.ctx.enter_context(self.nc.sbuf_tensor(f"{self.tag}_{name}", shape, dt))

    def pair(self, name, shape):
        return self.sb(name + "_hi", shape, F32R), self.sb(name + "_lo", shape, F32R)

    def sem(self, name):
        self.held.append(self.nc.alloc_semaphore(f"{self.tag}_{name}"))
        return self.held[-1]

    def sems(self, name, n):
        return [self.sem(f"{name}{i}") for i in range(n)]


def linear_attention(nc, ps, x, Wq, Wk, WvT, Wo, bo, ident_in, x1):
    B, N, _ = x.shape
    T = N // P
    H = 4
    SCALE = float(1.0 / np.sqrt(np.float32(HD))) / D
    with ExitStack() as ctx:
        s = Scope(nc, ctx, "a")
        W = {n: s.pair(f"w{n}", [P, C, D]) for n in ("q", "k", "vo")}
        xt = s.sb("xt", [P, T, D])
        h = s.sb("h", [P, H, D])
        hn = s.pair("hn", [P, T, D])
        hT = s.pair("hT", [P, C * N])
        hT_v = [a[:, :].rearrange("p (c n) -> p c n", c=C) for a in hT]
        k_v = [a[:, :].rearrange("p (t d) -> p t d", t=T) for a in hT]
        c_v = [a[:, 0:C * D].rearrange("p (c e) -> p c e", c=C) for a in hT]
        qT = s.pair("qT", [P, C, N])
        ek = s.sb("ek", [P, C, N])
        M = s.pair("M", [P, C, D])
        eq = s.sb("eq", [P, 2, D])
        ident, bob = s.sb("ident", [P, P]), s.sb("bob", [P, D])
        bn, mv, rstd = s.sb("bn", [P, H, 6]), s.sb("mv", [P, H, 2]), s.sb("rstd", [P, H])
        power, spare = s.sb("power", [P, 1]), s.sb("spare", [P, 1])
        nmq, smq, rsq = (s.sb(n, [P, T]) for n in ("nmq", "smq", "rsq"))
        nmk, smk, rsk = (s.sb(n, [P, C]) for n in ("nmk", "smk", "rsk"))

        ld_w, ld_c, ld_x, st_x = s.sems("ld_w", 4), s.sem("ld_c"), s.sems("ld_x", T), s.sems("st_x", T)
        prep_hi, prep_lo, prep_pe, setup = s.sem("prep_hi"), s.sem("prep_lo"), s.sem("prep_pe"), s.sem("setup")
        bn_ready, var_eps, var_ready, rstd_ready, h_ready = (s.sem(n) for n in ("bn", "ve", "var", "rstd", "h"))
        hn_hi, hn_lo, xb_done = s.sem("hn_hi"), s.sem("hn_lo"), s.sem("xb")
        hT_pe, hT_hi, hT_lo = s.sem("hT_pe"), s.sem("hT_hi"), s.sem("hT_lo")
        q_pe, q_max, q_exp = s.sem("q_pe"), s.sem("q_max"), s.sem("q_exp")
        qT_pe, qT_hi, qT_lo = s.sem("qT_pe"), s.sem("qT_hi"), s.sem("qT_lo")
        k_pe, k_max, k_exp = s.sem("k_pe"), s.sem("k_max"), s.sem("k_exp")
        kn_pe, kn_hi, kn_lo = s.sem("kn_pe"), s.sem("kn_hi"), s.sem("kn_lo")
        M_pe, M_hi, M_lo = s.sem("M_pe"), s.sem("M_hi"), s.sem("M_lo")
        rq_ready, rk_ready, c_scale = s.sem("rq"), s.sem("rk"), s.sem("c_scale")
        c_pe, c_tmp, c_hi, c_done = s.sem("c_pe"), s.sem("c_tmp"), s.sem("c_hi"), s.sem("c_done")
        o_pe, o_done = s.sem("o_pe"), s.sem("o_done")

        raw = {"q": ek[:, :, 0:D], "k": ek[:, :, D:2 * D], "v": xt[:, 0:C, :], "o": xt[:, C:2 * C, :]}
        wo = [a[:, :, 0:D] for a in qT]
        wvT = [a[:, :, 0:D] for a in hT_v]
        xf = x.rearrange("b n d -> (b n) d")
        block = s.block()

        def qT_bank(t):
            return 4 + t % 2 if t < T - 2 else 6 + t % 2

        @block.sync
        def _(sp):
            for i, (n, w) in enumerate((("v", WvT), ("o", Wo), ("q", Wq), ("k", Wk))):
                sp.dma_start(raw[n], w.rearrange("(c p) n -> p c n", p=P)).then_inc(ld_w[i], 16)
            sp.dma_start(ident[:, :], ident_in).then_inc(ld_c, 16)
            sp.dma_start(bob[:, :], bo.partition_broadcast(P)).then_inc(ld_c, 16)
            sp.wait_ge(prep_lo, 2)
            for t in range(T):
                sp.dma_start(xt[:, t, :], xf[t * P:(t + 1) * P, :]).then_inc(ld_x[t], 16)

            def store(b, t):
                sp.wait_ge(o_done, b * T + (t + 1))
                sp.dma_start(x1[bass.ds(b * N + t * P, P), :], xt[:, t, :]).then_inc(st_x[t], 16)

            with sp.Fori(0, B - 1) as b:
                for t in range(T):
                    store(b, t)
                    if t >= 2:
                        sp.wait_ge(st_x[t - 2], b * 16 + 16)
                        sp.dma_start(xt[:, t - 2, :], xf[bass.ds(b * N + (N + (t - 2) * P), P), :]
                                     ).then_inc(ld_x[t - 2], 16)
                for t in (T - 2, T - 1):
                    sp.wait_ge(st_x[t], b * 16 + 16)
                    sp.dma_start(xt[:, t, :], xf[bass.ds(b * N + (N + t * P), P), :]).then_inc(ld_x[t], 16)
            for t in range(T):
                store(B - 1, t)
            for t in range(T):
                sp.wait_ge(st_x[t], 16 * B)

        @block.gpsimd
        def _(pool):
            pool.memset(power[:, :], -0.5).then_inc(setup, 1)
            pool.wait_ge(setup, 1)

            def root(b, t):
                n = t % H
                pool.wait_ge(var_ready, b * T + (t + 1))
                pool.tensor_tensor(rstd[:, n:n + 1], mv[:, n, 1:2], power[:, :], ALU.pow).then_inc(rstd_ready, 1)

            def low_rows(b, t):
                pool.wait_ge(hn_hi, b * T + (t + 1))
                pool.tensor_tensor(hn[1][:, t, :], h[:, t % H, :], hn[0][:, t, :], ALU.subtract).then_inc(hn_lo, 1)

            def batch(b, last):
                for t in range(T):
                    if t + 3 < T:
                        root(b, t + 3)
                    low_rows(b, t)
                for t in range(T):
                    pool.tensor_tensor(xt[:, t, :], xt[:, t, :], bob[:, :], ALU.add).then_inc(xb_done, 1)
                if not last:
                    for t in range(3):
                        root(b + 1, t)

            for t in range(3):
                root(0, t)
            with pool.Fori(0, B - 1) as b:
                batch(b, False)
            batch(B - 1, True)

        @block.vector
        def _(v):
            def split(i, dst, src, n):
                v.wait_ge(prep_hi, n)
                v.tensor_tensor(dst[1], src, dst[0], ALU.subtract).then_inc(prep_lo, 1)

            split(1, wvT, raw["v"], 1)
            split(2, wo, raw["o"], 2)
            split(3, [a[:, :, :] for a in W["q"]], raw["q"], 3)
            split(4, [a[:, :, :] for a in W["k"]], raw["k"], 4)

            def stats(b, t):
                n = t % H
                v.wait_ge(ld_x[t], b * 16 + 16)
                v.bn_stats(bn[:, n, :], xt[:, t, :]).then_inc(bn_ready, 1)
                wait_apart(v, bn_ready, b * T + (t + 1), spare)
                v.bn_aggr(mv[:, n, :], bn[:, n, :]).then_inc(var_eps, 1)
                v.wait_ge(var_eps, b * T + (t + 1))
                v.tensor_scalar(mv[:, n, 1:2], mv[:, n, 1:2], EPS, None, ALU.add).then_inc(var_ready, 1)

            def layernorm(b, t):
                n = t % H
                if t >= H:
                    v.wait_ge(hn_lo, b * T + (t - H + 1))
                v.wait_ge(rstd_ready, b * T + (t + 1))
                v.tensor_scalar(h[:, n, :], xt[:, t, :], mv[:, n, 0:1], rstd[:, n:n + 1],
                                ALU.subtract, ALU.mult).then_inc(h_ready, 1)

            def q_max_of(b, t):
                v.wait_ge(q_pe, b * T + (t + 1))
                v.tensor_reduce(nmq[:, t:t + 1], ps[:, 2 + t % 2, :], AX, ALU.max, negate=True).then_inc(q_max, 1)

            def qT_low(b, t):
                v.wait_ge(qT_hi, b * T + (t + 1))
                bank = ps[:, qT_bank(t), :].rearrange("p (c n) -> p c n", c=C)
                v.tensor_tensor(qT[1][:, :, t * P:(t + 1) * P], bank, qT[0][:, :, t * P:(t + 1) * P],
                                ALU.subtract).then_inc(qT_lo, 1)

            def batch(b, last):
                for i in range(T):
                    v.wait_ge(hT_hi, b * T + (i + 1))
                    bank = ps[:, i % 2, :].rearrange("p (c n) -> p c n", c=C)
                    v.tensor_tensor(hT_v[1][:, :, i * P:(i + 1) * P], bank, hT_v[0][:, :, i * P:(i + 1) * P],
                                    ALU.subtract).then_inc(hT_lo, 1)
                    if i >= 3:
                        qT_low(b, i - 3)
                    if i + 2 < T:
                        layernorm(b, i + 2)
                    if i + 3 < T:
                        stats(b, i + 3)
                    if i >= 1:
                        q_max_of(b, i - 1)
                qT_low(b, T - 3)
                for dc in range(C):
                    v.wait_ge(k_pe, b * C + (dc + 1))
                    pair = ps[:, 6:8, :] if dc % 2 == 0 else ps[:, 4:6, :]
                    v.tensor_reduce(nmk[:, dc:dc + 1], pair.rearrange("p a n -> p (a n)"), AX, ALU.max,
                                    negate=True).then_inc(k_max, 1)
                q_max_of(b, T - 1)
                for t in range(T):
                    v.wait_ge(kn_hi, b * T + (t + 1))
                    v.tensor_tensor(k_v[1][:, t, :], ps[:, t % 2, :], k_v[0][:, t, :], ALU.subtract
                                    ).then_inc(kn_lo, 1)
                    if t < 2:
                        qT_low(b, T - 2 + t)
                v.wait_ge(q_exp, b * T + T)
                v.reciprocal(rsq[:, :], smq[:, :]).then_inc(rq_ready, 1)
                v.wait_ge(k_exp, b * C + C)
                v.reciprocal(rsk[:, :], smk[:, :]).then_inc(rk_ready, 1)
                v.wait_ge(rk_ready, b + 1)
                v.tensor_scalar(rsk[:, :], rsk[:, :], SCALE, None, ALU.mult).then_inc(c_scale, 1)
                for f in range(C):
                    v.wait_ge(M_hi, b * C + (f + 1))
                    v.tensor_tensor(M[1][:, f, :], ps[:, 2 + f, :], M[0][:, f, :], ALU.subtract).then_inc(M_lo, 1)
                for dc in range(C):
                    v.wait_ge(c_tmp, b * C + (dc + 1))
                    v.tensor_copy(c_v[0][:, dc, :], eq[:, dc % 2, :]).then_inc(c_hi, 1)
                    v.wait_ge(c_hi, b * C + (dc + 1))
                    v.tensor_tensor(c_v[1][:, dc, :], eq[:, dc % 2, :], c_v[0][:, dc, :], ALU.subtract
                                    ).then_inc(c_done, 1)
                v.wait_ge(xb_done, b * T + T)
                v.wait_ge(rq_ready, b + 1)
                for t in range(T):
                    v.wait_ge(o_pe, b * T + (t + 1))
                    v.scalar_tensor_tensor(out=xt[:, t, :], in0=ps[:, 6 + t % 2, :], scalar=rsq[:, t:t + 1],
                                           in1=xt[:, t, :], op0=ALU.mult, op1=ALU.add).then_inc(o_done, 1)
                    if not last and t >= T - 3:
                        stats(b + 1, t - (T - 3))
                    if not last and t >= T - 2:
                        layernorm(b + 1, t - (T - 2))

            for t in range(3):
                stats(0, t)
            layernorm(0, 0)
            layernorm(0, 1)
            for f in range(C):
                split(5, [a[:, f, :] for a in W["vo"]], ps[:, 4 + f, :], 5 + f)
            with v.Fori(0, B - 1) as b:
                batch(b, False)
            batch(B - 1, True)

        @block.scalar
        def _(act):
            def high(dst, src):
                act.activation(dst, src, ACT.Copy).then_inc(prep_hi, 1)

            act.wait_ge(ld_w[0], 16)
            high(wvT[0], raw["v"])
            act.wait_ge(ld_w[1], 16)
            high(wo[0], raw["o"])
            act.wait_ge(ld_w[2], 16)
            high(W["q"][0][:, :, :], raw["q"])
            act.wait_ge(ld_w[3], 16)
            high(W["k"][0][:, :, :], raw["k"])
            for f in range(C):
                act.wait_ge(prep_pe, f + 1)
                high(W["vo"][0][:, f, :], ps[:, 4 + f, :])

            def q_exp_of(b, t):
                act.wait_ge(q_max, b * T + (t + 1))
                if t >= 2:
                    act.wait_ge(qT_pe, b * T + (t - 1))
                act.activation(eq[:, t % 2, :], ps[:, 2 + t % 2, :], ACT.Exp, bias=nmq[:, t:t + 1],
                               accum_out=smq[:, t:t + 1]).then_inc(q_exp, 1)

            def qT_high(b, t):
                act.wait_ge(qT_pe, b * T + (t + 1))
                bank = ps[:, qT_bank(t), :].rearrange("p (c n) -> p c n", c=C)
                act.activation(qT[0][:, :, t * P:(t + 1) * P], bank, ACT.Copy).then_inc(qT_hi, 1)

            with act.Fori(0, B) as b:
                for i in range(T):
                    act.wait_ge(hT_pe, b * T + (i + 1))
                    bank = ps[:, i % 2, :].rearrange("p (c n) -> p c n", c=C)
                    act.activation(hT_v[0][:, :, i * P:(i + 1) * P], bank, ACT.Copy).then_inc(hT_hi, 1)
                    if i >= 3:
                        qT_high(b, i - 3)
                    act.activation(hn[0][:, i, :], h[:, i % H, :], ACT.Copy).then_inc(hn_hi, 1)
                    if i >= 1:
                        q_exp_of(b, i - 1)
                qT_high(b, T - 3)
                for dc in range(C):
                    act.wait_ge(k_max, b * C + (dc + 1))
                    pair = ps[:, 6:8, :] if dc % 2 == 0 else ps[:, 4:6, :]
                    act.activation(ek[:, dc, :], pair.rearrange("p a n -> p (a n)"), ACT.Exp,
                                   bias=nmk[:, dc:dc + 1], accum_out=smk[:, dc:dc + 1]).then_inc(k_exp, 1)
                q_exp_of(b, T - 1)
                for t in range(T):
                    act.wait_ge(kn_pe, b * T + (t + 1))
                    act.activation(k_v[0][:, t, :], ps[:, t % 2, :], ACT.Copy).then_inc(kn_hi, 1)
                    if t < 2:
                        qT_high(b, T - 2 + t)
                for f in range(C):
                    act.wait_ge(M_pe, b * C + (f + 1))
                    act.activation(M[0][:, f, :], ps[:, 2 + f, :], ACT.Copy).then_inc(M_hi, 1)
                act.wait_ge(c_scale, b + 1)
                for dc in range(C):
                    act.wait_ge(c_pe, b * C + (dc + 1))
                    if dc >= 2:
                        act.wait_ge(c_done, b * C + (dc - 1))
                    act.activation(eq[:, dc % 2, :], ps[:, 6 + dc % 2, :], ACT.Copy,
                                   scale=rsk[:, dc:dc + 1]).then_inc(c_tmp, 1)

        @block.tensor
        def _(pe):
            pe.wait_ge(ld_c, 32)
            pe.wait_ge(prep_lo, 2)
            for f in range(C):
                for oc in range(C):
                    last = mm3(pe, ps[:, 4 + f, :], [a[:, oc, f * P:(f + 1) * P] for a in wvT],
                               [a[:, oc, :] for a in wo], oc == 0, oc == C - 1)
                last.then_inc(prep_pe, 1)
            pe.wait_ge(prep_lo, 4)

            def q_product(b, t):
                pe.wait_ge(hT_lo, b * T + (t + 1))
                if t >= 2:
                    pe.wait_ge(q_exp, b * T + (t - 1))
                for c in range(C):
                    last = mm3(pe, ps[:, 2 + t % 2, :], [a[:, c, t * P:(t + 1) * P] for a in hT_v],
                               [a[:, c, :] for a in W["q"]], c == 0, c == C - 1)
                last.then_inc(q_pe, 1)

            def q_transposes(b, t):
                pe.wait_ge(q_exp, b * T + (t + 1))
                if 2 <= t < T - 2:
                    pe.wait_ge(qT_lo, b * T + (t - 1))
                transposes(pe, ps[:, qT_bank(t), :], [eq[:, t % 2, c * P:(c + 1) * P] for c in range(C)],
                           ident[:, :]).then_inc(qT_pe, 1)

            with pe.Fori(0, B) as b:
                for i in range(T):
                    pe.wait_ge(h_ready, b * T + (i + 1))
                    if i >= 2:
                        pe.wait_ge(hT_lo, b * T + (i - 1))
                    transposes(pe, ps[:, i % 2, :], [h[:, i % H, c * P:(c + 1) * P] for c in range(C)],
                               ident[:, :]).then_inc(hT_pe, 1)
                    if i >= 3:
                        q_transposes(b, i - 3)
                    if i >= 1:
                        q_product(b, i - 1)
                q_transposes(b, T - 3)
                pe.wait_ge(hT_lo, b * T + T)
                for dc in range(C):
                    if dc == 1:
                        pe.wait_ge(qT_lo, b * T + (T - 2))
                    if dc >= 2:
                        pe.wait_ge(k_exp, b * C + (dc - 1))
                    first_bank = 6 if dc % 2 == 0 else 4
                    for c in range(C):
                        lhsT = [a[:, c, dc * P:(dc + 1) * P] for a in W["k"]]
                        for half in range(2):
                            last = mm3(pe, ps[:, first_bank + half, :], lhsT,
                                       [a[:, c, half * 512:(half + 1) * 512] for a in hT_v], c == 0, c == C - 1)
                    last.then_inc(k_pe, 1)
                q_product(b, T - 1)
                pe.wait_ge(k_exp, b * C + C)
                for i in range(T + 1):
                    if i < T:
                        if i >= 2:
                            pe.wait_ge(kn_lo, b * T + (i - 1))
                        transposes(pe, ps[:, i % 2, :], [ek[:, dc, i * P:(i + 1) * P] for dc in range(C)],
                                   ident[:, :]).then_inc(kn_pe, 1)
                    if i == 0:
                        q_transposes(b, T - 2)
                    if i >= 1:
                        t = i - 1
                        if t == 0:
                            pe.wait_ge(q_exp, b * T + T)
                            pe.wait_ge(hn_lo, b * T + T)
                        pe.wait_ge(kn_lo, b * T + (t + 1))
                        for f in range(C):
                            last = mm3(pe, ps[:, 2 + f, :], [a[:, t, f * P:(f + 1) * P] for a in hn],
                                       [a[:, t, :] for a in k_v], t == 0, t == T - 1)
                            if t == T - 1:
                                last.then_inc(M_pe, 1)
                    if i == 1:
                        q_transposes(b, T - 1)
                pe.wait_ge(qT_lo, b * T + T)
                for dc in range(C):
                    if dc >= 2:
                        pe.wait_ge(c_tmp, b * C + (dc - 1))
                    for f in range(C):
                        if dc == 0:
                            pe.wait_ge(M_lo, b * C + (f + 1))
                        last = mm3(pe, ps[:, 6 + dc % 2, :], [a[:, f, dc * P:(dc + 1) * P] for a in M],
                                   [a[:, f, :] for a in W["vo"]], f == 0, f == C - 1)
                    last.then_inc(c_pe, 1)
                for t in range(T):
                    if t == 0:
                        pe.wait_ge(c_tmp, b * C + (C - 1))
                    if t >= 2:
                        pe.wait_ge(o_done, b * T + (t - 1))
                    for dc in range(C):
                        if t == 0:
                            pe.wait_ge(c_done, b * C + (dc + 1))
                        last = mm3(pe, ps[:, 6 + t % 2, :], [a[:, dc, t * P:(t + 1) * P] for a in qT],
                                   [a[:, dc, :] for a in c_v], dc == 0, dc == C - 1)
                    last.then_inc(o_pe, 1)


def projections(nc, ps, x1, cx, wqT, wkT, wvT, ident_in, qk, vd):
    ROWS = x1.shape[0]
    GR = 512
    G, T = ROWS // GR, GR // P
    UNITS = 3 * C
    BANKS = 6
    assert T == C and UNITS % BANKS == 0
    with ExitStack() as ctx:
        s = Scope(nc, ctx, "b")
        W = [s.pair(f"w{n}", [P, C, D]) for n in "qkv"]
        raw = [s.sb(f"raw{n}", [P, C, D]) for n in "qkv"]
        xt, ct = s.sb("xt", [P, T, D]), s.sb("ct", [P, T, D])
        h = s.sb("h", [P, T, D])
        hT, cT = s.pair("hT", [P, C, GR]), s.pair("cT", [P, C, GR])
        res = [s.pair("q", [P, C, GR]), s.pair("k", [P, C, GR])]
        vals = s.sb("v", [P, T, D])
        ident = s.sb("ident", [P, P])
        bn, mv, rstd = s.sb("bn", [P, T, 6]), s.sb("mv", [P, T, 2]), s.sb("rstd", [P, T])
        power, spare = s.sb("power", [P, 1]), s.sb("spare", [P, 1])

        ld_w, ld_c, ld_x, ld_t = s.sems("ld_w", 3), s.sem("ld_c"), s.sems("ld_x", T), s.sems("ld_t", T)
        st_r, st_v = [s.sems("st_q", C), s.sems("st_k", C)], s.sems("st_v", T)
        prep_hi, prep_lo, setup = s.sem("prep_hi"), s.sem("prep_lo"), s.sem("setup")
        bn_ready, var_eps, var_ready, rstd_ready, h_ready = (s.sem(n) for n in ("bn", "ve", "var", "rstd", "h"))
        hT_pe, hT_hi, hT_lo = s.sem("hT_pe"), s.sem("hT_hi"), s.sem("hT_lo")
        cT_pe, cT_hi, cT_lo = s.sem("cT_pe"), s.sem("cT_hi"), s.sem("cT_lo")
        q_pe, k_pe, v_pe, r_hi = s.sem("q_pe"), s.sem("k_pe"), s.sem("v_pe"), s.sem("r_hi")
        r_out = s.sem("r_out")
        block = s.block()

        def row0(g, t):
            return g * GR + t * P

        @block.sync
        def _(sp):
            sp.dma_start(ident[:, :], ident_in).then_inc(ld_c, 16)
            for t in range(T):
                sp.dma_start(xt[:, t, :], x1[t * P:(t + 1) * P, :]).then_inc(ld_x[t], 16)
            for i, w in enumerate((wqT, wkT, wvT)):
                sp.dma_start(raw[i][:, :, :], w.rearrange("(c p) n -> p c n", p=P)).then_inc(ld_w[i], 16)
                if i == 0:
                    for t in range(T):
                        sp.dma_start(ct[:, t, :], cx[t * P:(t + 1) * P, :]).then_inc(ld_t[t], 16)

            def load_x(g, t):
                sp.wait_ge(h_ready, g * T + (t + 1))
                sp.dma_start(xt[:, t, :], x1[bass.ds(row0(g, t) + GR, P), :]).then_inc(ld_x[t], 16)

            def group(g, more):
                for i in range(2):
                    for c in range(C):
                        sp.wait_ge(r_out, g * UNITS + (BANKS + i * C + c + 1))
                        for hl in (1, 0):
                            sp.dma_start(qk[i, hl, c * P:(c + 1) * P, bass.ds(g * GR, GR)], res[i][hl][:, c, :].bitcast(F32)
                                         ).then_inc(st_r[i][c], 16)
                        if more >= 1 and i == 0:
                            sp.wait_ge(cT_pe, g * T + (c + 1))
                            sp.dma_start(ct[:, c, :], cx[bass.ds(row0(g, c) + GR, P), :]).then_inc(ld_t[c], 16)
                        if more >= 2 and i == 1:
                            load_x(g + 1, c)
                for t in range(T):
                    sp.wait_ge(r_out, g * UNITS + (BANKS + 2 * C + t + 1))
                    sp.dma_start(vd[bass.ds(row0(g, t), P), :], vals[:, t, :]).then_inc(st_v[t], 16)

            for t in range(T):
                load_x(0, t)
            with sp.Fori(0, G - 2) as g:
                group(g, 2)
            group(G - 2, 1)
            group(G - 1, 0)
            for c in range(C):
                sp.wait_ge(st_r[0][c], 32 * G)
                sp.wait_ge(st_r[1][c], 32 * G)
                sp.wait_ge(st_v[c], 16 * G)

        @block.gpsimd
        def _(pool):
            pool.wait_ge(r_out, BANKS)
            with pool.Fori(0, G) as g:
                for t in range(T):
                    pool.wait_ge(var_ready, g * T + (t + 1))
                    pool.tensor_tensor(rstd[:, t:t + 1], mv[:, t, 1:2], power[:, :], ALU.pow).then_inc(rstd_ready, 1)

        @block.vector
        def _(v):
            v.memset(power[:, :], -0.5).then_inc(r_out, BANKS)

            def split(i):
                v.wait_ge(prep_hi, i + 1)
                v.tensor_tensor(W[i][1][:, :, :], raw[i][:, :, :], W[i][0][:, :, :], ALU.subtract).then_inc(prep_lo, 1)

            def stats(g, t):
                v.wait_ge(ld_x[t], g * 16 + 16)
                v.bn_stats(bn[:, t, :], xt[:, t, :]).then_inc(bn_ready, 1)
                wait_apart(v, bn_ready, g * T + (t + 1), spare)
                v.bn_aggr(mv[:, t, :], bn[:, t, :]).then_inc(var_eps, 1)
                v.wait_ge(var_eps, g * T + (t + 1))
                v.tensor_scalar(mv[:, t, 1:2], mv[:, t, 1:2], EPS, None, ALU.add).then_inc(var_ready, 1)

            def layernorm(g, t):
                v.wait_ge(rstd_ready, g * T + (t + 1))
                v.tensor_scalar(h[:, t, :], xt[:, t, :], mv[:, t, 0:1], rstd[:, t:t + 1],
                                ALU.subtract, ALU.mult).then_inc(h_ready, 1)

            def low(bank, dst, t, ready, at, done):
                v.wait_ge(ready, at)
                rows = slice(t * P, (t + 1) * P)
                v.tensor_tensor(dst[1][:, :, rows], ps[:, bank, :].rearrange("p (c n) -> p c n", c=C),
                                dst[0][:, :, rows], ALU.subtract).then_inc(done, 1)

            def result(g, i, c):
                v.wait_ge(r_hi, g * (2 * C) + (i * C + c + 1))
                v.tensor_tensor(res[i][1][:, c, :], ps[:, 2 + (i * C + c) % BANKS, :], res[i][0][:, c, :],
                                ALU.subtract).then_inc(r_out, 1)

            def group(g, last):
                for c in range(C):
                    low(c % 2, cT, c, cT_hi, g * T + (c + 1), cT_lo)
                    if not last:
                        stats(g + 1, c)
                        if c > 0:
                            layernorm(g + 1, c - 1)
                    result(g, 0, c)
                    if isinstance(g, int) and g == 0 and c < 2:
                        split(c + 1)
                for c in range(C):
                    if not last and c == 0:
                        layernorm(g + 1, T - 1)
                    if not last:
                        low(c % 2, hT, c, hT_hi, (g + 1) * T + (c + 1), hT_lo)
                    result(g, 1, c)
                for t in range(T):
                    v.wait_ge(v_pe, g * T + (t + 1))
                    v.wait_ge(st_v[t], g * 16)
                    v.tensor_copy(vals[:, t, :], ps[:, 2 + (2 * C + t) % BANKS, :]).then_inc(r_out, 1)

            for t in range(T):
                stats(0, t)
                if t > 0:
                    layernorm(0, t - 1)
            layernorm(0, T - 1)
            split(0)
            for t in range(T):
                low(t % 2, hT, t, hT_hi, t + 1, hT_lo)
            group(0, False)
            with v.Fori(1, G - 1) as g:
                group(g, False)
            group(G - 1, True)

        @block.scalar
        def _(act):
            def high_weight(i):
                act.wait_ge(ld_w[i], 16)
                act.activation(W[i][0][:, :, :], raw[i][:, :, :], ACT.Copy).then_inc(prep_hi, 1)

            def high(bank, dst, t, ready, at, done):
                act.wait_ge(ready, at)
                act.activation(dst[0][:, :, t * P:(t + 1) * P], ps[:, bank, :].rearrange("p (c n) -> p c n", c=C),
                               ACT.Copy).then_inc(done, 1)

            def result(g, i, c):
                act.wait_ge((q_pe, k_pe)[i], g * C + (c + 1))
                act.wait_ge(st_r[i][c], g * 32)
                act.activation(res[i][0][:, c, :], ps[:, 2 + (i * C + c) % BANKS, :], ACT.Copy).then_inc(r_hi, 1)

            def group(g, last):
                for c in range(C):
                    high(c % 2, cT, c, cT_pe, g * T + (c + 1), cT_hi)
                    result(g, 0, c)
                for c in range(C):
                    if not last:
                        high(c % 2, hT, c, hT_pe, (g + 1) * T + (c + 1), hT_hi)
                    result(g, 1, c)

            high_weight(0)
            for t in range(T):
                high(t % 2, hT, t, hT_pe, t + 1, hT_hi)
            high_weight(1)
            high_weight(2)
            group(0, False)
            with act.Fori(1, G - 1) as g:
                group(g, False)
            group(G - 1, True)

        @block.tensor
        def _(pe):
            pe.wait_ge(ld_c, 16)
            def turn_h(g, t, free):
                pe.wait_ge(h_ready, g * T + (t + 1))
                if free:
                    pe.wait_ge(free[0], free[1])
                transposes(pe, ps[:, t % 2, :], [h[:, t, c * P:(c + 1) * P] for c in range(C)], ident[:, :]
                           ).then_inc(hT_pe, 1)

            def group(g, last):
                for c in range(C):
                    pe.wait_ge(ld_t[c], g * 16 + 16)
                    if c < 2:
                        pe.wait_ge(hT_lo, g * T + (T - 1 + c))
                    else:
                        pe.wait_ge(cT_lo, g * T + (c - 1))
                    transposes(pe, ps[:, c % 2, :], [ct[:, c, f * P:(f + 1) * P] for f in range(C)], ident[:, :]
                               ).then_inc(cT_pe, 1)
                    if c == 0:
                        pe.wait_ge(hT_lo, g * T + T)
                        weight(g, 0)
                    product(g, c, W[0], hT, c, False).then_inc(q_pe, 1)
                for c in range(C):
                    if not last:
                        turn_h(g + 1, c, (cT_lo, g * T + (T - 1 + c)) if c < 2 else (hT_lo, g * T + (T + c - 1)))
                    if c == 0:
                        pe.wait_ge(cT_lo, g * T + T)
                        weight(g, 1)
                    product(g, C + c, W[1], cT, c, False).then_inc(k_pe, 1)
                weight(g, 2)
                for t in range(T):
                    product(g, 2 * C + t, cT, W[2], t, True).then_inc(v_pe, 1)

            def weight(g, i):
                if isinstance(g, int) and g == 0:
                    pe.wait_ge(prep_lo, i + 1)

            def product(g, u, lhs, rhs, m, rows):
                pe.wait_ge(r_out, g * UNITS + (u + 1))
                for c in range(C):
                    last = mm3(pe, ps[:, 2 + u % BANKS, :], [a[:, c, m * P:(m + 1) * P] for a in lhs],
                               [a[:, c, :] for a in rhs], c == 0, c == C - 1)
                return last

            for t in range(T):
                turn_h(0, t, (hT_lo, t - 1) if t >= 2 else None)
            group(0, False)
            with pe.Fori(1, G - 1) as g:
                group(g, False)
            group(G - 1, True)


def attention(nc, ps, x1, qk, vd, wo, ident_in, masks_in, nmd, x2):
    ROWS = x1.shape[0]
    PAIRS = ROWS // P
    R = P // 2
    U = R // 8
    NU = 2 * U
    K = 3 * HD
    BUF = 3
    LOOPS = (PAIRS - 2) // BUF
    FIRST = 6
    LAG = 2
    PT = 4
    SCALE = float(np.float32(1.0) / np.sqrt(np.float32(HD)))
    assert LOOPS * BUF == PAIRS - 2 and NU % PT == 0
    with ExitStack() as ctx:
        s = Scope(nc, ctx, "c")

        def banks(n, w):
            flat = ps[:, n:n + (2 if w > R // 2 else 1), :].rearrange("p a n -> p (a n)")
            return flat.rearrange("p (c r) -> p c r", c=HEADS)[:, :, 0:w]

        def scores(k):
            return banks(3 * (k % 2), 8 * (k % U + 1))

        def shifted(k):
            w = R - 8 * (k % U)
            return banks(3 * (k % 2) + (1 if w > R // 2 else 2), w)

        av = ps[:, 6, 0:256].rearrange("p (c r) -> p c r", c=C)
        den = ps[:, 6, 256:512].rearrange("p (c r) -> p c r", c=C)
        misc = ps[:, 7, :]
        qs = [s.sb(f"qs{i}", [P, HEADS, P], F32R) for i in range(BUF)]
        ks = [s.sb(f"ks{i}", [P, HEADS, P], F32R) for i in range(BUF)]
        qg, kg = s.sb("qg", [P, NU, P], F32R), s.sb("kg", [P, NU, P], F32R)
        vt = [s.sb(f"vt{i}", [P, NU, HD]) for i in range(BUF)]
        xt = [s.sb(f"xt{i}", [P, D]) for i in range(BUF)]
        W, raw = s.pair("w", [P, C, D]), s.sb("raw", [P, C, D])
        ident, identr = s.sb("ident", [P, P]), s.sb("identr", [P, P], F32R)
        maskf = [s.sb(f"maskf{i}", [P, HEADS, 8]) for i in range(2)]
        mask = [s.sb(f"mask{i}", [P, HEADS, 8], BF16) for i in range(2)]
        identb = s.sb("identb", [P, P], BF16)
        ones = s.sb("ones", [P, HD])
        pt = [s.sb(f"pt{i}", [P, HEADS * R]) for i in range(PT)]
        mx = s.sb("mx", [P, NU])
        nm = [s.sb(f"nm{i}", [P, P], F32R) for i in range(2)]
        nmt = [s.sb(f"nmt{i}", [2 * U, P], F32R) for i in range(2)]
        sums, rec, o = s.sb("sums", [P, 2 * C * R]), s.sb("rec", [P, C * R]), s.sb("o", [P, C, R])
        oT = s.pair("oT", [P, C, P])

        ld_c, ld_w, setup = s.sem("ld_c"), s.sem("ld_w"), s.sem("setup")
        ld_qk, ld_v, ld_x, st_x = s.sems("ld_qk", BUF), s.sems("ld_v", BUF), s.sems("ld_x", BUF), s.sems("st_x", BUF)
        prep_pe, prep_hi, prep_lo = s.sem("prep_pe"), s.sem("prep_hi"), s.sem("prep_lo")
        g_pe, g_max = s.sem("g_pe"), s.sem("g_max")
        nm_hi, nm_lo, nm_pe, nm_t, nm_st = (s.sem(n) for n in ("nm_hi", "nm_lo", "nm_pe", "nm_t", "nm_st"))
        nm_ld = s.sems("nm_ld", 2)
        qg_done, kg_done = s.sem("qg_done"), s.sem("kg_done")
        t_pe, t_exp, a_pe = s.sem("t_pe"), s.sem("t_exp"), s.sem("a_pe")
        o_out, r_done, o_done, o_hi, o_lo = s.sem("o_out"), s.sem("r_done"), s.sem("o_done"), s.sem("o_hi"), s.sem("o_lo")
        y_pe, y_done = s.sem("y_pe"), s.sem("y_done")
        block = s.block()
        vf = vd.rearrange("r (c e) -> (r c) e", e=HD)

        def probs(k):
            w = R - 8 * (k % U)
            rows = R if w > R // 2 else R // 2
            return pt[k % PT][:, 0:HEADS * rows].rearrange("p (c r) -> p c r", c=HEADS)[:, :, 0:w]

        def parts(w):
            return [slice(0, 8), slice(8, 16)] if w > R // 2 else [slice(0, 16)]

        @block.sync
        def _(sp):
            sp.dma_start(ident[:, :], ident_in).then_inc(ld_c, 16)
            for i in range(2):
                sp.dma_start(maskf[i][:, :, :], masks_in[i]).then_inc(ld_c, 16)
            sp.dma_start(raw[:, :, :], wo.rearrange("(c p) n -> p c n", p=P)).then_inc(ld_w, 16)

            def load_qk(p, a):
                for g in range(3):
                    for i, t in enumerate((qs[a], ks[a])):
                        hl = (0, 0, 1)[g] if i == 0 else (0, 1, 0)[g]
                        sp.dma_start(t[HD * g:HD * (g + 1), :, :].bitcast(F32),
                                     qk[i, hl].rearrange("(c d) r -> d c r", d=HD)[:, :, bass.ds(p * P, P)]
                                     ).then_inc(ld_qk[a], 16)

            def load_vx(p, a):
                sp.dma_start(vt[a][:, :, :], vf[bass.ds(p * (P * HEADS), P * HEADS), :].rearrange(
                    "(t p) e -> p t e", p=P)).then_inc(ld_v[a], 16)
                sp.dma_start(xt[a][:, :], x1[bass.ds(p * P, P), :]).then_inc(ld_x[a], 16)

            def maxima(p, a, hd):
                waits = [(nm_t, 2 * p + (hd + 1))]
                if not isinstance(p, int) or p > 0:
                    waits.append((nm_ld[hd], 16 * p))
                for sem, value in waits if hd else waits[::-1]:
                    sp.wait_ge(sem, value)
                for hl in range(2):
                    sp.dma_start(nmd[hd, hl].rearrange("c u r -> u c r"), nmt[hd][U * hl:U * (hl + 1), :].bitcast(F32)
                                 .rearrange("u (c r) -> u c r", c=HEADS)).then_inc(nm_st, 16)
                sp.wait_ge(nm_st, 64 * p + 32 * (hd + 1))
                sp.dma_start(qs[a][K:K + 2, :, R * hd:R * (hd + 1)].bitcast(F32),
                             nmd[hd].rearrange("l c u r -> l c (u r)")).then_inc(nm_ld[hd], 16)

            def store(i, a):
                p = i * BUF + a
                sp.wait_ge(y_done, p + 1)
                sp.dma_start(x2[bass.ds(p * P, P), :], xt[a][:, :]).then_inc(st_x[a], 16)

            def turn(i, a):
                p = i * BUF + a
                b = (a + 2) % BUF
                sp.wait_ge(t_pe, p * NU)
                load_qk(p + 2, b)
                maxima(p, a, 1)
                if not isinstance(p, int) or p > 0:
                    store(i - (a == 0), b)
                    sp.wait_ge(st_x[b], i * 16 + (16 if b < a else 0))
                load_vx(p + 2, b)
                maxima(p + 1, (a + 1) % BUF, 0)

            for p in range(2):
                load_qk(p, p)
                load_vx(p, p)
            maxima(0, 0, 0)
            for a in range(BUF):
                turn(0, a)
            with sp.Fori(1, LOOPS) as i:
                for a in range(BUF):
                    turn(i, a)
            maxima(PAIRS - 2, 0, 1)
            store(LOOPS - 1, BUF - 1)
            maxima(PAIRS - 1, 1, 0)
            maxima(PAIRS - 1, 1, 1)
            store(LOOPS, 0)
            store(LOOPS, 1)
            for a in range(BUF):
                sp.wait_ge(st_x[a], 16 * len(range(a, PAIRS, BUF)))

        @block.vector
        def _(v):
            v.memset(kg[K:K + 2, :, :].bitcast(F32), 1.0).then_inc(setup, 1)
            v.memset(ones[:, :], 1.0).then_inc(setup, 1)
            v.wait_ge(ld_c, 48)
            v.tensor_copy(identr[:, :], ident[:, :]).then_inc(setup, 1)
            v.tensor_copy(identb[:, :], ident[:, :]).then_inc(setup, 1)
            for i in range(2):
                v.tensor_copy(mask[i][:, :, :], maskf[i][:, :, :]).then_inc(setup, 1)
            for hd in range(2):
                v.tensor_scalar(nm[hd][:, :], ident[:, :], 0.0, None, ALU.mult).then_inc(setup, 1)
            for c in range(C):
                v.wait_ge(prep_hi, c + 1)
                v.tensor_tensor(W[1][:, c, :], ps[:, 2 + c, :], W[0][:, c, :], ALU.subtract).then_inc(prep_lo, 1)

            def first_pass(p, k):
                v.wait_ge(g_pe, p * NU + (k + 1))
                v.tensor_reduce(mx[:, k:k + 1], scores(k), mybir.AxisListType.XY, ALU.max,
                                negate=True).then_inc(g_max, 1)

            def negate(p, hd):
                v.wait_ge(g_max, p * NU + U * (hd + 1))
                if not isinstance(p, int) or p > 0:
                    v.wait_ge(nm_pe, 2 * p + (hd - 1))
                m = mx[:, U * hd:U * (hd + 1)]
                v.tensor_copy(nm[hd][:, 0:U], m).then_inc(nm_hi, 1)
                v.wait_ge(nm_hi, 2 * p + (hd + 1))
                v.tensor_tensor(nm[hd][:, U:2 * U], m, nm[hd][:, 0:U], ALU.subtract).then_inc(nm_lo, 1)

            def normalize(p, hd):
                v.wait_ge(a_pe, p * NU + U * (hd + 1))
                v.tensor_copy(sums[:, :], ps[:, 6, :]).then_inc(o_out, 1)
                v.wait_ge(o_out, 2 * p + (hd + 1))
                v.reciprocal(rec[:, :], sums[:, C * R:]).then_inc(r_done, 1)
                v.wait_ge(r_done, 2 * p + (hd + 1))
                v.tensor_tensor(o[:, :, :].rearrange("p c r -> p (c r)"), sums[:, 0:C * R], rec[:, :], ALU.mult
                                ).then_inc(o_done, 1)

            def low(p, hd):
                v.wait_ge(o_hi, 2 * p + (hd + 1))
                rows = slice(R * hd, R * (hd + 1))
                v.tensor_tensor(oT[1][:, :, rows], o[:, :, :], oT[0][:, :, rows], ALU.subtract).then_inc(o_lo, 1)

            def output(i, a):
                p = i * BUF + a
                v.wait_ge(y_pe, p + 1)
                v.wait_ge(ld_x[a], i * 16 + 16)
                v.tensor_tensor(xt[a][:, :], misc, xt[a][:, :], ALU.add).then_inc(y_done, 1)

            def turn(i, a, more):
                p = i * BUF + a
                for slot in range(FIRST, FIRST + NU):
                    if slot // NU + 1 <= more:
                        first_pass(p + (slot // NU + 1), slot % NU)
                    if more >= 1 and slot in (U, NU):
                        negate(p + 1, slot // U - 1)
                    if slot in (U + 1, NU + 1):
                        normalize(p, slot // U - 1)
                    if slot in (U + 3, NU + 3):
                        low(p, slot // U - 1)
                output(i, a)

            for k in range(NU):
                first_pass(0, k)
                if k == U:
                    negate(0, 0)
            negate(0, 1)
            for k in range(FIRST):
                first_pass(1, k)
            with v.Fori(0, LOOPS) as i:
                for a in range(BUF):
                    turn(i, a, 2)
            turn(LOOPS, 0, 1)
            turn(LOOPS, 1, 0)

        @block.scalar
        def _(act):
            for c in range(C):
                act.wait_ge(prep_pe, c + 1)
                act.activation(W[0][:, c, :], ps[:, 2 + c, :], ACT.Copy).then_inc(prep_hi, 1)

            def unit(p, k):
                n = p * NU + k
                act.wait_ge(t_pe, n + 1)
                if not isinstance(n, int) or n >= PT:
                    act.wait_ge(a_pe, n - (PT - 1))
                act.activation(probs(k), shifted(k), ACT.Exp, scale=SCALE).then_inc(t_exp, 1)

            def maxima(p, hd):
                act.wait_ge(nm_pe, 2 * p + (hd + 1))
                if not isinstance(p, int) or p > 0:
                    act.wait_ge(nm_st, 64 * p + 32 * (hd - 1))
                act.activation(nmt[hd][:, :], misc[0:2 * U, 0:P], ACT.Copy).then_inc(nm_t, 1)

            def gather(i, a, hd, done, before, dst, src, order, parts):
                q = i * BUF + a
                act.wait_ge(ld_qk[a % BUF], (i + a // BUF) * 96 + 96)
                if not isinstance(q, int) or q > 0:
                    act.wait_ge(before, q * NU - NU + U * (hd + 1))
                out = dst[0:K, U * hd:U * (hd + 1), :]
                rows = src[a % BUF][0:K, :, R * hd:R * (hd + 1)].rearrange("p c (u r) -> p u c r", u=U)
                for u in range(0, U, U // parts):
                    o4 = out[:, u:u + U // parts, :].rearrange(order, c=HEADS)
                    i4 = rows[:, u:u + U // parts]
                    last = act.activation(o4, i4.bitcast(F32), ACT.Copy)
                last.then_inc(done, 1)

            def gather_q(i, a, hd):
                gather(i, a, hd, qg_done, g_pe, qg, qs, "p u (c r) -> p u c r", 1)

            def gather_k(i, a, hd):
                gather(i, a, hd, kg_done, t_pe, kg, ks, "p u (r c) -> p u c r", 1)

            def high(p, hd):
                act.wait_ge(o_done, 2 * p + (hd + 1))
                act.activation(oT[0][:, :, R * hd:R * (hd + 1)], o[:, :, :], ACT.Copy).then_inc(o_hi, 1)

            def turn(i, a, more):
                p = i * BUF + a
                for slot in range(FIRST, FIRST + NU):
                    if slot // NU <= more:
                        unit(p + slot // NU, slot % NU)
                    if slot in (U + 2, NU + 2):
                        if more >= 1:
                            maxima(p + 1, slot // U - 1)
                        high(p, slot // U - 1)
                    if slot in (U + 4, NU + 3) and more >= 2:
                        gather_q(i, a + 2, slot // U - 1)
                    if slot in (U + 5, NU + 4) and more >= 1:
                        gather_k(i, a + 1, slot // U - 1)

            for hd in range(2):
                gather_q(0, 0, hd)
            for hd in range(2):
                gather_k(0, 0, hd)
            gather_q(0, 1, 0)
            maxima(0, 0)
            gather_q(0, 1, 1)
            maxima(0, 1)
            for k in range(FIRST):
                unit(0, k)
            with act.Fori(0, LOOPS) as i:
                for a in range(BUF):
                    turn(i, a, 2)
            turn(LOOPS, 0, 1)
            turn(LOOPS, 1, 0)

        @block.tensor
        def _(pe):
            pe.wait_ge(ld_c, 48)
            pe.wait_ge(ld_w, 16)
            for c in range(C):
                transposes(pe, ps[:, 2 + c, :], [raw[:, e, c * P:(c + 1) * P] for e in range(C)], ident[:, :]
                           ).then_inc(prep_pe, 1)
            pe.wait_ge(prep_lo, C)
            pe.wait_ge(setup, 8)

            def first_pass(i, a, k):
                q = i * BUF + a
                n = q * NU + k
                a = a % BUF
                if k % U == 0:
                    pe.wait_ge(qg_done, 2 * q + (k // U + 1))
                slot_free(n, n - NU)
                hd, w, out = k // U, 8 * (k % U + 1), scores(k)
                for cs in parts(w):
                    pe.matmul(out[:, cs, :], qg[0:K, k, :], ks[a][0:K, cs, R * hd:R * hd + w],
                              start=True, stop=False)
                for cs in parts(w):
                    last = pe.matmul(out[:, cs, w - 8:w], identb[:, :], mask[0][:, cs, :], start=False, stop=True)
                last.then_inc(g_pe, 1)

            def slot_free(g, t):
                if not isinstance(g, int) or g >= 2:
                    pe.wait_ge(g_max, g - 1)
                if not isinstance(t, int) or t >= 2:
                    pe.wait_ge(t_exp, t - 1)

            def second_pass(i, a, k, alone=False):
                p = i * BUF + a
                n = p * NU + k
                a = a % BUF
                hd, at = k // U, 8 * (k % U)
                if k % U == 0:
                    pe.wait_ge(nm_ld[hd], p * 16 + 16)
                    pe.wait_ge(kg_done, 2 * p + (hd + 1))
                if alone:
                    slot_free(min(n + NU, PAIRS * NU + 1), n)
                w, out = R - at, shifted(k)
                for cs in parts(w):
                    pe.matmul(out[:, cs, 0:8], identb[:, :], mask[1][:, cs, :], start=True, stop=False,
                              skip_group_check=True)
                for cs in parts(w):
                    last = pe.matmul(out[:, cs, :], kg[0:K + 2, k, :], qs[a][0:K + 2, cs, R * hd + at:R * (hd + 1)],
                                     start=False, stop=True, skip_group_check=True)
                last.then_inc(t_pe, 1)

            def values(i, a, k):
                p = i * BUF + a
                a, j = a % BUF, i + a // BUF
                hd, at = k // U, 8 * (k % U)
                pe.wait_ge(t_exp, p * NU + (k + 1))
                if k == 0:
                    pe.wait_ge(ld_v[a], j * 16 + 16)
                if k % U == 0:
                    pe.wait_ge(o_out, 2 * p + hd)
                rhs = probs(k).rearrange("p (c q) r -> p c q r", q=4)
                for lhsT, out in ((vt[a][:, k, :], av), (ones[:, :], den)):
                    for q in range(4):
                        last = pe.matmul(out[HD * q:HD * (q + 1), :, at:R], lhsT, rhs[:, :, q, :],
                                         start=(at == 0 and out is av), stop=(k % U == U - 1), skip_group_check=True)
                last.then_inc(a_pe, 1)

            def maxima(p, hd):
                pe.wait_ge(nm_lo, 2 * p + (hd + 1))
                if hd == 1:
                    pe.wait_ge(nm_t, 2 * p + 1)
                pe.matmul(misc[:, 0:P], nm[hd][:, :], identr[:, :], start=True, stop=True).then_inc(nm_pe, 1)

            def output(p, more):
                pe.wait_ge(o_lo, 2 * p + 2)
                if more:
                    pe.wait_ge(nm_t, 2 * p + 4)
                else:
                    pe.wait_ge(y_done, p)
                for c in range(C):
                    last = mm3(pe, misc, [t[:, c, :] for t in oT], [t[:, c, :] for t in W], c == 0, c == C - 1)
                last.then_inc(y_pe, 1)

            def turn(i, a, more):
                p = i * BUF + a
                for slot in range(FIRST, FIRST + NU):
                    if slot // NU + 1 <= more:
                        first_pass(i, a + slot // NU + 1, slot % NU)
                    if slot // NU <= more:
                        second_pass(i, a + slot // NU, slot % NU, slot // NU + 1 > more)
                    if (slot - LAG) // NU <= more:
                        values(i, a + (slot - LAG) // NU, (slot - LAG) % NU)
                    if more >= 1 and slot in (U + 2, NU + 2):
                        maxima(p + 1, slot // U - 1)
                    if slot == NU + 4:
                        output(p, more >= 1)

            for k in range(NU):
                first_pass(0, 0, k)
                if k == U + 2:
                    maxima(0, 0)
            maxima(0, 1)
            for k in range(FIRST):
                first_pass(0, 1, k)
                second_pass(0, 0, k)
                if k >= LAG:
                    values(0, 0, k - LAG)
            with pe.Fori(0, LOOPS) as i:
                for a in range(BUF):
                    turn(i, a, 2)
            turn(LOOPS, 0, 1)
            turn(LOOPS, 1, 0)


def feed_forward(nc, ps, x2, w, bias, aT, b, ident_in, out):
    ROWS = x2.shape[0]
    TILES = ROWS // P
    RANK = aT.shape[0]
    BUF = 4
    LOOPS = (TILES - 2) // BUF
    ROUND = 1.5 * 2.0 ** 23
    with ExitStack() as ctx:
        s = Scope(nc, ctx, "d")
        raw, W = s.sb("raw", [P, C, D]), s.pair("w", [P, C, D])
        whole = s.sb("whole", [P, C, D])
        aTs, bs = s.sb("aT", [RANK, D]), s.sb("b", [RANK, D])
        ident, bb, power = s.sb("ident", [P, P]), s.sb("bias", [P, D]), s.sb("power", [P, 1])
        spare = s.sb("spare", [P, 1])
        top, topall, step, inv = (s.sb(n, [P, 1]) for n in ("top", "topall", "step", "inv"))
        xt = [s.sb(f"xt{i}", [P, D]) for i in range(BUF)]
        yt = [s.sb(f"yt{i}", [P, D]) for i in range(BUF)]
        h = s.sb("h", [P, 2, D])
        hT = [s.pair(f"hT{i}", [P, C, P]) for i in range(2)]
        bn, mv, rstd = s.sb("bn", [P, 2, 6]), s.sb("mv", [P, 2, 2]), s.sb("rstd", [P, 2])

        ld_w, ld_c, ld_x, st_y = s.sem("ld_w"), s.sem("ld_c"), s.sems("ld_x", BUF), s.sems("st_y", BUF)
        setup, q_step, top_ready, lora, w_hi, w_lo = (s.sem(n) for n in (
            "setup", "q_step", "top_ready", "lora", "w_hi", "w_lo"))
        bn_ready, var_eps, var_ready, rstd_ready, h_ready = (s.sem(n) for n in ("bn", "ve", "var", "rstd", "h"))
        hT_pe, hT_hi, hT_lo, xb_done, y_pe, y_done = (s.sem(n) for n in (
            "hT_pe", "hT_hi", "hT_lo", "xb", "y_pe", "y_done"))
        block = s.block()

        @block.sync
        def _(sp):
            sp.dma_start(raw[:, :, :], w.rearrange("(c p) n -> p c n", p=P)).then_inc(ld_w, 16)
            sp.dma_start(aTs[:, :], aT).then_inc(ld_c, 16)
            sp.dma_start(bs[:, :], b).then_inc(ld_c, 16)
            sp.dma_start(ident[:, :], ident_in).then_inc(ld_c, 16)
            sp.dma_start(bb[:, :], bias.partition_broadcast(P)).then_inc(ld_c, 16)
            for a in range(BUF):
                sp.dma_start(xt[a][:, :], x2[a * P:(a + 1) * P, :]).then_inc(ld_x[a], 16)

            def turn(i, a, more):
                t = i * BUF + a
                sp.wait_ge(y_done, t + 1)
                sp.dma_start(out[bass.ds(t * P, P), :], yt[a][:, :]).then_inc(st_y[a], 16)
                if more:
                    sp.dma_start(xt[a][:, :], x2[bass.ds((t + BUF) * P, P), :]).then_inc(ld_x[a], 16)

            with sp.Fori(0, LOOPS) as i:
                for a in range(BUF):
                    turn(i, a, True)
            for t in range(LOOPS * BUF, TILES):
                turn(t // BUF, t % BUF, t + BUF < TILES)
            for a in range(BUF):
                sp.wait_ge(st_y[a], 16 * (TILES // BUF))

        @block.gpsimd
        def _(pool):
            pool.memset(power[:, :], -0.5).then_inc(setup, 1)
            pool.wait_ge(top_ready, 1)
            pool.wait_ge(setup, 1)
            pool.partition_all_reduce(topall[:, :], top[:, :], P, RED.max).then_inc(setup, 1)
            pool.wait_ge(setup, 2)
            pool.wait_ge(ld_c, 64)

            with pool.Fori(0, TILES // BUF) as i:
                for a in range(BUF):
                    t = i * BUF + a
                    pool.wait_ge(var_ready, t + 1)
                    pool.tensor_tensor(rstd[:, a % 2:a % 2 + 1], mv[:, a % 2, 1:2], power[:, :], ALU.pow
                                       ).then_inc(rstd_ready, 1)
                    pool.wait_ge(h_ready, t + 1)
                    pool.tensor_tensor(xt[a][:, :], xt[a][:, :], bb[:, :], ALU.add).then_inc(xb_done, 1)

        @block.vector
        def _(v):
            n = [0]

            def link(ins):
                n[0] += 1
                ins.then_inc(q_step, 1)
                v.wait_ge(q_step, n[0])

            v.wait_ge(ld_w, 16)
            flat = raw[:, :, :].rearrange("p c n -> p (c n)")
            v.tensor_reduce(top[:, :], flat, AX, ALU.max, apply_absolute_value=True).then_inc(top_ready, 1)
            v.wait_ge(setup, 2)
            link(v.tensor_scalar(step[:, :], topall[:, :], float(np.float32(1.0) / np.float32(7.0)), None, ALU.mult))
            link(v.reciprocal(inv[:, :], step[:, :]))
            link(v.tensor_scalar(flat, flat, inv[:, :], ROUND, ALU.mult, ALU.add))
            link(v.tensor_scalar(flat, flat, ROUND, 7.0, ALU.subtract, ALU.min))
            link(v.tensor_scalar(flat, flat, -8.0, None, ALU.max))
            for c in range(C):
                v.wait_ge(lora, c + 1)
                link(v.scalar_tensor_tensor(out=whole[:, c, :], in0=raw[:, c, :], scalar=step[:, 0:1],
                                            in1=ps[:, 2 + c, :], op0=ALU.mult, op1=ALU.add))
                v.tensor_copy(W[0][:, c, :], whole[:, c, :]).then_inc(w_hi, 1)
                v.wait_ge(w_hi, c + 1)
                v.tensor_tensor(W[1][:, c, :], whole[:, c, :], W[0][:, c, :], ALU.subtract).then_inc(w_lo, 1)

            def layernorm(i, a):
                t = i * BUF + a
                b, j = a % BUF, i + a // BUF
                x = xt[b]
                v.wait_ge(ld_x[b], j * 16 + 16)
                v.bn_stats(bn[:, a % 2, :], x[:, :]).then_inc(bn_ready, 1)
                wait_apart(v, bn_ready, t + 1, spare)
                v.bn_aggr(mv[:, a % 2, :], bn[:, a % 2, :]).then_inc(var_eps, 1)
                v.wait_ge(var_eps, t + 1)
                v.tensor_scalar(mv[:, a % 2, 1:2], mv[:, a % 2, 1:2], EPS, None, ALU.add).then_inc(var_ready, 1)
                v.wait_ge(rstd_ready, t + 1)
                v.tensor_scalar(h[:, a % 2, :], x[:, :], mv[:, a % 2, 0:1], rstd[:, a % 2:a % 2 + 1],
                                ALU.subtract, ALU.mult).then_inc(h_ready, 1)

            def low(i, a):
                v.wait_ge(hT_hi, i * BUF + (a + 1))
                v.tensor_tensor(hT[a % 2][1][:, :, :], ps[:, a % 2, :].rearrange("p (c n) -> p c n", c=C),
                                hT[a % 2][0][:, :, :], ALU.subtract).then_inc(hT_lo, 1)

            def output(i, a):
                t = i * BUF + a
                v.wait_ge(y_pe, t + 1)
                v.wait_ge(xb_done, t + 1)
                v.wait_ge(st_y[a], i * 16)
                v.tensor_tensor(yt[a][:, :], ps[:, 2 + a, :], xt[a][:, :], ALU.add).then_inc(y_done, 1)

            def turn(i, a, more):
                if more >= 2:
                    layernorm(i, a + 2)
                if more >= 1:
                    low(i, a + 1)
                output(i, a)

            layernorm(0, 0)
            layernorm(0, 1)
            low(0, 0)
            for a in range(BUF):
                turn(0, a, 2)
            with v.Fori(1, LOOPS) as i:
                for a in range(BUF):
                    turn(i, a, 2)
            for t in range(LOOPS * BUF, TILES):
                turn(t // BUF, t % BUF, TILES - 1 - t)

        @block.scalar
        def _(act):
            with act.Fori(0, TILES // BUF) as i:
                for a in range(BUF):
                    act.wait_ge(hT_pe, i * BUF + (a + 1))
                    act.activation(hT[a % 2][0][:, :, :], ps[:, a % 2, :].rearrange("p (c n) -> p c n", c=C),
                                   ACT.Copy).then_inc(hT_hi, 1)

        @block.tensor
        def _(pe):
            pe.wait_ge(ld_c, 64)
            for c in range(C):
                pe.matmul(ps[:, 2 + c, :], aTs[:, c * P:(c + 1) * P], bs[:, :], start=True, stop=True
                          ).then_inc(lora, 1)

            def turn_h(i, a):
                t = i * BUF + a
                pe.wait_ge(h_ready, t + 1)
                if not isinstance(t, int) or t >= 2:
                    pe.wait_ge(hT_lo, t - 1)
                transposes(pe, ps[:, a % 2, :], [h[:, a % 2, c * P:(c + 1) * P] for c in range(C)], ident[:, :]
                           ).then_inc(hT_pe, 1)

            def product(i, a):
                t = i * BUF + a
                pe.wait_ge(hT_lo, t + 1)
                if not isinstance(t, int) or t >= BUF:
                    pe.wait_ge(y_done, t - (BUF - 1))
                for c in range(C):
                    last = mm3(pe, ps[:, 2 + a, :], [u[:, c, :] for u in hT[a % 2]], [u[:, c, :] for u in W],
                               c == 0, c == C - 1)
                last.then_inc(y_pe, 1)

            turn_h(0, 0)
            pe.wait_ge(w_lo, C)
            for a in range(BUF):
                turn_h(0, a + 1)
                product(0, a)
            with pe.Fori(1, LOOPS) as i:
                for a in range(BUF):
                    turn_h(i, a + 1)
                    product(i, a)
            for t in range(LOOPS * BUF, TILES):
                if t + 1 < TILES:
                    turn_h(t // BUF, t % BUF + 1)
                product(t // BUF, t % BUF)


def decoder(nc, x, cx, Wq, Wk, Wv, Wo, bo, wq, wk, wv, wo, w, bias, aT, b, ident, masks_in, out):
    rows = x.shape[0] * x.shape[1]
    x1 = nc.dram_tensor("x1", (rows, D), F32, kind="Internal").ap()
    x2 = nc.dram_tensor("x2", (rows, D), F32, kind="Internal").ap()
    qk = nc.dram_tensor("qk", (2, 2, D, rows), F32, kind="Internal").ap()
    vd = nc.dram_tensor("vd", (rows, D), F32, kind="Internal").ap()
    nmd = nc.dram_tensor("nmd", (2, 2, HEADS, P // 16, 8), F32, kind="Internal").ap()
    with nc.psum_tensor("psum", [P, 8, 512], F32) as ps:
        linear_attention(nc, ps, x, Wq, Wk, Wv, Wo, bo, ident, x1)
        projections(nc, ps, x1, cx.rearrange("b n d -> (b n) d"), wq, wk, wv, ident, qk, vd)
        attention(nc, ps, x1, qk, vd, wo, ident, masks_in, nmd, x2)
        feed_forward(nc, ps, x2, w, bias, aT, b, ident, out.rearrange("b n d -> (b n) d"))


def masks():
    c, r = np.divmod(np.arange(P), 8)
    own = np.arange(HEADS)[:, None] + HEADS * np.arange(8)[None, :]
    keys_after = np.where(own[None] <= (HEADS * r + c)[:, None, None], 0.0, MASKED)
    queries_before = np.where(np.arange(P)[:, None, None] <= own[None], 0.0, MASKED)
    return np.stack([keys_after, queries_before]).astype(np.float32)


_INS = ['x', 'ctx_1024', 'L0_attn_Wq', 'L0_attn_Wk', 'L0_attn_Wv', 'L0_attn_Wo', 'L0_attn_bo', 'L0_xattn_wq',
        'L0_xattn_wk', 'L0_xattn_wv', 'L0_xattn_wo', 'L0_ffn_kernel', 'L0_ffn_bias', 'L0_ffn_a', 'L0_ffn_b']


_TRANSPOSED = ('L0_attn_Wv', 'L0_xattn_wq', 'L0_xattn_wk', 'L0_xattn_wv', 'L0_ffn_a')


def kernel(**inputs):
    import concourse.bacc as _bacc
    from concourse.bass_utils import run_bass_kernel_spmd as _run

    nc = _bacc.Bacc("TRN2", target_bir_lowering=False, num_devices=1)
    arrays, args = {}, []

    def add(name, a):
        arrays[f"in_{name}_dram"] = a
        args.append(nc.dram_tensor(f"in_{name}_dram", a.shape, mybir.dt.from_np(a.dtype), kind="ExternalInput").ap())

    for name in _INS:
        a = np.asarray(inputs[name])
        add(name, np.ascontiguousarray(a.T if name in _TRANSPOSED else a))
    add("ident", np.eye(P, dtype=np.float32))
    add("masks", masks())
    args.append(nc.dram_tensor("out_0_dram", (4, 1024, D), F32, kind="ExternalOutput").ap())
    decoder(nc, *args)
    r = _run(nc, [arrays], core_ids=[0])
    return r.results[0]["out_0_dram"]
```

```python
from contextlib import ExitStack

import numpy as np

import concourse.bass as bass
from concourse import mybir

F32 = mybir.dt.float32
F32R = mybir.dt.float32r
BF16 = mybir.dt.bfloat16
ALU = mybir.AluOpType
ACT = mybir.ActivationFunctionType
RED = bass.bass_isa.ReduceOp
AX = mybir.AxisListType.X

P = 128
D = 512
C = D // P
HEADS = 16
HD = D // HEADS
EPS = 1e-5
MASKED = -1.0e30


def mm3(pe, out, lhsT, rhs, first, last):
    (lh, ll), (rh, rl) = lhsT, rhs
    pe.matmul(out, lh, rh, start=first, stop=False)
    pe.matmul(out, lh, rl, start=False, stop=False)
    return pe.matmul(out, ll, rh, start=False, stop=last)


def transposes(pe, bank, src, ident):
    for i, s in enumerate(src):
        last = pe.transpose(bank[:, i * P:(i + 1) * P], s, ident)
    return last


def wait_apart(v, sem, value, spare):
    v.wait_ge(sem, value)
    v.memset(spare[:, :], 0.0)


class Scope:

    def __init__(self, nc, ctx, tag):
        self.nc, self.ctx, self.tag, self.held = nc, ctx, tag, []

    def block(self):
        self.ctx.callback(self.release)
        return self.ctx.enter_context(self.nc.Block())

    def release(self):
        self.nc.clear_and_free_semaphores(self.held)
        self.nc.all_engine_barrier()

    def sb(self, name, shape, dt=F32):
        return self.ctx.enter_context(self.nc.sbuf_tensor(f"{self.tag}_{name}", shape, dt))

    def pair(self, name, shape):
        return self.sb(name + "_hi", shape, F32R), self.sb(name + "_lo", shape, F32R)

    def sem(self, name):
        self.held.append(self.nc.alloc_semaphore(f"{self.tag}_{name}"))
        return self.held[-1]

    def sems(self, name, n):
        return [self.sem(f"{name}{i}") for i in range(n)]


def linear_attention(nc, ps, x, Wq, Wk, WvT, Wo, bo, ident_in, x1):
    B, N, _ = x.shape
    T = N // P
    H = 4
    SCALE = float(1.0 / np.sqrt(np.float32(HD))) / D
    with ExitStack() as ctx:
        s = Scope(nc, ctx, "a")
        W = {n: s.pair(f"w{n}", [P, C, D]) for n in ("q", "k", "vo")}
        xt = s.sb("xt", [P, T, D])
        h = s.sb("h", [P, H, D])
        hn = s.pair("hn", [P, T, D])
        hT = s.pair("hT", [P, C * N])
        hT_v = [a[:, :].rearrange("p (c n) -> p c n", c=C) for a in hT]
        k_v = [a[:, :].rearrange("p (t d) -> p t d", t=T) for a in hT]
        c_v = [a[:, 0:C * D].rearrange("p (c e) -> p c e", c=C) for a in hT]
        qT = s.pair("qT", [P, C, N])
        ek = s.sb("ek", [P, C, N])
        M = s.pair("M", [P, C, D])
        eq = s.sb("eq", [P, 2, D])
        ident, bob = s.sb("ident", [P, P]), s.sb("bob", [P, D])
        bn, mv, rstd = s.sb("bn", [P, H, 6]), s.sb("mv", [P, H, 2]), s.sb("rstd", [P, H])
        power, spare = s.sb("power", [P, 1]), s.sb("spare", [P, 1])
        nmq, smq, rsq = (s.sb(n, [P, T]) for n in ("nmq", "smq", "rsq"))
        nmk, smk, rsk = (s.sb(n, [P, C]) for n in ("nmk", "smk", "rsk"))

        ld_vo = s.sems("ld_vo", C)
        ld_w, ld_c, ld_x, st_x = s.sems("ld_w", 2), s.sem("ld_c"), s.sems("ld_x", T), s.sems("st_x", T)
        prep_hi, prep_lo, prep_pe, setup = s.sem("prep_hi"), s.sem("prep_lo"), s.sem("prep_pe"), s.sem("setup")
        bn_ready, var_eps, var_ready, rstd_ready, h_ready = (s.sem(n) for n in ("bn", "ve", "var", "rstd", "h"))
        hn_hi, hn_lo, xb_done = s.sem("hn_hi"), s.sem("hn_lo"), s.sem("xb")
        hT_pe, hT_hi, hT_lo = s.sem("hT_pe"), s.sem("hT_hi"), s.sem("hT_lo")
        q_pe, q_max, q_exp = s.sem("q_pe"), s.sem("q_max"), s.sem("q_exp")
        qT_pe, qT_hi, qT_lo = s.sem("qT_pe"), s.sem("qT_hi"), s.sem("qT_lo")
        k_pe, k_max, k_exp = s.sem("k_pe"), s.sem("k_max"), s.sem("k_exp")
        kn_pe, kn_hi, kn_lo = s.sem("kn_pe"), s.sem("kn_hi"), s.sem("kn_lo")
        M_pe, M_hi, M_lo = s.sem("M_pe"), s.sem("M_hi"), s.sem("M_lo")
        rq_ready, rk_ready, c_scale = s.sem("rq"), s.sem("rk"), s.sem("c_scale")
        c_pe, c_tmp, c_hi, c_done = s.sem("c_pe"), s.sem("c_tmp"), s.sem("c_hi"), s.sem("c_done")
        o_pe, o_done = s.sem("o_pe"), s.sem("o_done")

        raw = {"q": ek[:, :, 0:D], "k": ek[:, :, D:2 * D], "v": xt[:, 0:C, :], "o": xt[:, C:2 * C, :]}
        wo = [a[:, :, 0:D] for a in qT]
        wvT = [a[:, :, 0:D] for a in hT_v]
        xf = x.rearrange("b n d -> (b n) d")
        block = s.block()

        def qT_bank(t):
            return 4 + t % 2 if t < T - 2 else 6 + t % 2

        @block.sync
        def _(sp):
            for c in range(C):
                for n, w in (("v", WvT), ("o", Wo)):
                    sp.dma_start(raw[n][:, c, :], w[c * P:(c + 1) * P, :]).then_inc(ld_vo[c], 16)
            for i, (n, w) in enumerate((("q", Wq), ("k", Wk))):
                sp.dma_start(raw[n], w.rearrange("(c p) n -> p c n", p=P)).then_inc(ld_w[i], 16)
            sp.dma_start(ident[:, :], ident_in).then_inc(ld_c, 16)
            sp.dma_start(bob[:, :], bo.partition_broadcast(P)).then_inc(ld_c, 16)
            sp.wait_ge(prep_lo, 2 * C)
            for t in range(T):
                sp.dma_start(xt[:, t, :], xf[t * P:(t + 1) * P, :]).then_inc(ld_x[t], 16)

            def store(b, t):
                sp.wait_ge(o_done, b * T + (t + 1))
                sp.dma_start(x1[bass.ds(b * N + t * P, P), :], xt[:, t, :]).then_inc(st_x[t], 16)

            with sp.Fori(0, B - 1) as b:
                for t in range(T):
                    store(b, t)
                    if t >= 2:
                        sp.wait_ge(st_x[t - 2], b * 16 + 16)
                        sp.dma_start(xt[:, t - 2, :], xf[bass.ds(b * N + (N + (t - 2) * P), P), :]
                                     ).then_inc(ld_x[t - 2], 16)
                for t in (T - 2, T - 1):
                    sp.wait_ge(st_x[t], b * 16 + 16)
                    sp.dma_start(xt[:, t, :], xf[bass.ds(b * N + (N + t * P), P), :]).then_inc(ld_x[t], 16)
            for t in range(T):
                store(B - 1, t)
            for t in range(T):
                sp.wait_ge(st_x[t], 16 * B)

        @block.gpsimd
        def _(pool):
            pool.memset(power[:, :], -0.5).then_inc(setup, 1)
            pool.wait_ge(setup, 1)

            def root(b, t):
                n = t % H
                pool.wait_ge(var_ready, b * T + (t + 1))
                pool.tensor_tensor(rstd[:, n:n + 1], mv[:, n, 1:2], power[:, :], ALU.pow).then_inc(rstd_ready, 1)

            def low_rows(b, t):
                pool.wait_ge(hn_hi, b * T + (t + 1))
                pool.tensor_tensor(hn[1][:, t, :], h[:, t % H, :], hn[0][:, t, :], ALU.subtract).then_inc(hn_lo, 1)

            def batch(b, last):
                for t in range(T):
                    if t + 3 < T:
                        root(b, t + 3)
                    low_rows(b, t)
                for t in range(T):
                    pool.tensor_tensor(xt[:, t, :], xt[:, t, :], bob[:, :], ALU.add).then_inc(xb_done, 1)
                if not last:
                    for t in range(3):
                        root(b + 1, t)

            for t in range(3):
                root(0, t)
            with pool.Fori(0, B - 1) as b:
                batch(b, False)
            batch(B - 1, True)

        @block.vector
        def _(v):
            def split(dst, src, n):
                v.wait_ge(prep_hi, n)
                v.tensor_tensor(dst[1], src, dst[0], ALU.subtract).then_inc(prep_lo, 1)

            for c in range(C):
                split([a[:, c, :] for a in wvT], raw["v"][:, c, :], 2 * c + 1)
                split([a[:, c, :] for a in wo], raw["o"][:, c, :], 2 * c + 2)
            split([a[:, :, :] for a in W["q"]], raw["q"], 2 * C + 1)
            split([a[:, :, :] for a in W["k"]], raw["k"], 2 * C + 2)

            def stats(b, t):
                n = t % H
                v.wait_ge(ld_x[t], b * 16 + 16)
                v.bn_stats(bn[:, n, :], xt[:, t, :]).then_inc(bn_ready, 1)
                wait_apart(v, bn_ready, b * T + (t + 1), spare)
                v.bn_aggr(mv[:, n, :], bn[:, n, :]).then_inc(var_eps, 1)
                v.wait_ge(var_eps, b * T + (t + 1))
                v.tensor_scalar(mv[:, n, 1:2], mv[:, n, 1:2], EPS, None, ALU.add).then_inc(var_ready, 1)

            def layernorm(b, t):
                n = t % H
                if t >= H:
                    v.wait_ge(hn_lo, b * T + (t - H + 1))
                v.wait_ge(rstd_ready, b * T + (t + 1))
                v.tensor_scalar(h[:, n, :], xt[:, t, :], mv[:, n, 0:1], rstd[:, n:n + 1],
                                ALU.subtract, ALU.mult).then_inc(h_ready, 1)

            def q_max_of(b, t):
                v.wait_ge(q_pe, b * T + (t + 1))
                v.tensor_reduce(nmq[:, t:t + 1], ps[:, 2 + t % 2, :], AX, ALU.max, negate=True).then_inc(q_max, 1)

            def qT_low(b, t):
                v.wait_ge(qT_hi, b * T + (t + 1))
                bank = ps[:, qT_bank(t), :].rearrange("p (c n) -> p c n", c=C)
                v.tensor_tensor(qT[1][:, :, t * P:(t + 1) * P], bank, qT[0][:, :, t * P:(t + 1) * P],
                                ALU.subtract).then_inc(qT_lo, 1)

            def batch(b, last):
                for i in range(T):
                    v.wait_ge(hT_hi, b * T + (i + 1))
                    bank = ps[:, i % 2, :].rearrange("p (c n) -> p c n", c=C)
                    v.tensor_tensor(hT_v[1][:, :, i * P:(i + 1) * P], bank, hT_v[0][:, :, i * P:(i + 1) * P],
                                    ALU.subtract).then_inc(hT_lo, 1)
                    if i >= 3:
                        qT_low(b, i - 3)
                    if i + 2 < T:
                        layernorm(b, i + 2)
                    if i + 3 < T:
                        stats(b, i + 3)
                    if i >= 1:
                        q_max_of(b, i - 1)
                qT_low(b, T - 3)
                for dc in range(C):
                    v.wait_ge(k_pe, b * C + (dc + 1))
                    pair = ps[:, 6:8, :] if dc % 2 == 0 else ps[:, 4:6, :]
                    v.tensor_reduce(nmk[:, dc:dc + 1], pair.rearrange("p a n -> p (a n)"), AX, ALU.max,
                                    negate=True).then_inc(k_max, 1)
                q_max_of(b, T - 1)
                for t in range(T):
                    v.wait_ge(kn_hi, b * T + (t + 1))
                    v.tensor_tensor(k_v[1][:, t, :], ps[:, t % 2, :], k_v[0][:, t, :], ALU.subtract
                                    ).then_inc(kn_lo, 1)
                    if t < 2:
                        qT_low(b, T - 2 + t)
                v.wait_ge(q_exp, b * T + T)
                v.reciprocal(rsq[:, :], smq[:, :]).then_inc(rq_ready, 1)
                v.wait_ge(k_exp, b * C + C)
                v.reciprocal(rsk[:, :], smk[:, :]).then_inc(rk_ready, 1)
                v.wait_ge(rk_ready, b + 1)
                v.tensor_scalar(rsk[:, :], rsk[:, :], SCALE, None, ALU.mult).then_inc(c_scale, 1)
                for f in range(C):
                    v.wait_ge(M_hi, b * C + (f + 1))
                    v.tensor_tensor(M[1][:, f, :], ps[:, 2 + f, :], M[0][:, f, :], ALU.subtract).then_inc(M_lo, 1)
                for dc in range(C):
                    v.wait_ge(c_tmp, b * C + (dc + 1))
                    v.tensor_copy(c_v[0][:, dc, :], eq[:, dc % 2, :]).then_inc(c_hi, 1)
                    v.wait_ge(c_hi, b * C + (dc + 1))
                    v.tensor_tensor(c_v[1][:, dc, :], eq[:, dc % 2, :], c_v[0][:, dc, :], ALU.subtract
                                    ).then_inc(c_done, 1)
                v.wait_ge(xb_done, b * T + T)
                v.wait_ge(rq_ready, b + 1)
                for t in range(T):
                    v.wait_ge(o_pe, b * T + (t + 1))
                    v.scalar_tensor_tensor(out=xt[:, t, :], in0=ps[:, 6 + t % 2, :], scalar=rsq[:, t:t + 1],
                                           in1=xt[:, t, :], op0=ALU.mult, op1=ALU.add).then_inc(o_done, 1)
                    if not last and t >= T - 3:
                        stats(b + 1, t - (T - 3))
                    if not last and t >= T - 2:
                        layernorm(b + 1, t - (T - 2))

            for t in range(3):
                stats(0, t)
            layernorm(0, 0)
            layernorm(0, 1)
            for f in range(C):
                split([a[:, f, :] for a in W["vo"]], ps[:, 4 + f, :], 2 * C + 3 + f)
            with v.Fori(0, B - 1) as b:
                batch(b, False)
            batch(B - 1, True)

        @block.scalar
        def _(act):
            def high(dst, src):
                act.activation(dst, src, ACT.Copy).then_inc(prep_hi, 1)

            for c in range(C):
                act.wait_ge(ld_vo[c], 32)
                high(wvT[0][:, c, :], raw["v"][:, c, :])
                high(wo[0][:, c, :], raw["o"][:, c, :])
            act.wait_ge(ld_w[0], 16)
            high(W["q"][0][:, :, :], raw["q"])
            act.wait_ge(ld_w[1], 16)
            high(W["k"][0][:, :, :], raw["k"])
            for f in range(C):
                act.wait_ge(prep_pe, f + 1)
                high(W["vo"][0][:, f, :], ps[:, 4 + f, :])

            def q_exp_of(b, t):
                act.wait_ge(q_max, b * T + (t + 1))
                if t >= 2:
                    act.wait_ge(qT_pe, b * T + (t - 1))
                act.activation(eq[:, t % 2, :], ps[:, 2 + t % 2, :], ACT.Exp, bias=nmq[:, t:t + 1],
                               accum_out=smq[:, t:t + 1]).then_inc(q_exp, 1)

            def qT_high(b, t):
                act.wait_ge(qT_pe, b * T + (t + 1))
                bank = ps[:, qT_bank(t), :].rearrange("p (c n) -> p c n", c=C)
                act.activation(qT[0][:, :, t * P:(t + 1) * P], bank, ACT.Copy).then_inc(qT_hi, 1)

            with act.Fori(0, B) as b:
                for i in range(T):
                    act.wait_ge(hT_pe, b * T + (i + 1))
                    bank = ps[:, i % 2, :].rearrange("p (c n) -> p c n", c=C)
                    act.activation(hT_v[0][:, :, i * P:(i + 1) * P], bank, ACT.Copy).then_inc(hT_hi, 1)
                    if i >= 3:
                        qT_high(b, i - 3)
                    act.activation(hn[0][:, i, :], h[:, i % H, :], ACT.Copy).then_inc(hn_hi, 1)
                    if i >= 1:
                        q_exp_of(b, i - 1)
                qT_high(b, T - 3)
                for dc in range(C):
                    act.wait_ge(k_max, b * C + (dc + 1))
                    pair = ps[:, 6:8, :] if dc % 2 == 0 else ps[:, 4:6, :]
                    act.activation(ek[:, dc, :], pair.rearrange("p a n -> p (a n)"), ACT.Exp,
                                   bias=nmk[:, dc:dc + 1], accum_out=smk[:, dc:dc + 1]).then_inc(k_exp, 1)
                q_exp_of(b, T - 1)
                for t in range(T):
                    act.wait_ge(kn_pe, b * T + (t + 1))
                    act.activation(k_v[0][:, t, :], ps[:, t % 2, :], ACT.Copy).then_inc(kn_hi, 1)
                    if t < 2:
                        qT_high(b, T - 2 + t)
                for f in range(C):
                    act.wait_ge(M_pe, b * C + (f + 1))
                    act.activation(M[0][:, f, :], ps[:, 2 + f, :], ACT.Copy).then_inc(M_hi, 1)
                act.wait_ge(c_scale, b + 1)
                for dc in range(C):
                    act.wait_ge(c_pe, b * C + (dc + 1))
                    if dc >= 2:
                        act.wait_ge(c_done, b * C + (dc - 1))
                    act.activation(eq[:, dc % 2, :], ps[:, 6 + dc % 2, :], ACT.Copy,
                                   scale=rsk[:, dc:dc + 1]).then_inc(c_tmp, 1)

        @block.tensor
        def _(pe):
            for oc in range(C):
                pe.wait_ge(prep_lo, 2 * oc + 2)
                for f in range(C):
                    last = mm3(pe, ps[:, 4 + f, :], [a[:, oc, f * P:(f + 1) * P] for a in wvT],
                               [a[:, oc, :] for a in wo], oc == 0, oc == C - 1)
                    if oc == C - 1:
                        last.then_inc(prep_pe, 1)
            pe.wait_ge(ld_c, 32)
            pe.wait_ge(prep_lo, 2 * C + 2)

            def q_product(b, t):
                pe.wait_ge(hT_lo, b * T + (t + 1))
                if t >= 2:
                    pe.wait_ge(q_exp, b * T + (t - 1))
                for c in range(C):
                    last = mm3(pe, ps[:, 2 + t % 2, :], [a[:, c, t * P:(t + 1) * P] for a in hT_v],
                               [a[:, c, :] for a in W["q"]], c == 0, c == C - 1)
                last.then_inc(q_pe, 1)

            def q_transposes(b, t):
                pe.wait_ge(q_exp, b * T + (t + 1))
                if 2 <= t < T - 2:
                    pe.wait_ge(qT_lo, b * T + (t - 1))
                transposes(pe, ps[:, qT_bank(t), :], [eq[:, t % 2, c * P:(c + 1) * P] for c in range(C)],
                           ident[:, :]).then_inc(qT_pe, 1)

            with pe.Fori(0, B) as b:
                for i in range(T):
                    pe.wait_ge(h_ready, b * T + (i + 1))
                    if i >= 2:
                        pe.wait_ge(hT_lo, b * T + (i - 1))
                    transposes(pe, ps[:, i % 2, :], [h[:, i % H, c * P:(c + 1) * P] for c in range(C)],
                               ident[:, :]).then_inc(hT_pe, 1)
                    if i >= 3:
                        q_transposes(b, i - 3)
                    if i >= 1:
                        q_product(b, i - 1)
                q_transposes(b, T - 3)
                pe.wait_ge(hT_lo, b * T + T)
                for dc in range(C):
                    if dc == 1:
                        pe.wait_ge(qT_lo, b * T + (T - 2))
                    if dc >= 2:
                        pe.wait_ge(k_exp, b * C + (dc - 1))
                    first_bank = 6 if dc % 2 == 0 else 4
                    for c in range(C):
                        lhsT = [a[:, c, dc * P:(dc + 1) * P] for a in W["k"]]
                        for half in range(2):
                            last = mm3(pe, ps[:, first_bank + half, :], lhsT,
                                       [a[:, c, half * 512:(half + 1) * 512] for a in hT_v], c == 0, c == C - 1)
                    last.then_inc(k_pe, 1)
                q_product(b, T - 1)
                pe.wait_ge(k_exp, b * C + C)
                for i in range(T + 1):
                    if i < T:
                        if i >= 2:
                            pe.wait_ge(kn_lo, b * T + (i - 1))
                        transposes(pe, ps[:, i % 2, :], [ek[:, dc, i * P:(i + 1) * P] for dc in range(C)],
                                   ident[:, :]).then_inc(kn_pe, 1)
                    if i == 0:
                        q_transposes(b, T - 2)
                    if i >= 1:
                        t = i - 1
                        if t == 0:
                            pe.wait_ge(q_exp, b * T + T)
                            pe.wait_ge(hn_lo, b * T + T)
                        pe.wait_ge(kn_lo, b * T + (t + 1))
                        for f in range(C):
                            last = mm3(pe, ps[:, 2 + f, :], [a[:, t, f * P:(f + 1) * P] for a in hn],
                                       [a[:, t, :] for a in k_v], t == 0, t == T - 1)
                            if t == T - 1:
                                last.then_inc(M_pe, 1)
                    if i == 1:
                        q_transposes(b, T - 1)
                pe.wait_ge(qT_lo, b * T + T)
                for dc in range(C):
                    if dc >= 2:
                        pe.wait_ge(c_tmp, b * C + (dc - 1))
                    for f in range(C):
                        if dc == 0:
                            pe.wait_ge(M_lo, b * C + (f + 1))
                        last = mm3(pe, ps[:, 6 + dc % 2, :], [a[:, f, dc * P:(dc + 1) * P] for a in M],
                                   [a[:, f, :] for a in W["vo"]], f == 0, f == C - 1)
                    last.then_inc(c_pe, 1)
                for t in range(T):
                    if t == 0:
                        pe.wait_ge(c_tmp, b * C + (C - 1))
                    if t >= 2:
                        pe.wait_ge(o_done, b * T + (t - 1))
                    for dc in range(C):
                        if t == 0:
                            pe.wait_ge(c_done, b * C + (dc + 1))
                        last = mm3(pe, ps[:, 6 + t % 2, :], [a[:, dc, t * P:(t + 1) * P] for a in qT],
                                   [a[:, dc, :] for a in c_v], dc == 0, dc == C - 1)
                    last.then_inc(o_pe, 1)


def projections(nc, ps, x1, cx, wqT, wkT, wvT, ident_in, qk, vd, w, aT, b, ffn):
    ROWS = x1.shape[0]
    GR = 512
    G, T = ROWS // GR, GR // P
    UNITS = 3 * C
    BANKS = 6
    RANK = aT.shape[0]
    ROUND = 1.5 * 2.0 ** 23
    assert T == C and UNITS % BANKS == 0
    with ExitStack() as ctx:
        s = Scope(nc, ctx, "b")
        W = [s.pair(f"w{n}", [P, C, D]) for n in "qkv"]
        raw = [s.sb(f"raw{n}", [P, C, D]) for n in "qkv"]
        xt, ct = s.sb("xt", [P, T, D]), s.sb("ct", [P, T, D])
        h = s.sb("h", [P, T, D])
        hT, cT = s.pair("hT", [P, C, GR]), s.pair("cT", [P, C, GR])
        res = [s.pair("q", [P, C, GR]), s.pair("k", [P, C, GR])]
        vals = s.sb("v", [P, T, D])
        ident = s.sb("ident", [P, P])
        bn, mv, rstd = s.sb("bn", [P, T, 6]), s.sb("mv", [P, T, 2]), s.sb("rstd", [P, T])
        aTs, bs = s.sb("aT", [RANK, D]), s.sb("b", [RANK, D])
        top, topall, step, inv = (s.sb(n, [P, 1]) for n in ("top", "topall", "step", "inv"))
        ints, whole = raw[0], raw[1]
        power, spare = s.sb("power", [P, 1]), s.sb("spare", [P, 1])

        ld_f, q_step, top_ready, all_ready = s.sem("ld_f"), s.sem("q_step"), s.sem("top"), s.sem("all")
        lora, ffn_whole = s.sem("lora"), s.sem("ffn_whole")
        ld_w, ld_c, ld_x, ld_t = s.sems("ld_w", 3), s.sem("ld_c"), s.sems("ld_x", T), s.sems("ld_t", T)
        st_r, st_v = [s.sems("st_q", C), s.sems("st_k", C)], s.sems("st_v", T)
        prep_hi, prep_lo, setup = s.sem("prep_hi"), s.sem("prep_lo"), s.sem("setup")
        bn_ready, var_eps, var_ready, rstd_ready, h_ready = (s.sem(n) for n in ("bn", "ve", "var", "rstd", "h"))
        hT_pe, hT_hi, hT_lo = s.sem("hT_pe"), s.sem("hT_hi"), s.sem("hT_lo")
        cT_pe, cT_hi, cT_lo = s.sem("cT_pe"), s.sem("cT_hi"), s.sem("cT_lo")
        q_pe, k_pe, v_pe, r_hi = s.sem("q_pe"), s.sem("k_pe"), s.sem("v_pe"), s.sem("r_hi")
        r_out = s.sem("r_out")
        block = s.block()

        def row0(g, t):
            return g * GR + t * P

        @block.sync
        def _(sp):
            sp.dma_start(ident[:, :], ident_in).then_inc(ld_c, 16)
            for t in range(T):
                sp.dma_start(xt[:, t, :], x1[t * P:(t + 1) * P, :]).then_inc(ld_x[t], 16)
            for i, wT in enumerate((wqT, wkT, wvT)):
                sp.dma_start(raw[i][:, :, :], wT.rearrange("(c p) n -> p c n", p=P)).then_inc(ld_w[i], 16)
                if i == 0:
                    for t in range(T):
                        sp.dma_start(ct[:, t, :], cx[t * P:(t + 1) * P, :]).then_inc(ld_t[t], 16)

            def load_x(g, t):
                sp.wait_ge(h_ready, g * T + (t + 1))
                sp.dma_start(xt[:, t, :], x1[bass.ds(row0(g, t) + GR, P), :]).then_inc(ld_x[t], 16)

            def group(g, more):
                for i in range(2):
                    for c in range(C):
                        sp.wait_ge(r_out, g * UNITS + (BANKS + i * C + c + 1))
                        for hl in (1, 0):
                            sp.dma_start(qk[i, hl, c * P:(c + 1) * P, bass.ds(g * GR, GR)],
                                         res[i][hl][:, c, :].bitcast(F32)).then_inc(st_r[i][c], 16)
                        if more >= 1 and i == 0:
                            sp.wait_ge(cT_pe, g * T + (c + 1))
                            sp.dma_start(ct[:, c, :], cx[bass.ds(row0(g, c) + GR, P), :]).then_inc(ld_t[c], 16)
                        if more >= 2 and i == 1:
                            load_x(g + 1, c)
                for t in range(T):
                    sp.wait_ge(r_out, g * UNITS + (BANKS + 2 * C + t + 1))
                    sp.dma_start(vd[bass.ds(row0(g, t), P), :], vals[:, t, :]).then_inc(st_v[t], 16)

            for t in range(T):
                load_x(0, t)
            sp.wait_ge(prep_lo, 2)
            sp.dma_start(ints[:, :, :], w.rearrange("(c p) n -> p c n", p=P)).then_inc(ld_f, 16)
            sp.dma_start(aTs[:, :], aT).then_inc(ld_c, 16)
            sp.dma_start(bs[:, :], b).then_inc(ld_c, 16)
            with sp.Fori(0, G - 2) as g:
                group(g, 2)
            group(G - 2, 1)
            group(G - 1, 0)
            for c in range(C):
                sp.wait_ge(st_r[0][c], 32 * G)
                sp.wait_ge(st_r[1][c], 32 * G)
                sp.wait_ge(st_v[c], 16 * G)

        @block.gpsimd
        def _(pool):
            pool.wait_ge(r_out, BANKS)
            with pool.Fori(0, G) as g:
                for t in range(T):
                    pool.wait_ge(var_ready, g * T + (t + 1))
                    pool.tensor_tensor(rstd[:, t:t + 1], mv[:, t, 1:2], power[:, :], ALU.pow).then_inc(rstd_ready, 1)
            pool.wait_ge(top_ready, 1)
            pool.wait_ge(rstd_ready, G * T)
            pool.partition_all_reduce(topall[:, :], top[:, :], P, RED.max).then_inc(all_ready, 1)

        @block.vector
        def _(v):
            v.memset(power[:, :], -0.5).then_inc(r_out, BANKS)

            def split(i):
                v.wait_ge(prep_hi, i + 1)
                v.tensor_tensor(W[i][1][:, :, :], raw[i][:, :, :], W[i][0][:, :, :], ALU.subtract).then_inc(prep_lo, 1)

            def stats(g, t):
                v.wait_ge(ld_x[t], g * 16 + 16)
                v.bn_stats(bn[:, t, :], xt[:, t, :]).then_inc(bn_ready, 1)
                wait_apart(v, bn_ready, g * T + (t + 1), spare)
                v.bn_aggr(mv[:, t, :], bn[:, t, :]).then_inc(var_eps, 1)
                v.wait_ge(var_eps, g * T + (t + 1))
                v.tensor_scalar(mv[:, t, 1:2], mv[:, t, 1:2], EPS, None, ALU.add).then_inc(var_ready, 1)

            def layernorm(g, t):
                v.wait_ge(rstd_ready, g * T + (t + 1))
                v.tensor_scalar(h[:, t, :], xt[:, t, :], mv[:, t, 0:1], rstd[:, t:t + 1],
                                ALU.subtract, ALU.mult).then_inc(h_ready, 1)

            def low(bank, dst, t, ready, at, done):
                v.wait_ge(ready, at)
                rows = slice(t * P, (t + 1) * P)
                v.tensor_tensor(dst[1][:, :, rows], ps[:, bank, :].rearrange("p (c n) -> p c n", c=C),
                                dst[0][:, :, rows], ALU.subtract).then_inc(done, 1)

            def result(g, i, c):
                v.wait_ge(r_hi, g * (2 * C) + (i * C + c + 1))
                v.tensor_tensor(res[i][1][:, c, :], ps[:, 2 + (i * C + c) % BANKS, :], res[i][0][:, c, :],
                                ALU.subtract).then_inc(r_out, 1)

            flat = ints[:, :, :].rearrange("p c n -> p (c n)")

            def link(ins, n):
                ins.then_inc(q_step, 1)
                v.wait_ge(q_step, n)

            def quantize(c):
                if c == 0:
                    v.wait_ge(all_ready, 1)
                    link(v.tensor_scalar(step[:, :], topall[:, :], float(np.float32(1.0) / np.float32(7.0)), None,
                                         ALU.mult), 1)
                    link(v.reciprocal(inv[:, :], step[:, :]), 2)
                elif c == 1:
                    link(v.tensor_scalar(flat, flat, inv[:, :], ROUND, ALU.mult, ALU.add), 3)
                elif c == 2:
                    link(v.tensor_scalar(flat, flat, ROUND, 7.0, ALU.subtract, ALU.min), 4)
                else:
                    link(v.tensor_scalar(flat, flat, -8.0, None, ALU.max), 5)

            def dequantize(c):
                v.wait_ge(lora, c + 1)
                v.scalar_tensor_tensor(out=whole[:, c, :], in0=ints[:, c, :], scalar=step[:, 0:1],
                                       in1=ps[:, c % 2, :], op0=ALU.mult, op1=ALU.add).then_inc(ffn_whole, 1)
                v.wait_ge(ffn_whole, c + 1)
                link(v.tensor_copy(ffn[0][:, c, :], whole[:, c, :]), 6 + c)
                v.tensor_tensor(ffn[1][:, c, :], whole[:, c, :], ffn[0][:, c, :], ALU.subtract)

            def group(g, last):
                for c in range(C):
                    low(c % 2, cT, c, cT_hi, g * T + (c + 1), cT_lo)
                    if not last:
                        stats(g + 1, c)
                        if c > 0:
                            layernorm(g + 1, c - 1)
                    result(g, 0, c)
                    if isinstance(g, int) and g == 0 and c < 2:
                        split(c + 1)
                    if last:
                        quantize(c)
                for c in range(C):
                    if not last and c == 0:
                        layernorm(g + 1, T - 1)
                    if not last:
                        low(c % 2, hT, c, hT_hi, (g + 1) * T + (c + 1), hT_lo)
                    result(g, 1, c)
                    if last:
                        dequantize(c)
                if isinstance(g, int) and g == 0:
                    v.wait_ge(ld_f, 16)
                    v.tensor_reduce(top[:, :], flat, AX, ALU.max, apply_absolute_value=True).then_inc(top_ready, 1)
                for t in range(T):
                    v.wait_ge(v_pe, g * T + (t + 1))
                    v.wait_ge(st_v[t], g * 16)
                    v.tensor_copy(vals[:, t, :], ps[:, 2 + (2 * C + t) % BANKS, :]).then_inc(r_out, 1)

            for t in range(T):
                stats(0, t)
                if t > 0:
                    layernorm(0, t - 1)
            layernorm(0, T - 1)
            split(0)
            for t in range(T):
                low(t % 2, hT, t, hT_hi, t + 1, hT_lo)
            group(0, False)
            with v.Fori(1, G - 1) as g:
                group(g, False)
            group(G - 1, True)

        @block.scalar
        def _(act):
            def high_weight(i):
                act.wait_ge(ld_w[i], 16)
                act.activation(W[i][0][:, :, :], raw[i][:, :, :], ACT.Copy).then_inc(prep_hi, 1)

            def high(bank, dst, t, ready, at, done):
                act.wait_ge(ready, at)
                act.activation(dst[0][:, :, t * P:(t + 1) * P], ps[:, bank, :].rearrange("p (c n) -> p c n", c=C),
                               ACT.Copy).then_inc(done, 1)

            def result(g, i, c):
                act.wait_ge((q_pe, k_pe)[i], g * C + (c + 1))
                act.wait_ge(st_r[i][c], g * 32)
                act.activation(res[i][0][:, c, :], ps[:, 2 + (i * C + c) % BANKS, :], ACT.Copy).then_inc(r_hi, 1)

            def group(g, last):
                for c in range(C):
                    high(c % 2, cT, c, cT_pe, g * T + (c + 1), cT_hi)
                    result(g, 0, c)
                for c in range(C):
                    if not last:
                        high(c % 2, hT, c, hT_pe, (g + 1) * T + (c + 1), hT_hi)
                    result(g, 1, c)

            high_weight(0)
            for t in range(T):
                high(t % 2, hT, t, hT_pe, t + 1, hT_hi)
            high_weight(1)
            high_weight(2)
            group(0, False)
            with act.Fori(1, G - 1) as g:
                group(g, False)
            group(G - 1, True)

        @block.tensor
        def _(pe):
            pe.wait_ge(ld_c, 16)
            def turn_h(g, t, free):
                pe.wait_ge(h_ready, g * T + (t + 1))
                if free:
                    pe.wait_ge(free[0], free[1])
                transposes(pe, ps[:, t % 2, :], [h[:, t, c * P:(c + 1) * P] for c in range(C)], ident[:, :]
                           ).then_inc(hT_pe, 1)

            def group(g, last):
                for c in range(C):
                    pe.wait_ge(ld_t[c], g * 16 + 16)
                    if c < 2:
                        pe.wait_ge(hT_lo, g * T + (T - 1 + c))
                    else:
                        pe.wait_ge(cT_lo, g * T + (c - 1))
                    transposes(pe, ps[:, c % 2, :], [ct[:, c, f * P:(f + 1) * P] for f in range(C)], ident[:, :]
                               ).then_inc(cT_pe, 1)
                    if c == 0:
                        pe.wait_ge(hT_lo, g * T + T)
                        weight(g, 0)
                    product(g, c, W[0], hT, c, False).then_inc(q_pe, 1)
                for c in range(C):
                    if not last:
                        turn_h(g + 1, c, (cT_lo, g * T + (T - 1 + c)) if c < 2 else (hT_lo, g * T + (T + c - 1)))
                    if c == 0:
                        pe.wait_ge(cT_lo, g * T + T)
                        weight(g, 1)
                    if last:
                        if c == 0:
                            pe.wait_ge(ld_c, 48)
                        if c >= 2:
                            pe.wait_ge(ffn_whole, c - 1)
                        pe.matmul(ps[:, c % 2, :], aTs[:, c * P:(c + 1) * P], bs[:, :], start=True, stop=True
                                  ).then_inc(lora, 1)
                    product(g, C + c, W[1], cT, c, False).then_inc(k_pe, 1)
                weight(g, 2)
                for t in range(T):
                    product(g, 2 * C + t, cT, W[2], t, True).then_inc(v_pe, 1)

            def weight(g, i):
                if isinstance(g, int) and g == 0:
                    pe.wait_ge(prep_lo, i + 1)

            def product(g, u, lhs, rhs, m, rows):
                pe.wait_ge(r_out, g * UNITS + (u + 1))
                for c in range(C):
                    last = mm3(pe, ps[:, 2 + u % BANKS, :], [a[:, c, m * P:(m + 1) * P] for a in lhs],
                               [a[:, c, :] for a in rhs], c == 0, c == C - 1)
                return last

            for t in range(T):
                turn_h(0, t, (hT_lo, t - 1) if t >= 2 else None)
            group(0, False)
            with pe.Fori(1, G - 1) as g:
                group(g, False)
            group(G - 1, True)


def attention(nc, ps, x1, qk, vd, woT, ident_in, masks_in, nmd, x2):
    ROWS = x1.shape[0]
    PAIRS = ROWS // P
    R = P // 2
    U = R // 8
    NU = 2 * U
    K = 3 * HD
    BUF = 3
    LOOPS = (PAIRS - 2) // BUF
    FIRST = U + 2
    LAG = 2
    PT = U
    SCALE = float(np.float32(1.0) / np.sqrt(np.float32(HD)))
    HALF = C * R // 2
    assert LOOPS * BUF == PAIRS - 2 and NU % PT == 0
    with ExitStack() as ctx:
        s = Scope(nc, ctx, "c")

        def banks(n, w):
            flat = ps[:, n:n + (2 if w > R // 2 else 1), :].rearrange("p a n -> p (a n)")
            return flat.rearrange("p (c r) -> p c r", c=HEADS)[:, :, 0:w]

        def scores(k):
            return banks(3 * (k % 2), 8 * (k % U + 1))

        def shifted(k):
            w = R - 8 * (k % U)
            return banks(3 * (k % 2) + (1 if w > R // 2 else 2), w)

        av = ps[:, 6, 0:256].rearrange("p (c r) -> p c r", c=C)
        misc = ps[:, 7, :]
        den = misc[:, 0:C * R].rearrange("p (c r) -> p c r", c=C)
        qs = [s.sb(f"qs{i}", [P, HEADS, P], F32R) for i in range(BUF)]
        ks = [s.sb(f"ks{i}", [P, HEADS, P], F32R) for i in range(BUF)]
        qg, kg = s.sb("qg", [P, NU, P], F32R), s.sb("kg", [P, NU, P], F32R)
        vt = [s.sb(f"vt{i}", [P, NU, HD]) for i in range(BUF)]
        xt = [s.sb(f"xt{i}", [P, D]) for i in range(BUF)]
        W, raw = s.pair("w", [P, C, D]), s.sb("raw", [P, C, D])
        ident, identr = s.sb("ident", [P, P]), s.sb("identr", [P, P], F32R)
        maskf = [s.sb(f"maskf{i}", [P, HEADS, 8]) for i in range(2)]
        mask = [s.sb(f"mask{i}", [P, HEADS, 8], BF16) for i in range(2)]
        identb = s.sb("identb", [P, P], BF16)
        ones = s.sb("ones", [P, HD])
        pt = [s.sb(f"pt{i}", [P, HEADS * R]) for i in range(PT)]
        mx = s.sb("mx", [P, NU])
        nm = [s.sb(f"nm{i}", [P, P], F32R) for i in range(2)]
        nmt = [s.sb(f"nmt{i}", [2 * U, P], F32R) for i in range(2)]
        total = [s.sb(f"total{i}", [P, HEADS, R]) for i in range(2)]
        avs, rec, o = s.sb("avs", [P, C * R]), s.sb("rec", [P, C * R]), s.sb("o", [P, C, R])
        oT = s.pair("oT", [P, C, P])

        ld_c, ld_w, setup = s.sem("ld_c"), s.sem("ld_w"), s.sem("setup")
        ld_qk, ld_v, ld_x, st_x = s.sems("ld_qk", BUF), s.sems("ld_v", BUF), s.sems("ld_x", BUF), s.sems("st_x", BUF)
        prep_hi, prep_lo = s.sem("prep_hi"), s.sem("prep_lo")
        g_pe, g_max = s.sem("g_pe"), s.sem("g_max")
        nm_hi, nm_lo, nm_pe, nm_t, nm_st = (s.sem(n) for n in ("nm_hi", "nm_lo", "nm_pe", "nm_t", "nm_st"))
        nm_ld = s.sems("nm_ld", 2)
        qg_done, kg_done = s.sem("qg_done"), s.sem("kg_done")
        t_pe, t_exp, a_pe = s.sem("t_pe"), s.sem("t_exp"), s.sem("a_pe")
        s_first, s_add, den_pe = s.sem("s_first"), s.sem("s_add"), s.sem("den_pe")
        o_out, r_done, o_done = s.sem("o_out"), s.sem("r_done"), s.sem("o_done")
        o_hi, o_lo = s.sem("o_hi"), s.sem("o_lo")
        y_pe, y_done = s.sem("y_pe"), s.sem("y_done")
        block = s.block()
        vf = vd.rearrange("r (c e) -> (r c) e", e=HD)

        def probs(k):
            w = R - 8 * (k % U)
            rows = R if w > R // 2 else R // 2
            return pt[k % PT][:, 0:HEADS * rows].rearrange("p (c r) -> p c r", c=HEADS)[:, :, 0:w]

        def parts(w):
            return [slice(0, 8), slice(8, 16)] if w > R // 2 else [slice(0, 16)]

        @block.sync
        def _(sp):
            def load_qk(p, a):
                for g in range(3):
                    for i, t in enumerate((qs[a], ks[a])):
                        hl = (0, 0, 1)[g] if i == 0 else (0, 1, 0)[g]
                        sp.dma_start(t[HD * g:HD * (g + 1), :, :].bitcast(F32),
                                     qk[i, hl].rearrange("(c d) r -> d c r", d=HD)[:, :, bass.ds(p * P, P)]
                                     ).then_inc(ld_qk[a], 16)

            def load_vx(p, a):
                sp.dma_start(vt[a][:, :, :], vf[bass.ds(p * (P * HEADS), P * HEADS), :].rearrange(
                    "(t p) e -> p t e", p=P)).then_inc(ld_v[a], 16)
                sp.dma_start(xt[a][:, :], x1[bass.ds(p * P, P), :]).then_inc(ld_x[a], 16)

            def maxima(p, a, hd):
                waits = [(nm_t, 2 * p + (hd + 1))]
                if not isinstance(p, int) or p > 0:
                    waits.append((nm_ld[hd], 16 * p))
                for sem, value in waits if hd else waits[::-1]:
                    sp.wait_ge(sem, value)
                for hl in range(2):
                    sp.dma_start(nmd[hd, hl].rearrange("c u r -> u c r"), nmt[hd][U * hl:U * (hl + 1), :].bitcast(F32)
                                 .rearrange("u (c r) -> u c r", c=HEADS)).then_inc(nm_st, 16)
                sp.wait_ge(nm_st, 64 * p + 32 * (hd + 1))
                sp.dma_start(qs[a][K:K + 2, :, R * hd:R * (hd + 1)].bitcast(F32),
                             nmd[hd].rearrange("l c u r -> l c (u r)")).then_inc(nm_ld[hd], 16)

            def store(i, a):
                p = i * BUF + a
                sp.wait_ge(y_done, p + 1)
                sp.dma_start(x2[bass.ds(p * P, P), :], xt[a][:, :]).then_inc(st_x[a], 16)

            def turn(i, a):
                p = i * BUF + a
                b = (a + 2) % BUF
                sp.wait_ge(t_pe, p * NU)
                load_qk(p + 2, b)
                maxima(p, a, 1)
                if not isinstance(p, int) or p > 0:
                    store(i - (a == 0), b)
                maxima(p + 1, (a + 1) % BUF, 0)
                if not isinstance(p, int) or p > 0:
                    sp.wait_ge(st_x[b], i * 16 + (16 if b < a else 0))
                load_vx(p + 2, b)

            load_qk(0, 0)
            sp.dma_start(ident[:, :], ident_in).then_inc(ld_c, 16)
            for i in range(2):
                sp.dma_start(maskf[i][:, :, :], masks_in[i]).then_inc(ld_c, 16)
            load_qk(1, 1)
            for p in range(2):
                load_vx(p, p)
            sp.dma_start(raw[:, :, :], woT.rearrange("(c p) n -> p c n", p=P)).then_inc(ld_w, 16)
            maxima(0, 0, 0)
            for a in range(BUF):
                turn(0, a)
            with sp.Fori(1, LOOPS) as i:
                for a in range(BUF):
                    turn(i, a)
            maxima(PAIRS - 2, 0, 1)
            store(LOOPS - 1, BUF - 1)
            maxima(PAIRS - 1, 1, 0)
            maxima(PAIRS - 1, 1, 1)
            store(LOOPS, 0)
            store(LOOPS, 1)
            for a in range(BUF):
                sp.wait_ge(st_x[a], 16 * len(range(a, PAIRS, BUF)))

        @block.gpsimd
        def _(pool):
            def unit(p, k):
                if k % U == 0:
                    return
                hd, at = k // U, 8 * (k % U)
                out = total[hd]
                pool.wait_ge(t_exp, p * NU + (k + 1))
                if k % U > 1:
                    pool.wait_ge(s_add, (2 * p + hd) * (U - 1) + (k % U - 1))
                    before = out[:, :, at:R]
                else:
                    if not isinstance(p, int) or 2 * p + hd >= 2:
                        pool.wait_ge(den_pe, 2 * p + (hd - 1))
                    before = probs(k - 1)[:, :, at:R]
                pool.tensor_tensor(out[:, :, at:R], before, probs(k), ALU.add).then_inc(s_add, 1)

            for k in range(NU):
                unit(0, k)
            with pool.Fori(1, PAIRS) as p:
                for k in range(NU):
                    unit(p, k)

        @block.vector
        def _(v):
            v.memset(kg[K:K + 2, :, :].bitcast(F32), 1.0).then_inc(setup, 1)
            v.memset(ones[:, :], 1.0).then_inc(setup, 1)
            v.wait_ge(ld_c, 48)
            v.tensor_copy(identr[:, :], ident[:, :]).then_inc(setup, 1)
            v.tensor_copy(identb[:, :], ident[:, :]).then_inc(setup, 1)
            for i in range(2):
                v.tensor_copy(mask[i][:, :, :], maskf[i][:, :, :]).then_inc(setup, 1)
            for hd in range(2):
                v.tensor_scalar(nm[hd][:, :], ident[:, :], 0.0, None, ALU.mult).then_inc(setup, 1)

            def first_pass(p, k):
                v.wait_ge(g_pe, p * NU + (k + 1))
                v.tensor_reduce(mx[:, k:k + 1], scores(k), mybir.AxisListType.XY, ALU.max,
                                negate=True).then_inc(g_max, 1)

            def negate(p, hd):
                v.wait_ge(g_max, p * NU + U * (hd + 1))
                if not isinstance(p, int) or p > 0:
                    v.wait_ge(nm_pe, 2 * p + (hd - 1))
                m = mx[:, U * hd:U * (hd + 1)]
                v.tensor_copy(nm[hd][:, 0:U], m).then_inc(nm_hi, 1)
                v.wait_ge(nm_hi, 2 * p + (hd + 1))
                v.tensor_tensor(nm[hd][:, U:2 * U], m, nm[hd][:, 0:U], ALU.subtract).then_inc(nm_lo, 1)

            def values_out(p, hd):
                v.wait_ge(a_pe, p * NU + U * (hd + 1))
                v.tensor_copy(avs[:, :], av.rearrange("p c r -> p (c r)")).then_inc(o_out, 1)

            def invert(p, hd, part):
                if part == 0:
                    v.wait_ge(den_pe, 2 * p + (hd + 1))
                cols = slice(part * HALF, (part + 1) * HALF)
                v.reciprocal(rec[:, cols], misc[:, cols]).then_inc(r_done, 1)

            def normalize(p, hd):
                v.wait_ge(r_done, 4 * p + 2 * (hd + 1))
                v.tensor_tensor(o[:, :, :].rearrange("p c r -> p (c r)"), avs[:, :], rec[:, :], ALU.mult
                                ).then_inc(o_done, 1)

            def low(p, hd):
                v.wait_ge(o_hi, 2 * p + (hd + 1))
                rows = slice(R * hd, R * (hd + 1))
                v.tensor_tensor(oT[1][:, :, rows], o[:, :, :], oT[0][:, :, rows], ALU.subtract).then_inc(o_lo, 1)

            def output(i, a):
                p = i * BUF + a
                v.wait_ge(y_pe, p + 1)
                v.wait_ge(ld_x[a], i * 16 + 16)
                v.tensor_tensor(xt[a][:, :], misc, xt[a][:, :], ALU.add).then_inc(y_done, 1)

            def turn(i, a, more):
                p = i * BUF + a
                for slot in range(FIRST, FIRST + NU):
                    if slot in (U + 2, NU + 2):
                        values_out(p, slot // U - 1)
                    if slot == FIRST + NU - 1:
                        output(i, a)
                    if slot // NU + 1 <= more:
                        first_pass(p + (slot // NU + 1), slot % NU)
                    if slot == NU and more >= 1:
                        negate(p + 1, 1)
                    if slot == NU + U and more >= 2:
                        negate(p + 2, 0)
                    if slot in (U + 2, NU + 2):
                        invert(p, slot // U - 1, 0)
                    if slot in (U + 3, NU + 3):
                        invert(p, slot // U - 1, 1)
                        normalize(p, slot // U - 1)
                    if slot in (U + 5, NU + 5):
                        low(p, slot // U - 1)

            for k in range(NU):
                first_pass(0, k)
                if k == U:
                    negate(0, 0)
            negate(0, 1)
            v.wait_ge(prep_hi, 1)
            v.tensor_tensor(W[1][:, :, :], raw[:, :, :], W[0][:, :, :], ALU.subtract).then_inc(prep_lo, 1)
            for k in range(FIRST):
                first_pass(1, k)
                if k == U:
                    negate(1, 0)
            with v.Fori(0, LOOPS) as i:
                for a in range(BUF):
                    turn(i, a, 2)
            turn(LOOPS, 0, 1)
            turn(LOOPS, 1, 0)

        @block.scalar
        def _(act):
            def unit(p, k):
                n = p * NU + k
                act.wait_ge(t_pe, n + 1)
                if not isinstance(n, int) or n >= PT:
                    act.wait_ge(a_pe, n - (PT - 1))
                    act.wait_ge(s_add, (2 * p + (k // U - 1)) * (U - 1) + max(k % U, 1))
                act.activation(probs(k), shifted(k), ACT.Exp, scale=SCALE).then_inc(t_exp, 1)
                if k % U == 1:
                    first_rows(p, k // U)

            def first_rows(p, hd):
                act.wait_ge(t_exp, p * NU + (U * hd + 1))
                if not isinstance(p, int) or p > 0:
                    act.wait_ge(den_pe, 2 * p + (hd - 1))
                act.activation(total[hd][:, :, 0:8], probs(U * hd)[:, :, 0:8], ACT.Copy).then_inc(s_first, 1)

            def maxima(p, hd):
                act.wait_ge(nm_pe, 2 * p + (hd + 1))
                if not isinstance(p, int) or p > 0:
                    act.wait_ge(nm_st, 64 * p + 32 * (hd - 1))
                act.activation(nmt[hd][:, :], misc[0:2 * U, 0:P], ACT.Copy).then_inc(nm_t, 1)

            def gather(i, a, hd, done, before, dst, src, order, parts):
                q = i * BUF + a
                act.wait_ge(ld_qk[a % BUF], (i + a // BUF) * 96 + 96)
                if not isinstance(q, int) or q > 0:
                    act.wait_ge(before, q * NU - NU + U * (hd + 1))
                out = dst[0:K, U * hd:U * (hd + 1), :]
                rows = src[a % BUF][0:K, :, R * hd:R * (hd + 1)].rearrange("p c (u r) -> p u c r", u=U)
                for u in range(0, U, U // parts):
                    o4 = out[:, u:u + U // parts, :].rearrange(order, c=HEADS)
                    i4 = rows[:, u:u + U // parts]
                    last = act.activation(o4, i4.bitcast(F32), ACT.Copy)
                last.then_inc(done, 1)

            def gather_q(i, a, hd):
                gather(i, a, hd, qg_done, g_pe, qg, qs, "p u (c r) -> p u c r", 1)

            def gather_k(i, a, hd):
                gather(i, a, hd, kg_done, t_pe, kg, ks, "p u (r c) -> p u c r", 1)

            def high(p, hd):
                act.wait_ge(o_done, 2 * p + (hd + 1))
                act.activation(oT[0][:, :, R * hd:R * (hd + 1)], o[:, :, :], ACT.Copy).then_inc(o_hi, 1)

            def turn(i, a, more):
                p = i * BUF + a
                for slot in range(FIRST, FIRST + NU):
                    if slot // NU <= more:
                        unit(p + slot // NU, slot % NU)
                    if slot == NU + 1 and more >= 1:
                        maxima(p + 1, 1)
                    if slot == NU + U + 1 and more >= 2:
                        maxima(p + 2, 0)
                    if slot in (U + 4, NU + 4):
                        high(p, slot // U - 1)
                    if slot in (U + 5, NU + 5) and more >= 2:
                        gather_q(i, a + 2, slot // U - 1)
                    if slot in (U + 3, NU + 3) and more >= 1:
                        gather_k(i, a + 1, slot // U - 1)

            for hd in range(2):
                gather_q(0, 0, hd)
            for hd in range(2):
                gather_k(0, 0, hd)
            act.wait_ge(ld_w, 16)
            act.activation(W[0][:, :, :], raw[:, :, :], ACT.Copy).then_inc(prep_hi, 1)
            gather_q(0, 1, 0)
            maxima(0, 0)
            gather_q(0, 1, 1)
            maxima(0, 1)
            for k in range(FIRST):
                unit(0, k)
                if k == U + 1:
                    maxima(1, 0)
            with act.Fori(0, LOOPS) as i:
                for a in range(BUF):
                    turn(i, a, 2)
            turn(LOOPS, 0, 1)
            turn(LOOPS, 1, 0)

        @block.tensor
        def _(pe):
            pe.wait_ge(setup, 8)

            def first_pass(i, a, k):
                q = i * BUF + a
                n = q * NU + k
                a = a % BUF
                if k % U == 0:
                    pe.wait_ge(qg_done, 2 * q + (k // U + 1))
                if not isinstance(n, int) or n >= 2:
                    pe.wait_ge(g_max, n - 1)
                if k % U in (U // 2, U // 2 + 1) and (not isinstance(n, int) or n >= NU):
                    pe.wait_ge(t_exp, n - (NU + 1))
                hd, w, out = k // U, 8 * (k % U + 1), scores(k)
                for cs in parts(w):
                    pe.matmul(out[:, cs, :], qg[0:K, k, :], ks[a][0:K, cs, R * hd:R * hd + w],
                              start=True, stop=False)

            def first_mask(k):
                w, out = 8 * (k % U + 1), scores(k)
                for cs in parts(w):
                    last = pe.matmul(out[:, cs, w - 8:w], identb[:, :], mask[0][:, cs, :], start=False, stop=True)
                last.then_inc(g_pe, 1)

            def second_pass(i, a, k):
                p = i * BUF + a
                n = p * NU + k
                a = a % BUF
                hd, at = k // U, 8 * (k % U)
                if k % U == 0:
                    pe.wait_ge(nm_ld[hd], p * 16 + 16)
                    pe.wait_ge(kg_done, 2 * p + (hd + 1))
                if not isinstance(n, int) or n >= 2:
                    pe.wait_ge(t_exp, n - 1)
                if k % U in (0, 1):
                    last_g = n + (NU - 1)
                    pe.wait_ge(g_max, min(last_g, PAIRS * NU) if isinstance(n, int) else last_g)
                w, out = R - at, shifted(k)
                for cs in parts(w):
                    pe.matmul(out[:, cs, :], kg[0:K + 2, k, :], qs[a][0:K + 2, cs, R * hd + at:R * (hd + 1)],
                              start=True, stop=False)

            def second_mask(k):
                out = shifted(k)
                for cs in parts(R - 8 * (k % U)):
                    last = pe.matmul(out[:, cs, 0:8], identb[:, :], mask[1][:, cs, :], start=False, stop=True)
                last.then_inc(t_pe, 1)

            def value_units(slot):
                return (slot - LAG - 1, slot - LAG) if slot % 2 == 1 and slot > LAG else ()

            def values(i, a, k):
                p = i * BUF + a
                a, j = a % BUF, i + a // BUF
                hd, at = k // U, 8 * (k % U)
                pe.wait_ge(t_exp, p * NU + (k + 1))
                if k == 0:
                    pe.wait_ge(ld_v[a], j * 16 + 16)
                if k % U == 0:
                    pe.wait_ge(o_out, 2 * p + hd)
                rhs = probs(k).rearrange("p (c q) r -> p c q r", q=4)
                for q in range(4):
                    last = pe.matmul(av[HD * q:HD * (q + 1), :, at:R], vt[a][:, k, :], rhs[:, :, q, :],
                                     start=(at == 0), stop=(k % U == U - 1), skip_group_check=True)
                last.then_inc(a_pe, 1)

            def sums(p, hd, more):
                pe.wait_ge(s_first, 2 * p + (hd + 1))
                pe.wait_ge(s_add, (2 * p + (hd + 1)) * (U - 1))
                if more >= 1:
                    pe.wait_ge(nm_t, 2 * p + (3 + hd))
                elif hd == 1:
                    pe.wait_ge(r_done, 4 * p + 2)
                else:
                    pe.wait_ge(y_done, p)
                rhs = total[hd][:, :, :].rearrange("p (c q) r -> p c q r", q=4)
                for q in range(4):
                    last = pe.matmul(den[HD * q:HD * (q + 1), :, :], ones[:, :], rhs[:, :, q, :],
                                     start=True, stop=True, skip_group_check=True)
                last.then_inc(den_pe, 1)

            def maxima(p, hd):
                pe.wait_ge(nm_lo, 2 * p + (hd + 1))
                if isinstance(p, int) and 2 * p + hd < 3:
                    if 2 * p + hd > 0:
                        pe.wait_ge(nm_t, 2 * p + hd)
                elif hd == 1:
                    pe.wait_ge(r_done, 4 * p - 2)
                else:
                    pe.wait_ge(y_done, p - 1)
                pe.matmul(misc[:, 0:P], nm[hd][:, :], identr[:, :], start=True, stop=True).then_inc(nm_pe, 1)

            def output(p):
                pe.wait_ge(o_lo, 2 * p + 2)
                for c in range(C):
                    last = mm3(pe, misc, [t[:, c, :] for t in oT], [t[:, c, :] for t in W], c == 0, c == C - 1)
                last.then_inc(y_pe, 1)

            def turn(i, a, more):
                p = i * BUF + a
                for slot in range(FIRST, FIRST + NU):
                    if slot // NU <= more:
                        second_pass(i, a + slot // NU, slot % NU)
                    if slot // NU + 1 <= more:
                        first_pass(i, a + slot // NU + 1, slot % NU)
                    if slot // NU + 1 <= more:
                        first_mask(slot % NU)
                    if slot // NU <= more:
                        second_mask(slot % NU)
                    for n in value_units(slot):
                        if n // NU <= more:
                            values(i, a + n // NU, n % NU)
                    if slot in (U + 2, NU + 2):
                        sums(p, slot // U - 1, more)
                    if slot == NU + 1 and more >= 1:
                        maxima(p + 1, 1)
                    if slot == NU + U:
                        output(p)
                    if slot == NU + U + 1 and more >= 2:
                        maxima(p + 2, 0)

            for k in range(NU):
                first_pass(0, 0, k)
                first_mask(k)
                if k == U + 2:
                    maxima(0, 0)
            maxima(0, 1)
            for k in range(FIRST):
                second_pass(0, 0, k)
                first_pass(0, 1, k)
                first_mask(k)
                second_mask(k)
                for n in value_units(k):
                    values(0, 0, n)
                if k == U + 1:
                    maxima(1, 0)
            with pe.Fori(0, LOOPS) as i:
                for a in range(BUF):
                    turn(i, a, 2)
            turn(LOOPS, 0, 1)
            turn(LOOPS, 1, 0)


def feed_forward(nc, ps, x2, W, bias, ident_in, out):
    ROWS = x2.shape[0]
    TILES = ROWS // P
    BUF = 8
    YB = 4
    LOOPS = (TILES - 2) // BUF
    with ExitStack() as ctx:
        s = Scope(nc, ctx, "d")
        ident, bb, power = s.sb("ident", [P, P]), s.sb("bias", [P, D]), s.sb("power", [P, 1])
        spare = s.sb("spare", [P, 1])
        xt = [s.sb(f"xt{i}", [P, D]) for i in range(BUF)]
        yt = [s.sb(f"yt{i}", [P, D]) for i in range(BUF)]
        h = s.sb("h", [P, 2, D])
        hT = [s.pair(f"hT{i}", [P, C, P]) for i in range(2)]
        bn, mv, rstd = s.sb("bn", [P, 2, 6]), s.sb("mv", [P, 2, 2]), s.sb("rstd", [P, 2])

        ld_c, ld_x, st_y = s.sem("ld_c"), s.sems("ld_x", BUF), s.sems("st_y", BUF)
        setup = s.sem("setup")
        bn_ready, var_eps, var_ready, rstd_ready, h_ready = (s.sem(n) for n in ("bn", "ve", "var", "rstd", "h"))
        hT_pe, hT_hi, hT_lo, xb_done, y_pe, y_done = (s.sem(n) for n in (
            "hT_pe", "hT_hi", "hT_lo", "xb", "y_pe", "y_done"))
        block = s.block()

        @block.sync
        def _(sp):
            for a in range(BUF):
                sp.dma_start(xt[a][:, :], x2[a * P:(a + 1) * P, :]).then_inc(ld_x[a], 16)
                if a == 0:
                    sp.dma_start(ident[:, :], ident_in).then_inc(ld_c, 16)
                    sp.dma_start(bb[:, :], bias.partition_broadcast(P)).then_inc(ld_c, 16)

            def turn(i, a, more):
                t = i * BUF + a
                sp.wait_ge(y_done, t + 1)
                sp.dma_start(out[bass.ds(t * P, P), :], yt[a][:, :]).then_inc(st_y[a], 16)
                if more:
                    sp.dma_start(xt[a][:, :], x2[bass.ds((t + BUF) * P, P), :]).then_inc(ld_x[a], 16)

            with sp.Fori(0, LOOPS) as i:
                for a in range(BUF):
                    turn(i, a, True)
            for t in range(LOOPS * BUF, TILES):
                turn(t // BUF, t % BUF, t + BUF < TILES)
            for a in range(BUF):
                sp.wait_ge(st_y[a], 16 * (TILES // BUF))

        @block.gpsimd
        def _(pool):
            pool.memset(power[:, :], -0.5).then_inc(setup, 1)
            pool.wait_ge(setup, 1)
            pool.wait_ge(ld_c, 32)

            with pool.Fori(0, TILES // BUF) as i:
                for a in range(BUF):
                    t = i * BUF + a
                    pool.wait_ge(var_ready, t + 1)
                    pool.tensor_tensor(rstd[:, a % 2:a % 2 + 1], mv[:, a % 2, 1:2], power[:, :], ALU.pow
                                       ).then_inc(rstd_ready, 1)
                    pool.wait_ge(h_ready, t + 1)
                    pool.tensor_tensor(xt[a][:, :], xt[a][:, :], bb[:, :], ALU.add).then_inc(xb_done, 1)

        @block.vector
        def _(v):
            def stats(i, a):
                t = i * BUF + a
                b, j = a % BUF, i + a // BUF
                x = xt[b]
                v.wait_ge(ld_x[b], j * 16 + 16)
                v.bn_stats(bn[:, a % 2, :], x[:, :]).then_inc(bn_ready, 1)
                wait_apart(v, bn_ready, t + 1, spare)
                v.bn_aggr(mv[:, a % 2, :], bn[:, a % 2, :]).then_inc(var_eps, 1)
                v.wait_ge(var_eps, t + 1)
                v.tensor_scalar(mv[:, a % 2, 1:2], mv[:, a % 2, 1:2], EPS, None, ALU.add).then_inc(var_ready, 1)

            def layernorm(i, a):
                t, x = i * BUF + a, xt[a % BUF]
                v.wait_ge(rstd_ready, t + 1)
                v.tensor_scalar(h[:, a % 2, :], x[:, :], mv[:, a % 2, 0:1], rstd[:, a % 2:a % 2 + 1],
                                ALU.subtract, ALU.mult).then_inc(h_ready, 1)

            def low(i, a):
                v.wait_ge(hT_hi, i * BUF + (a + 1))
                v.tensor_tensor(hT[a % 2][1][:, :, :], ps[:, a % 2, :].rearrange("p (c n) -> p c n", c=C),
                                hT[a % 2][0][:, :, :], ALU.subtract).then_inc(hT_lo, 1)

            def output(i, a):
                t = i * BUF + a
                v.wait_ge(y_pe, t + 1)
                v.wait_ge(xb_done, t + 1)
                v.wait_ge(st_y[a], i * 16)
                v.tensor_tensor(yt[a][:, :], ps[:, 2 + a % YB, :], xt[a][:, :], ALU.add).then_inc(y_done, 1)

            def turn(i, a, more):
                if more >= 1:
                    low(i, a + 1)
                if more >= 2:
                    layernorm(i, a + 2)
                if more >= 3:
                    stats(i, a + 3)
                output(i, a)

            stats(0, 0)
            stats(0, 1)
            layernorm(0, 0)
            stats(0, 2)
            layernorm(0, 1)
            low(0, 0)
            for a in range(BUF):
                turn(0, a, 3)
            with v.Fori(1, LOOPS) as i:
                for a in range(BUF):
                    turn(i, a, 3)
            for t in range(LOOPS * BUF, TILES):
                turn(t // BUF, t % BUF, TILES - 1 - t)

        @block.scalar
        def _(act):
            with act.Fori(0, TILES // BUF) as i:
                for a in range(BUF):
                    act.wait_ge(hT_pe, i * BUF + (a + 1))
                    act.activation(hT[a % 2][0][:, :, :], ps[:, a % 2, :].rearrange("p (c n) -> p c n", c=C),
                                   ACT.Copy).then_inc(hT_hi, 1)

        @block.tensor
        def _(pe):
            pe.wait_ge(ld_c, 32)

            def turn_h(i, a):
                t = i * BUF + a
                pe.wait_ge(h_ready, t + 1)
                if not isinstance(t, int) or t >= 2:
                    pe.wait_ge(hT_lo, t - 1)
                transposes(pe, ps[:, a % 2, :], [h[:, a % 2, c * P:(c + 1) * P] for c in range(C)], ident[:, :]
                           ).then_inc(hT_pe, 1)

            def product(i, a):
                t = i * BUF + a
                pe.wait_ge(hT_lo, t + 1)
                if not isinstance(t, int) or t >= YB:
                    pe.wait_ge(y_done, t - (YB - 1))
                for c in range(C):
                    last = mm3(pe, ps[:, 2 + a % YB, :], [u[:, c, :] for u in hT[a % 2]], [u[:, c, :] for u in W],
                               c == 0, c == C - 1)
                last.then_inc(y_pe, 1)

            turn_h(0, 0)
            for a in range(BUF):
                turn_h(0, a + 1)
                product(0, a)
            with pe.Fori(1, LOOPS) as i:
                for a in range(BUF):
                    turn_h(i, a + 1)
                    product(i, a)
            for t in range(LOOPS * BUF, TILES):
                if t + 1 < TILES:
                    turn_h(t // BUF, t % BUF + 1)
                product(t // BUF, t % BUF)


def decoder(nc, x, cx, Wq, Wk, WvT, Wo, bo, wqT, wkT, wvT, woT, w, bias, aT, b, ident, masks_in, out):
    rows = x.shape[0] * x.shape[1]
    x1 = nc.dram_tensor("x1", (rows, D), F32, kind="Internal").ap()
    x2 = nc.dram_tensor("x2", (rows, D), F32, kind="Internal").ap()
    qk = nc.dram_tensor("qk", (2, 2, D, rows), F32, kind="Internal").ap()
    vd = nc.dram_tensor("vd", (rows, D), F32, kind="Internal").ap()
    nmd = nc.dram_tensor("nmd", (2, 2, HEADS, P // 16, 8), F32, kind="Internal").ap()
    with nc.psum_tensor("psum", [P, 8, 512], F32) as ps:
        linear_attention(nc, ps, x, Wq, Wk, WvT, Wo, bo, ident, x1)
        with nc.sbuf_tensor("ffn_hi", [P, C, D], F32R) as hi, nc.sbuf_tensor("ffn_lo", [P, C, D], F32R) as lo:
            projections(nc, ps, x1, cx.rearrange("b n d -> (b n) d"), wqT, wkT, wvT, ident, qk, vd, w, aT, b, (hi, lo))
            attention(nc, ps, x1, qk, vd, woT, ident, masks_in, nmd, x2)
            feed_forward(nc, ps, x2, (hi, lo), bias, ident, out.rearrange("b n d -> (b n) d"))


def masks():
    c, r = np.divmod(np.arange(P), 8)
    own = np.arange(HEADS)[:, None] + HEADS * np.arange(8)[None, :]
    keys_after = np.where(own[None] <= (HEADS * r + c)[:, None, None], 0.0, MASKED)
    queries_before = np.where(np.arange(P)[:, None, None] <= own[None], 0.0, MASKED)
    return np.stack([keys_after, queries_before]).astype(np.float32)


_INS = ['x', 'ctx_1024', 'L0_attn_Wq', 'L0_attn_Wk', 'L0_attn_Wv', 'L0_attn_Wo', 'L0_attn_bo', 'L0_xattn_wq',
        'L0_xattn_wk', 'L0_xattn_wv', 'L0_xattn_wo', 'L0_ffn_kernel', 'L0_ffn_bias', 'L0_ffn_a', 'L0_ffn_b']


_TRANSPOSED = ('L0_attn_Wv', 'L0_xattn_wq', 'L0_xattn_wk', 'L0_xattn_wv', 'L0_xattn_wo', 'L0_ffn_a')


def kernel(**inputs):
    import concourse.bacc as _bacc
    from concourse.bass_utils import run_bass_kernel_spmd as _run

    nc = _bacc.Bacc("TRN2", target_bir_lowering=False, num_devices=1)
    arrays, args = {}, []

    def add(name, a):
        arrays[f"in_{name}_dram"] = a
        args.append(nc.dram_tensor(f"in_{name}_dram", a.shape, mybir.dt.from_np(a.dtype), kind="ExternalInput").ap())

    for name in _INS:
        a = np.asarray(inputs[name])
        add(name, np.ascontiguousarray(a.T if name in _TRANSPOSED else a))
    add("ident", np.eye(P, dtype=np.float32))
    add("masks", masks())
    args.append(nc.dram_tensor("out_0_dram", (4, 1024, D), F32, kind="ExternalOutput").ap())
    decoder(nc, *args)
    r = _run(nc, [arrays], core_ids=[0])
    return r.results[0]["out_0_dram"]
```
